# Optimizing a Trainium2 kernel written in Bass

```python
import numpy as np
import jax
import jax.numpy as jnp

def _softmax(x, axis=-1):
    return jax.nn.softmax(x, axis=axis)

def _gelu(x):
    return jax.nn.gelu(x, approximate=True)

def _silu(x):
    return jax.nn.silu(x)

def _sigmoid(x):
    return jax.nn.sigmoid(x)

def _layernorm(x, axis=-1, eps=1e-05):
    m = jnp.mean(x, axis=axis, keepdims=True)
    v = jnp.var(x, axis=axis, keepdims=True)
    return (x - m) / jnp.sqrt(v + eps)

def _scatter_add(tgt, idx, src, axis=0):
    return tgt.at[idx].add(src)

def _segment_sum(src, seg, n):
    return jax.ops.segment_sum(src, seg, n)
kernel_name = 'mk_perceiver_d4_seqx_r4_7c42d2'

def setup_inputs(seed: int=0):
    np.random.seed(seed)
    _w = jnp.asarray

    def _rec_inputs():
        import jax
        import jax.numpy as jnp
        _rk = jax.random.key(seed)
        x = -0.0002928 + 1 * jax.random.normal(jax.random.fold_in(_rk, 1), (16, 64, 256), jnp.float32)
        _lenS = 64 - jax.random.randint(jax.random.fold_in(_rk, 7), (16,), 0, max(1, 64 // 4) + 1, jnp.int32)
        _lenS2 = 1601 - jax.random.randint(jax.random.fold_in(_rk, 8), (16,), 0, max(1, 1601 // 4) + 1, jnp.int32)
        _ctx_512P = jax.random.normal(jax.random.fold_in(_rk, 11), (16, 16, 128), jnp.float32)
        _ctx_512c = jax.random.dirichlet(jax.random.fold_in(_rk, 511), 0.3 * jnp.ones((16,), jnp.float32), (16, 1601))
        _ctx_512t = jnp.einsum('bsk,bkd->bsd', _ctx_512c, _ctx_512P)
        _ctx_512t = _ctx_512t * jax.lax.rsqrt(jnp.mean(jnp.square(_ctx_512t)) + 1e-12) * 0.953939
        ctx_512 = 0.00222621 + 0.99962 * (_ctx_512t + 0.3 * jax.random.normal(jax.random.fold_in(_rk, 611), (16, 1601, 128), jnp.float32))
        return (x, ctx_512)
    x, ctx_512 = _rec_inputs()

    def _L0_xattn_setup():
        import jax, jax.numpy as jnp
        import numpy as np
        H, D, C1, C2, S, M, B, W = (16, 32, 256, 128, 512, 128, 2, 4)

        def _ln(x, g, b):
            m = jnp.mean(x, -1, keepdims=True)
            v = jnp.var(x, -1, keepdims=True)
            return (x - m) * jax.lax.rsqrt(v + 1e-05) * g + b

        def _mha(x, y, wq, wk, wv, li1_w, li1_b, lnx_g, lnx_b, lny_g, lny_b, ln3_g, ln3_b, li2_w, li2_b, li3_w, li3_b, causal):
            xn = _ln(x, lnx_g, lnx_b)
            yn = _ln(y, lny_g, lny_b)
            q = jnp.einsum('bsc,hcd->bhsd', xn, wq)
            k = jnp.einsum('btc,hcd->bhtd', yn, wk)
            v = jnp.einsum('btc,hcd->bhtd', yn, wv)
            a = jax.nn.softmax(jnp.einsum('bhsd,bhtd->bhst', q, k) * D ** (-0.5), axis=-1)
            if causal:
                s, t = (a.shape[-2], a.shape[-1])
                mask = (jnp.arange(t)[None, :] > jnp.arange(s)[:, None]).astype(a.dtype)
                a = a * mask
            o = jnp.einsum('bhst,bhtd->bhsd', a, v)
            o = o.transpose(0, 2, 1, 3).reshape(x.shape[0], x.shape[1], H * D)
            x_out = x + o @ li1_w + li1_b
            h = jax.nn.gelu(_ln(x_out, ln3_g, ln3_b) @ li2_w + li2_b, approximate=False)
            return x_out + h @ li3_w + li3_b
        key = jax.random.key(seed)
        ks = iter(jax.random.split(key, 64))

        def w(shape, scale=0.02):
            return jax.random.normal(next(ks), shape, jnp.float32) * scale
        inp = {'xx': jax.random.normal(next(ks), (B, S, C1), jnp.float32), 'ee': jax.random.normal(next(ks), (B, M, C2), jnp.float32), 'ln1_g': jnp.ones(C1, jnp.float32), 'ln1_b': jnp.zeros(C1, jnp.float32), 'ln2_g': jnp.ones(C1, jnp.float32), 'ln2_b': jnp.zeros(C1, jnp.float32)}
        for pfx, cy in (('a1', C1), ('a2', C2)):
            inp[pfx + '_wq'] = w((H, C1, D))
            inp[pfx + '_wk'] = w((H, cy, D))
            inp[pfx + '_wv'] = w((H, cy, D))
            inp[pfx + '_li1_w'] = w((H * D, C1))
            inp[pfx + '_li1_b'] = jnp.zeros(C1, jnp.float32)
            inp[pfx + '_lnx_g'] = jnp.ones(C1, jnp.float32)
            inp[pfx + '_lnx_b'] = jnp.zeros(C1, jnp.float32)
            inp[pfx + '_lny_g'] = jnp.ones(cy, jnp.float32)
            inp[pfx + '_lny_b'] = jnp.zeros(cy, jnp.float32)
            inp[pfx + '_ln3_g'] = jnp.ones(C1, jnp.float32)
            inp[pfx + '_ln3_b'] = jnp.zeros(C1, jnp.float32)
            inp[pfx + '_li2_w'] = w((C1, C1 * W))
            inp[pfx + '_li2_b'] = jnp.zeros(C1 * W, jnp.float32)
            inp[pfx + '_li3_w'] = w((C1 * W, C1))
            inp[pfx + '_li3_b'] = jnp.zeros(C1, jnp.float32)
        inp['training'] = 0
        return inp
    _L0_xattn_all = _L0_xattn_setup()
    _L0_xattn_in = {k: v for k, v in _L0_xattn_all.items() if k in ('ln1_g', 'ln1_b', 'ln2_g', 'ln2_b', 'a1_wq', 'a1_wk', 'a1_wv', 'a1_li1_w', 'a1_li1_b', 'a1_lnx_g', 'a1_lnx_b', 'a1_lny_g', 'a1_lny_b', 'a1_ln3_g', 'a1_ln3_b', 'a1_li2_w', 'a1_li2_b', 'a1_li3_w', 'a1_li3_b', 'a2_wq', 'a2_wk', 'a2_wv', 'a2_li1_w', 'a2_li1_b', 'a2_lnx_g', 'a2_lnx_b', 'a2_lny_g', 'a2_lny_b', 'a2_ln3_g', 'a2_ln3_b', 'a2_li2_w', 'a2_li2_b', 'a2_li3_w', 'a2_li3_b')}
    del _L0_xattn_all

    def _L0_attn_setup():
        import jax, jax.numpy as jnp
        import numpy as np
        B, N, E, H, DEPTH = (2, 512, 256, 8, 12)
        D = E // H // 2
        LN_EPS = 1e-05
        key = jax.random.key(seed)
        ks = jax.random.split(key, 10)
        w = lambda k: jax.random.normal(k, (E, E), jnp.float32) * E ** (-0.5)
        lp = lambda k: jax.random.normal(k, (D,), jnp.float32) * 0.1
        return {'x': jax.random.normal(ks[0], (B, N, E), jnp.float32), 'Wq': w(ks[1]), 'Wk': w(ks[2]), 'Wv': w(ks[3]), 'Wo': w(ks[4]), 'lq1': lp(ks[5]), 'lk1': lp(ks[6]), 'lq2': lp(ks[7]), 'lk2': lp(ks[8]), 'ln_g': jnp.ones((2 * D,), jnp.float32), 'ln_b': jnp.zeros((2 * D,), jnp.float32)}
    _L0_attn_all = _L0_attn_setup()
    _L0_attn_in = {k: v for k, v in _L0_attn_all.items() if k in ('Wq', 'Wk', 'Wv', 'Wo', 'lq1', 'lk1', 'lq2', 'lk2', 'ln_g', 'ln_b')}
    del _L0_attn_all

    def _L0_ffn_setup():
        import jax, jax.numpy as jnp
        import numpy as np
        B, S, H, E, K = (2, 512, 256, 8, 2)
        FF = 4 * H
        EPS = 1e-05
        key = jax.random.key(seed)
        ks = jax.random.split(key, 5)
        rn = lambda k, shape, scale: jax.random.normal(k, shape, dtype=jnp.float32) * scale
        return {'x': rn(ks[0], (B, S, H), 1.0), 'router_W': rn(ks[1], (H, E), H ** (-0.5)), 'router_b': jnp.zeros((E,), jnp.float32), 'ln_g': jnp.ones((E, H), jnp.float32), 'ln_b': jnp.zeros((E, H), jnp.float32), 'W1': rn(ks[2], (E, H, FF), H ** (-0.5)), 'b1': jnp.zeros((E, FF), jnp.float32), 'W2': rn(ks[3], (E, FF, H), FF ** (-0.5)), 'b2': jnp.zeros((E, H), jnp.float32)}
    _L0_ffn_all = _L0_ffn_setup()
    _L0_ffn_in = {k: v for k, v in _L0_ffn_all.items() if k in ('router_W', 'router_b', 'ln_g', 'ln_b', 'W1', 'b1', 'W2', 'b2')}
    del _L0_ffn_all

    def _L1_xattn_setup():
        import jax, jax.numpy as jnp
        import numpy as np
        HEADS = 16
        D_MODEL = 256
        IMG_MODEL = 128
        D_K = D_MODEL // HEADS
        key = jax.random.key(seed)
        ks = jax.random.split(key, 12)
        B, LQ, LKV = (8, 512, 256)
        s_dm = 1.0 / np.sqrt(D_MODEL)
        s_im = 1.0 / np.sqrt(IMG_MODEL)
        return {'q': jax.random.normal(ks[0], (B, LQ, D_MODEL), jnp.float32), 'k': jax.random.normal(ks[1], (B, LKV, IMG_MODEL), jnp.float32), 'v': jax.random.normal(ks[2], (B, LKV, IMG_MODEL), jnp.float32), 'Wq': jax.random.normal(ks[3], (D_MODEL, D_MODEL), jnp.float32) * s_dm, 'bq': jnp.zeros((D_MODEL,), jnp.float32), 'Wk': jax.random.normal(ks[4], (IMG_MODEL, D_MODEL), jnp.float32) * s_im, 'bk': jnp.zeros((D_MODEL,), jnp.float32), 'Wv': jax.random.normal(ks[5], (IMG_MODEL, D_MODEL), jnp.float32) * s_im, 'bv': jnp.zeros((D_MODEL,), jnp.float32), 'Wo': jax.random.normal(ks[6], (D_MODEL, D_MODEL), jnp.float32) * s_dm, 'bo': jnp.zeros((D_MODEL,), jnp.float32)}
    _L1_xattn_all = _L1_xattn_setup()
    _L1_xattn_in = {k: v for k, v in _L1_xattn_all.items() if k in ('Wq', 'bq', 'Wk', 'bk', 'Wv', 'bv', 'Wo', 'bo')}
    del _L1_xattn_all

    def _L1_attn_setup():
        import jax, jax.numpy as jnp
        import numpy as np
        D_MODEL, D_STATE, EXPAND = (256, 16, 2)
        D_INNER = D_MODEL * EXPAND
        LN_EPS = 1e-05
        key = jax.random.key(seed)
        ks = jax.random.split(key, 10)
        B, T = (2, 1024)
        s_in = 1.0 / np.sqrt(D_MODEL)
        s_inner = 1.0 / np.sqrt(D_INNER)
        return {'x': jax.random.normal(ks[0], (B, T, D_MODEL), jnp.float32), 'norm_w': jnp.ones((D_MODEL,), jnp.float32), 'norm_b': jnp.zeros((D_MODEL,), jnp.float32), 'W_in': jax.random.normal(ks[1], (D_MODEL, D_INNER), jnp.float32) * s_in, 'W_gate': jax.random.normal(ks[2], (D_MODEL, D_INNER), jnp.float32) * s_in, 'W_dt': jax.random.normal(ks[3], (D_INNER, D_INNER), jnp.float32) * s_inner, 'b_dt': jax.random.normal(ks[4], (D_INNER,), jnp.float32) * 0.01, 'W_B': jax.random.normal(ks[5], (D_INNER, D_STATE), jnp.float32) * s_inner, 'W_C': jax.random.normal(ks[6], (D_INNER, D_STATE), jnp.float32) * s_inner, 'A_log': -jax.random.uniform(ks[7], (D_INNER, D_STATE), jnp.float32) * 0.5, 'W_out': jax.random.normal(ks[8], (D_INNER, D_MODEL), jnp.float32) * s_inner}
    _L1_attn_all = _L1_attn_setup()
    _L1_attn_in = {k: v for k, v in _L1_attn_all.items() if k in ('norm_w', 'norm_b', 'W_in', 'W_gate', 'W_dt', 'b_dt', 'W_B', 'W_C', 'A_log', 'W_out')}
    del _L1_attn_all

    def _L1_ffn_setup():
        import jax, jax.numpy as jnp
        import numpy as np
        B, S, D, F, E, K = (4, 512, 256, 1024, 8, 2)
        key = jax.random.key(seed)
        ks = jax.random.split(key, 8)
        x = jax.random.normal(ks[0], (B, S, D), dtype=jnp.float32)
        router_w = jax.random.normal(ks[1], (E, D), dtype=jnp.float32) * 0.02
        w1_w = jax.random.normal(ks[2], (E, F, D), dtype=jnp.float32) * 0.02
        w1_b = jax.random.normal(ks[3], (E, F), dtype=jnp.float32) * 0.02
        w2_w = jax.random.normal(ks[4], (E, D, F), dtype=jnp.float32) * 0.02
        w2_b = jax.random.normal(ks[5], (E, D), dtype=jnp.float32) * 0.02
        wg_w = jax.random.normal(ks[6], (E, F, D), dtype=jnp.float32) * 0.02
        wg_b = jax.random.normal(ks[7], (E, F), dtype=jnp.float32) * 0.02
        return {'x': x, 'router_w': router_w, 'w1_w': w1_w, 'w1_b': w1_b, 'w2_w': w2_w, 'w2_b': w2_b, 'wg_w': wg_w, 'wg_b': wg_b}
    _L1_ffn_all = _L1_ffn_setup()
    _L1_ffn_in = {k: v for k, v in _L1_ffn_all.items() if k in ('router_w', 'w1_w', 'w1_b', 'w2_w', 'w2_b', 'wg_w', 'wg_b')}
    del _L1_ffn_all

    def _L2_xattn_setup():
        import jax, jax.numpy as jnp
        import numpy as np
        B, LQ, LK = (8, 512, 512)
        QD, KD, VD = (256, 128, 128)
        key = jax.random.key(seed)
        ks = jax.random.split(key, 9)
        s = 0.02
        return {'query': jax.random.normal(ks[0], (B, LQ, QD), jnp.float32), 'key': jax.random.normal(ks[1], (B, LK, KD), jnp.float32), 'value': jax.random.normal(ks[2], (B, LK, VD), jnp.float32), 'Wq': jax.random.normal(ks[3], (QD, QD), jnp.float32) * s, 'bq': jnp.zeros((QD,), jnp.float32), 'Wk': jax.random.normal(ks[4], (KD, QD), jnp.float32) * s, 'bk': jnp.zeros((QD,), jnp.float32), 'Wv': jax.random.normal(ks[5], (VD, QD), jnp.float32) * s, 'bv': jnp.zeros((QD,), jnp.float32)}
    _L2_xattn_all = _L2_xattn_setup()
    _L2_xattn_in = {k: v for k, v in _L2_xattn_all.items() if k in ('Wq', 'bq', 'Wk', 'bk', 'Wv', 'bv')}
    del _L2_xattn_all

    def _L2_attn_setup():
        import jax, jax.numpy as jnp
        import numpy as np
        DIM = 256
        H = 16
        D = DIM // H
        HID = H * D
        N, T = (2, 256)
        key = jax.random.key(seed)
        ks = jax.random.split(key, 6)
        x = jax.random.normal(ks[0], (N, T, DIM), dtype=jnp.float32)
        key_w = jax.random.normal(ks[1], (HID, DIM), dtype=jnp.float32) * DIM ** (-0.5)
        key_b = jax.random.uniform(ks[2], (HID,), minval=-4.0, maxval=4.0, dtype=jnp.float32)
        vq_w = jax.random.normal(ks[3], (2 * HID, DIM), dtype=jnp.float32) * DIM ** (-0.5)
        out_w = jax.random.normal(ks[4], (DIM, HID), dtype=jnp.float32) * HID ** (-0.5)
        out_b = jax.random.normal(ks[5], (DIM,), dtype=jnp.float32) * 0.02
        return {'x': x, 'key_w': key_w, 'key_b': key_b, 'vq_w': vq_w, 'out_w': out_w, 'out_b': out_b}
    _L2_attn_all = _L2_attn_setup()
    _L2_attn_in = {k: v for k, v in _L2_attn_all.items() if k in ('key_w', 'key_b', 'vq_w', 'out_w', 'out_b')}
    del _L2_attn_all

    def _L2_ffn_setup():
        import jax, jax.numpy as jnp
        import numpy as np
        B, S, D, E, K = (2, 512, 256, 8, 2)
        H = 4 * D
        key = jax.random.key(seed)
        ks = jax.random.split(key, 6)
        x = jax.random.normal(ks[0], (B, S, D), dtype=jnp.float32)
        lim_g = np.sqrt(6.0 / (D + E)).astype(np.float32)
        W_gate = jax.random.uniform(ks[1], (D, E), minval=-lim_g, maxval=lim_g, dtype=jnp.float32)
        lim1 = np.sqrt(1.0 / D).astype(np.float32)
        lim2 = np.sqrt(1.0 / H).astype(np.float32)
        W1 = jax.random.uniform(ks[2], (E, D, H), minval=-lim1, maxval=lim1, dtype=jnp.float32)
        b1 = jax.random.uniform(ks[3], (E, H), minval=-lim1, maxval=lim1, dtype=jnp.float32)
        W2 = jax.random.uniform(ks[4], (E, H, D), minval=-lim2, maxval=lim2, dtype=jnp.float32)
        b2 = jax.random.uniform(ks[5], (E, D), minval=-lim2, maxval=lim2, dtype=jnp.float32)
        return {'x': x, 'W_gate': W_gate, 'W1': W1, 'b1': b1, 'W2': W2, 'b2': b2}
    _L2_ffn_all = _L2_ffn_setup()
    _L2_ffn_in = {k: v for k, v in _L2_ffn_all.items() if k in ('W_gate', 'W1', 'b1', 'W2', 'b2')}
    del _L2_ffn_all

    def _L3_xattn_setup():
        import jax, jax.numpy as jnp
        import numpy as np
        DIM = 256
        LATENT_DIM = 128
        NUM_HEADS = 16
        HEAD_DIM = DIM // NUM_HEADS
        SCALE = HEAD_DIM ** (-0.5)
        key = jax.random.key(seed)
        k1, k2, k3, k4, k5 = jax.random.split(key, 5)
        B, xN, zN = (2, 512, 512)
        x = jax.random.normal(k1, (B, xN, DIM), dtype=jnp.float32)
        z = jax.random.normal(k2, (B, zN, LATENT_DIM), dtype=jnp.float32)
        Wq = jax.random.normal(k3, (DIM, DIM), dtype=jnp.float32) * DIM ** (-0.5)
        Wkv = jax.random.normal(k4, (2 * DIM, LATENT_DIM), dtype=jnp.float32) * LATENT_DIM ** (-0.5)
        Wo = jax.random.normal(k5, (DIM, DIM), dtype=jnp.float32) * DIM ** (-0.5)
        return {'x': x, 'z': z, 'Wq': Wq, 'Wkv': Wkv, 'Wo': Wo}
    _L3_xattn_all = _L3_xattn_setup()
    _L3_xattn_in = {k: v for k, v in _L3_xattn_all.items() if k in ('Wq', 'Wkv', 'Wo')}
    del _L3_xattn_all

    def _L3_attn_setup():
        import jax, jax.numpy as jnp
        import numpy as np
        B, N, D = (4, 512, 256)
        H, HD = (16, 64)
        MAX_SEQ = 1024
        INNER = H * HD

        def _rope_tables(n, head_dim):
            inv_freq = 1.0 / 10000.0 ** (jnp.arange(0, head_dim, 2, dtype=jnp.float32) / head_dim)
            pos = jnp.arange(n, dtype=jnp.float32)
            ang = pos[:, None] * inv_freq[None, :]
            return (jnp.sin(ang), jnp.cos(ang))
        key = jax.random.key(seed)
        ks = jax.random.split(key, 5)
        s = 0.02
        return {'x': jax.random.normal(ks[0], (B, N, D), dtype=jnp.float32), 'ln_gamma': jnp.ones((D,), jnp.float32), 'ln_beta': jnp.zeros((D,), jnp.float32), 'w_qkv': jax.random.normal(ks[1], (D, 3 * INNER), dtype=jnp.float32) * s, 'w_out': jax.random.normal(ks[2], (INNER, D), dtype=jnp.float32) * s, 'b_out': jnp.zeros((D,), jnp.float32)}
    _L3_attn_all = _L3_attn_setup()
    _L3_attn_in = {k: v for k, v in _L3_attn_all.items() if k in ('ln_gamma', 'ln_beta', 'w_qkv', 'w_out', 'b_out')}
    del _L3_attn_all

    def _L3_ffn_setup():
        import jax, jax.numpy as jnp
        import numpy as np
        B, T, D, E, H = (4, 512, 256, 4, 8)
        EPS = 1e-05

        def _uniform(k, shape, bound):
            return jax.random.uniform(k, shape, jnp.float32, -bound, bound)

        def _layernorm(x, w, b):
            mu = jnp.mean(x, axis=-1, keepdims=True)
            var = jnp.mean(jnp.square(x - mu), axis=-1, keepdims=True)
            return (x - mu) * jax.lax.rsqrt(var + EPS) * w + b
        key = jax.random.key(seed)
        ks = jax.random.split(key, 12)
        wb = np.sqrt(6.0 / D) / np.sqrt(6.0)
        wb = 1.0 / np.sqrt(D)
        return {'x': jax.random.normal(ks[0], (B, T, D), jnp.float32), 'router_prob': jax.random.uniform(ks[1], (B, T, E), jnp.float32), 'norm_w': jnp.ones((D,), jnp.float32), 'norm_b': jnp.zeros((D,), jnp.float32), 'q_w': _uniform(ks[2], (D, D), wb), 'q_b': _uniform(ks[3], (D,), wb), 'k_w': _uniform(ks[4], (D, D), wb), 'k_b': _uniform(ks[5], (D,), wb), 'v_w': _uniform(ks[6], (D, D), wb), 'v_b': _uniform(ks[7], (D,), wb), 'o_w': _uniform(ks[8], (D, D), wb), 'o_b': _uniform(ks[9], (D,), wb)}
    _L3_ffn_all = _L3_ffn_setup()
    _L3_ffn_in = {k: v for k, v in _L3_ffn_all.items() if k in ('router_prob', 'norm_w', 'norm_b', 'q_w', 'q_b', 'k_w', 'k_b', 'v_w', 'v_b', 'o_w', 'o_b')}
    del _L3_ffn_all
    return {'x': x, 'ctx_512': ctx_512, 'L0_xattn_ln1_g': _L0_xattn_in['ln1_g'], 'L0_xattn_ln1_b': _L0_xattn_in['ln1_b'], 'L0_xattn_ln2_g': _L0_xattn_in['ln2_g'], 'L0_xattn_ln2_b': _L0_xattn_in['ln2_b'], 'L0_xattn_a1_wq': _L0_xattn_in['a1_wq'], 'L0_xattn_a1_wk': _L0_xattn_in['a1_wk'], 'L0_xattn_a1_wv': _L0_xattn_in['a1_wv'], 'L0_xattn_a1_li1_w': _L0_xattn_in['a1_li1_w'], 'L0_xattn_a1_li1_b': _L0_xattn_in['a1_li1_b'], 'L0_xattn_a1_lnx_g': _L0_xattn_in['a1_lnx_g'], 'L0_xattn_a1_lnx_b': _L0_xattn_in['a1_lnx_b'], 'L0_xattn_a1_lny_g': _L0_xattn_in['a1_lny_g'], 'L0_xattn_a1_lny_b': _L0_xattn_in['a1_lny_b'], 'L0_xattn_a1_ln3_g': _L0_xattn_in['a1_ln3_g'], 'L0_xattn_a1_ln3_b': _L0_xattn_in['a1_ln3_b'], 'L0_xattn_a1_li2_w': _L0_xattn_in['a1_li2_w'], 'L0_xattn_a1_li2_b': _L0_xattn_in['a1_li2_b'], 'L0_xattn_a1_li3_w': _L0_xattn_in['a1_li3_w'], 'L0_xattn_a1_li3_b': _L0_xattn_in['a1_li3_b'], 'L0_xattn_a2_wq': _L0_xattn_in['a2_wq'], 'L0_xattn_a2_wk': _L0_xattn_in['a2_wk'], 'L0_xattn_a2_wv': _L0_xattn_in['a2_wv'], 'L0_xattn_a2_li1_w': _L0_xattn_in['a2_li1_w'], 'L0_xattn_a2_li1_b': _L0_xattn_in['a2_li1_b'], 'L0_xattn_a2_lnx_g': _L0_xattn_in['a2_lnx_g'], 'L0_xattn_a2_lnx_b': _L0_xattn_in['a2_lnx_b'], 'L0_xattn_a2_lny_g': _L0_xattn_in['a2_lny_g'], 'L0_xattn_a2_lny_b': _L0_xattn_in['a2_lny_b'], 'L0_xattn_a2_ln3_g': _L0_xattn_in['a2_ln3_g'], 'L0_xattn_a2_ln3_b': _L0_xattn_in['a2_ln3_b'], 'L0_xattn_a2_li2_w': _L0_xattn_in['a2_li2_w'], 'L0_xattn_a2_li2_b': _L0_xattn_in['a2_li2_b'], 'L0_xattn_a2_li3_w': _L0_xattn_in['a2_li3_w'], 'L0_xattn_a2_li3_b': _L0_xattn_in['a2_li3_b'], 'L0_attn_Wq': _L0_attn_in['Wq'], 'L0_attn_Wk': _L0_attn_in['Wk'], 'L0_attn_Wv': _L0_attn_in['Wv'], 'L0_attn_Wo': _L0_attn_in['Wo'], 'L0_attn_lq1': _L0_attn_in['lq1'], 'L0_attn_lk1': _L0_attn_in['lk1'], 'L0_attn_lq2': _L0_attn_in['lq2'], 'L0_attn_lk2': _L0_attn_in['lk2'], 'L0_attn_ln_g': _L0_attn_in['ln_g'], 'L0_attn_ln_b': _L0_attn_in['ln_b'], 'L0_ffn_router_W': _L0_ffn_in['router_W'], 'L0_ffn_router_b': _L0_ffn_in['router_b'], 'L0_ffn_ln_g': _L0_ffn_in['ln_g'], 'L0_ffn_ln_b': _L0_ffn_in['ln_b'], 'L0_ffn_W1': _L0_ffn_in['W1'], 'L0_ffn_b1': _L0_ffn_in['b1'], 'L0_ffn_W2': _L0_ffn_in['W2'], 'L0_ffn_b2': _L0_ffn_in['b2'], 'L1_xattn_Wq': _L1_xattn_in['Wq'], 'L1_xattn_bq': _L1_xattn_in['bq'], 'L1_xattn_Wk': _L1_xattn_in['Wk'], 'L1_xattn_bk': _L1_xattn_in['bk'], 'L1_xattn_Wv': _L1_xattn_in['Wv'], 'L1_xattn_bv': _L1_xattn_in['bv'], 'L1_xattn_Wo': _L1_xattn_in['Wo'], 'L1_xattn_bo': _L1_xattn_in['bo'], 'L1_attn_norm_w': _L1_attn_in['norm_w'], 'L1_attn_norm_b': _L1_attn_in['norm_b'], 'L1_attn_W_in': _L1_attn_in['W_in'], 'L1_attn_W_gate': _L1_attn_in['W_gate'], 'L1_attn_W_dt': _L1_attn_in['W_dt'], 'L1_attn_b_dt': _L1_attn_in['b_dt'], 'L1_attn_W_B': _L1_attn_in['W_B'], 'L1_attn_W_C': _L1_attn_in['W_C'], 'L1_attn_A_log': _L1_attn_in['A_log'], 'L1_attn_W_out': _L1_attn_in['W_out'], 'L1_ffn_router_w': _L1_ffn_in['router_w'], 'L1_ffn_w1_w': _L1_ffn_in['w1_w'], 'L1_ffn_w1_b': _L1_ffn_in['w1_b'], 'L1_ffn_w2_w': _L1_ffn_in['w2_w'], 'L1_ffn_w2_b': _L1_ffn_in['w2_b'], 'L1_ffn_wg_w': _L1_ffn_in['wg_w'], 'L1_ffn_wg_b': _L1_ffn_in['wg_b'], 'L2_xattn_Wq': _L2_xattn_in['Wq'], 'L2_xattn_bq': _L2_xattn_in['bq'], 'L2_xattn_Wk': _L2_xattn_in['Wk'], 'L2_xattn_bk': _L2_xattn_in['bk'], 'L2_xattn_Wv': _L2_xattn_in['Wv'], 'L2_xattn_bv': _L2_xattn_in['bv'], 'L2_attn_key_w': _L2_attn_in['key_w'], 'L2_attn_key_b': _L2_attn_in['key_b'], 'L2_attn_vq_w': _L2_attn_in['vq_w'], 'L2_attn_out_w': _L2_attn_in['out_w'], 'L2_attn_out_b': _L2_attn_in['out_b'], 'L2_ffn_W_gate': _L2_ffn_in['W_gate'], 'L2_ffn_W1': _L2_ffn_in['W1'], 'L2_ffn_b1': _L2_ffn_in['b1'], 'L2_ffn_W2': _L2_ffn_in['W2'], 'L2_ffn_b2': _L2_ffn_in['b2'], 'L3_xattn_Wq': _L3_xattn_in['Wq'], 'L3_xattn_Wkv': _L3_xattn_in['Wkv'], 'L3_xattn_Wo': _L3_xattn_in['Wo'], 'L3_attn_ln_gamma': _L3_attn_in['ln_gamma'], 'L3_attn_ln_beta': _L3_attn_in['ln_beta'], 'L3_attn_w_qkv': _L3_attn_in['w_qkv'], 'L3_attn_w_out': _L3_attn_in['w_out'], 'L3_attn_b_out': _L3_attn_in['b_out'], 'L3_ffn_router_prob': _L3_ffn_in['router_prob'], 'L3_ffn_norm_w': _L3_ffn_in['norm_w'], 'L3_ffn_norm_b': _L3_ffn_in['norm_b'], 'L3_ffn_q_w': _L3_ffn_in['q_w'], 'L3_ffn_q_b': _L3_ffn_in['q_b'], 'L3_ffn_k_w': _L3_ffn_in['k_w'], 'L3_ffn_k_b': _L3_ffn_in['k_b'], 'L3_ffn_v_w': _L3_ffn_in['v_w'], 'L3_ffn_v_b': _L3_ffn_in['v_b'], 'L3_ffn_o_w': _L3_ffn_in['o_w'], 'L3_ffn_o_b': _L3_ffn_in['o_b']}

def reference(x, ctx_512, L0_xattn_ln1_g, L0_xattn_ln1_b, L0_xattn_ln2_g, L0_xattn_ln2_b, L0_xattn_a1_wq, L0_xattn_a1_wk, L0_xattn_a1_wv, L0_xattn_a1_li1_w, L0_xattn_a1_li1_b, L0_xattn_a1_lnx_g, L0_xattn_a1_lnx_b, L0_xattn_a1_lny_g, L0_xattn_a1_lny_b, L0_xattn_a1_ln3_g, L0_xattn_a1_ln3_b, L0_xattn_a1_li2_w, L0_xattn_a1_li2_b, L0_xattn_a1_li3_w, L0_xattn_a1_li3_b, L0_xattn_a2_wq, L0_xattn_a2_wk, L0_xattn_a2_wv, L0_xattn_a2_li1_w, L0_xattn_a2_li1_b, L0_xattn_a2_lnx_g, L0_xattn_a2_lnx_b, L0_xattn_a2_lny_g, L0_xattn_a2_lny_b, L0_xattn_a2_ln3_g, L0_xattn_a2_ln3_b, L0_xattn_a2_li2_w, L0_xattn_a2_li2_b, L0_xattn_a2_li3_w, L0_xattn_a2_li3_b, L0_attn_Wq, L0_attn_Wk, L0_attn_Wv, L0_attn_Wo, L0_attn_lq1, L0_attn_lk1, L0_attn_lq2, L0_attn_lk2, L0_attn_ln_g, L0_attn_ln_b, L0_ffn_router_W, L0_ffn_router_b, L0_ffn_ln_g, L0_ffn_ln_b, L0_ffn_W1, L0_ffn_b1, L0_ffn_W2, L0_ffn_b2, L1_xattn_Wq, L1_xattn_bq, L1_xattn_Wk, L1_xattn_bk, L1_xattn_Wv, L1_xattn_bv, L1_xattn_Wo, L1_xattn_bo, L1_attn_norm_w, L1_attn_norm_b, L1_attn_W_in, L1_attn_W_gate, L1_attn_W_dt, L1_attn_b_dt, L1_attn_W_B, L1_attn_W_C, L1_attn_A_log, L1_attn_W_out, L1_ffn_router_w, L1_ffn_w1_w, L1_ffn_w1_b, L1_ffn_w2_w, L1_ffn_w2_b, L1_ffn_wg_w, L1_ffn_wg_b, L2_xattn_Wq, L2_xattn_bq, L2_xattn_Wk, L2_xattn_bk, L2_xattn_Wv, L2_xattn_bv, L2_attn_key_w, L2_attn_key_b, L2_attn_vq_w, L2_attn_out_w, L2_attn_out_b, L2_ffn_W_gate, L2_ffn_W1, L2_ffn_b1, L2_ffn_W2, L2_ffn_b2, L3_xattn_Wq, L3_xattn_Wkv, L3_xattn_Wo, L3_attn_ln_gamma, L3_attn_ln_beta, L3_attn_w_qkv, L3_attn_w_out, L3_attn_b_out, L3_ffn_router_prob, L3_ffn_norm_w, L3_ffn_norm_b, L3_ffn_q_w, L3_ffn_q_b, L3_ffn_k_w, L3_ffn_k_b, L3_ffn_v_w, L3_ffn_v_b, L3_ffn_o_w, L3_ffn_o_b):
    import jax
    import jax.numpy as jnp

    def _L0_xattn_ref(xx, ee, ln1_g, ln1_b, ln2_g, ln2_b, a1_wq, a1_wk, a1_wv, a1_li1_w, a1_li1_b, a1_lnx_g, a1_lnx_b, a1_lny_g, a1_lny_b, a1_ln3_g, a1_ln3_b, a1_li2_w, a1_li2_b, a1_li3_w, a1_li3_b, a2_wq, a2_wk, a2_wv, a2_li1_w, a2_li1_b, a2_lnx_g, a2_lnx_b, a2_lny_g, a2_lny_b, a2_ln3_g, a2_ln3_b, a2_li2_w, a2_li2_b, a2_li3_w, a2_li3_b, training):
        import jax, jax.numpy as jnp
        import numpy as np
        H, D, C1, C2, S, M, B, W = (16, 32, 256, 128, 512, 128, 2, 4)

        def _ln(x, g, b):
            m = jnp.mean(x, -1, keepdims=True)
            v = jnp.var(x, -1, keepdims=True)
            return (x - m) * jax.lax.rsqrt(v + 1e-05) * g + b

        def _mha(x, y, wq, wk, wv, li1_w, li1_b, lnx_g, lnx_b, lny_g, lny_b, ln3_g, ln3_b, li2_w, li2_b, li3_w, li3_b, causal):
            xn = _ln(x, lnx_g, lnx_b)
            yn = _ln(y, lny_g, lny_b)
            q = jnp.einsum('bsc,hcd->bhsd', xn, wq)
            k = jnp.einsum('btc,hcd->bhtd', yn, wk)
            v = jnp.einsum('btc,hcd->bhtd', yn, wv)
            a = jax.nn.softmax(jnp.einsum('bhsd,bhtd->bhst', q, k) * D ** (-0.5), axis=-1)
            if causal:
                s, t = (a.shape[-2], a.shape[-1])
                mask = (jnp.arange(t)[None, :] > jnp.arange(s)[:, None]).astype(a.dtype)
                a = a * mask
            o = jnp.einsum('bhst,bhtd->bhsd', a, v)
            o = o.transpose(0, 2, 1, 3).reshape(x.shape[0], x.shape[1], H * D)
            x_out = x + o @ li1_w + li1_b
            h = jax.nn.gelu(_ln(x_out, ln3_g, ln3_b) @ li2_w + li2_b, approximate=False)
            return x_out + h @ li3_w + li3_b
        x = _ln(xx, ln1_g, ln1_b)
        x = x + _mha(x, x, a1_wq, a1_wk, a1_wv, a1_li1_w, a1_li1_b, a1_lnx_g, a1_lnx_b, a1_lny_g, a1_lny_b, a1_ln3_g, a1_ln3_b, a1_li2_w, a1_li2_b, a1_li3_w, a1_li3_b, causal=True)
        x = _ln(x, ln2_g, ln2_b)
        return x + _mha(x, ee, a2_wq, a2_wk, a2_wv, a2_li1_w, a2_li1_b, a2_lnx_g, a2_lnx_b, a2_lny_g, a2_lny_b, a2_ln3_g, a2_ln3_b, a2_li2_w, a2_li2_b, a2_li3_w, a2_li3_b, causal=False)

    def _L0_attn_ref(x, Wq, Wk, Wv, Wo, lq1, lk1, lq2, lk2, ln_g, ln_b):
        import jax, jax.numpy as jnp
        import numpy as np
        B, N, E, H, DEPTH = (2, 512, 256, 8, 12)
        D = E // H // 2
        LN_EPS = 1e-05
        b, n, e = x.shape
        lam_init = 0.8 - 0.6 * np.exp(-0.3 * DEPTH)
        q = (x @ Wq).reshape(b, n, 2 * H, D).transpose(0, 2, 1, 3) * D ** (-0.5)
        k = (x @ Wk).reshape(b, n, 2 * H, D).transpose(0, 2, 1, 3)
        v = (x @ Wv).reshape(b, n, H, 2 * D).transpose(0, 2, 1, 3)
        scores = jnp.einsum('bhqd,bhkd->bhqk', q, k)
        attn = jax.nn.softmax(scores, axis=-1).reshape(b, H, 2, n, n)
        lam = jnp.exp(jnp.sum(lq1 * lk1)) - jnp.exp(jnp.sum(lq2 * lk2)) + lam_init
        w_diff = attn[:, :, 0] - lam * attn[:, :, 1]
        o = jnp.einsum('bhqk,bhkd->bhqd', w_diff, v)
        mu = o.mean(-1, keepdims=True)
        var = ((o - mu) ** 2).mean(-1, keepdims=True)
        o = (o - mu) * jax.lax.rsqrt(var + LN_EPS) * ln_g + ln_b
        o = o.transpose(0, 2, 1, 3).reshape(b, n, e)
        return o @ Wo

    def _L0_ffn_ref(x, router_W, router_b, ln_g, ln_b, W1, b1, W2, b2):
        import jax, jax.numpy as jnp
        import numpy as np
        B, S, H, E, K = (2, 512, 256, 8, 2)
        FF = 4 * H
        EPS = 1e-05
        logits = x @ router_W + router_b
        w, idx = jax.lax.top_k(logits, K)
        w = jax.nn.softmax(w, axis=-1)
        gates = jnp.einsum('bske,bsk->bse', jax.nn.one_hot(idx, E, dtype=x.dtype), w)
        mu = jnp.mean(x, axis=-1, keepdims=True)
        var = jnp.mean(jnp.square(x - mu), axis=-1, keepdims=True)
        xhat = (x - mu) * jax.lax.rsqrt(var + EPS)
        h = xhat[:, :, None, :] * ln_g + ln_b
        a = jax.nn.gelu(jnp.einsum('bseh,ehf->bsef', h, W1) + b1, approximate=False)
        y = jnp.einsum('bsef,efh->bseh', a, W2) + b2
        y = y + x[:, :, None, :]
        out = jnp.einsum('bseh,bse->bsh', y, gates)
        return out

    def _L1_xattn_ref(q, k, v, Wq, bq, Wk, bk, Wv, bv, Wo, bo):
        import jax, jax.numpy as jnp
        import numpy as np
        HEADS = 16
        D_MODEL = 256
        IMG_MODEL = 128
        D_K = D_MODEL // HEADS
        B, LQ, _ = q.shape
        LKV = k.shape[1]
        qh = (q @ Wq + bq).reshape(B, LQ, HEADS, D_K).transpose(0, 2, 1, 3)
        kh = (k @ Wk + bk).reshape(B, LKV, HEADS, D_K).transpose(0, 2, 1, 3)
        vh = (v @ Wv + bv).reshape(B, LKV, HEADS, D_K).transpose(0, 2, 1, 3)
        scale = 1.0 / np.sqrt(D_K)
        scores = jnp.einsum('bhqd,bhkd->bhqk', qh, kh) * scale
        attn = jax.nn.softmax(scores, axis=-1)
        out = jnp.einsum('bhqk,bhkd->bhqd', attn, vh)
        concat = out.transpose(0, 2, 1, 3).reshape(B, LQ, D_MODEL)
        return concat @ Wo + bo

    def _L1_attn_ref(x, norm_w, norm_b, W_in, W_gate, W_dt, b_dt, W_B, W_C, A_log, W_out):
        import jax, jax.numpy as jnp
        import numpy as np
        D_MODEL, D_STATE, EXPAND = (256, 16, 2)
        D_INNER = D_MODEL * EXPAND
        LN_EPS = 1e-05
        residual = x
        mu = jnp.mean(x, axis=-1, keepdims=True)
        var = jnp.mean((x - mu) ** 2, axis=-1, keepdims=True)
        xn = (x - mu) / jnp.sqrt(var + LN_EPS) * norm_w + norm_b
        z = xn @ W_in
        gate = jax.nn.silu(xn @ W_gate)
        dt = jnp.clip(jax.nn.softplus(z @ W_dt + b_dt), 0.001, 1.0)
        Bp = z @ W_B
        Cp = z @ W_C
        A = -jnp.clip(jnp.exp(A_log), 1e-06, 1.0)
        Bsz, T, d_inner = z.shape
        d_state = Bp.shape[-1]

        def step(h, inp):
            dt_t, B_t, C_t, z_t = inp
            dA = jnp.exp(jnp.clip(dt_t[:, :, None] * A, -20.0, 0.0))
            dB = dt_t[:, :, None] * B_t[:, None, :]
            h = dA * h + dB * z_t[:, :, None]
            y_t = jnp.einsum('bds,bs->bd', h, C_t)
            return (h, y_t)
        h0 = jnp.zeros((Bsz, d_inner, d_state), jnp.float32)
        seq = (jnp.swapaxes(dt, 0, 1), jnp.swapaxes(Bp, 0, 1), jnp.swapaxes(Cp, 0, 1), jnp.swapaxes(z, 0, 1))
        _, ys = jax.lax.scan(step, h0, seq)
        y = jnp.swapaxes(ys, 0, 1) * gate
        return residual + y @ W_out

    def _L1_ffn_ref(x, router_w, w1_w, w1_b, w2_w, w2_b, wg_w, wg_b):
        import jax, jax.numpy as jnp
        import numpy as np
        B, S, D, F, E, K = (4, 512, 256, 1024, 8, 2)
        probs = jax.nn.softmax(jnp.einsum('bsd,ed->bse', x, router_w), axis=-1)
        token_probs, probs_idx = jax.lax.top_k(probs, K)
        gates = jnp.sum(token_probs[..., None] * jax.nn.one_hot(probs_idx, E, dtype=x.dtype), axis=-2)
        gates_e = jnp.moveaxis(gates, -1, 0)

        def body(acc, params):
            w1w, w1b, w2w, w2b, wgw, wgb, g = params
            y = jax.nn.gelu(jnp.einsum('bsd,fd->bsf', x, wgw) + wgb, approximate=False)
            h = y * (jnp.einsum('bsd,fd->bsf', x, w1w) + w1b)
            out = jnp.einsum('bsf,df->bsd', h, w2w) + w2b
            return (acc + out * g[..., None], None)
        acc0 = jnp.zeros_like(x)
        out, _ = jax.lax.scan(body, acc0, (w1_w, w1_b, w2_w, w2_b, wg_w, wg_b, gates_e))
        return out

    def _L2_xattn_ref(query, key, value, Wq, bq, Wk, bk, Wv, bv):
        import jax, jax.numpy as jnp
        import numpy as np
        B, LQ, LK = (8, 512, 512)
        QD, KD, VD = (256, 128, 128)
        q = jnp.einsum('bld,de->ble', query, Wq) + bq
        k = jnp.einsum('bld,de->ble', key, Wk) + bk
        v = jnp.einsum('bld,de->ble', value, Wv) + bv
        scores = jnp.einsum('bqe,bke->bqk', q, k)
        attn = jax.nn.softmax(scores, axis=-1)
        out = jnp.einsum('bqk,bke->bqe', attn, v)
        return out

    def _L2_attn_ref(x, key_w, key_b, vq_w, out_w, out_b):
        import jax, jax.numpy as jnp
        import numpy as np
        DIM = 256
        H = 16
        D = DIM // H
        HID = H * D
        N, T = (2, 256)
        n, t, dim = x.shape
        vq = x @ vq_w.T
        v, q = jnp.split(vq, 2, axis=-1)
        k = jax.nn.sigmoid(x @ key_w.T + key_b)
        k = k.reshape(n, t, H, D)
        v = v.reshape(n, t, H, D)
        upd = (1.0 - k)[..., :, None] * v[..., None, :]
        decay = k[..., :, None]

        def combine(c1, c2):
            a1, b1 = c1
            a2, b2 = c2
            return (a1 * a2, b1 * a2 + b2)
        _, kv = jax.lax.associative_scan(combine, (decay, upd), axis=1)
        qh = q.reshape(n, t, H, D)
        h = jnp.einsum('nthd,nthde->nthe', qh, kv).reshape(n, t, HID)
        return h @ out_w.T + out_b

    def _L2_ffn_ref(x, W_gate, W1, b1, W2, b2):
        import jax, jax.numpy as jnp
        import numpy as np
        B, S, D, E, K = (2, 512, 256, 8, 2)
        H = 4 * D
        gate = jnp.einsum('bsd,de->bse', x, W_gate)
        kth = jax.lax.top_k(gate, K)[0][..., -1:]
        mask = jax.nn.softmax(jnp.where(gate >= kth, gate, -jnp.inf), axis=-1)
        h = jax.nn.relu(jnp.einsum('bsd,edh->bseh', x, W1) + b1)
        y = jnp.einsum('bseh,ehd->bsed', h, W2) + b2
        return (y * mask[..., None]).mean(axis=-2)

    def _L3_xattn_ref(x, z, Wq, Wkv, Wo):
        import jax, jax.numpy as jnp
        import numpy as np
        DIM = 256
        LATENT_DIM = 128
        NUM_HEADS = 16
        HEAD_DIM = DIM // NUM_HEADS
        SCALE = HEAD_DIM ** (-0.5)
        B, xN, _ = x.shape
        _, zN, _ = z.shape
        Q = (x @ Wq.T).reshape(B, xN, NUM_HEADS, HEAD_DIM)
        KV = (z @ Wkv.T).reshape(B, zN, 2, NUM_HEADS, HEAD_DIM)
        K = KV[:, :, 0]
        V = KV[:, :, 1]
        attn = jnp.einsum('bqhd,bkhd->bhqk', Q, K) * SCALE
        attn = jax.nn.softmax(attn, axis=-1)
        O = jnp.einsum('bhqk,bkhd->bqhd', attn, V).reshape(B, xN, DIM)
        return O @ Wo.T

    def _L3_attn_ref(x, ln_gamma, ln_beta, w_qkv, w_out, b_out):
        import jax, jax.numpy as jnp
        import numpy as np
        B, N, D = (4, 512, 256)
        H, HD = (16, 64)
        MAX_SEQ = 1024
        INNER = H * HD

        def _rope_tables(n, head_dim):
            inv_freq = 1.0 / 10000.0 ** (jnp.arange(0, head_dim, 2, dtype=jnp.float32) / head_dim)
            pos = jnp.arange(n, dtype=jnp.float32)
            ang = pos[:, None] * inv_freq[None, :]
            return (jnp.sin(ang), jnp.cos(ang))
        b, n, d = x.shape
        mu = jnp.mean(x, axis=-1, keepdims=True)
        var = jnp.var(x, axis=-1, keepdims=True)
        xn = (x - mu) / jnp.sqrt(var + 1e-05) * ln_gamma + ln_beta
        qkv = xn @ w_qkv
        q, k, v = jnp.split(qkv, 3, axis=-1)

        def to_heads(t):
            return t.reshape(b, n, H, HD).transpose(0, 2, 1, 3)
        q, k, v = (to_heads(q), to_heads(k), to_heads(v))
        sin, cos = _rope_tables(n, HD)
        sin = sin[None, None]
        cos = cos[None, None]
        half = HD // 2

        def rotate(t):
            t1, t2 = (t[..., :half], t[..., half:])
            return jnp.concatenate([t1 * cos - t2 * sin, t2 * cos + t1 * sin], axis=-1)
        qr, kr = (rotate(q), rotate(k))
        scale = HD ** (-0.5)
        scores = jnp.einsum('bhid,bhjd->bhij', qr, kr) * scale
        probs = jax.nn.softmax(scores, axis=-1)
        out = jnp.einsum('bhij,bhjd->bhid', probs, v)
        out = out.transpose(0, 2, 1, 3).reshape(b, n, INNER)
        return out @ w_out + b_out

    def _L3_ffn_ref(x, router_prob, norm_w, norm_b, q_w, q_b, k_w, k_b, v_w, v_b, o_w, o_b):
        import jax, jax.numpy as jnp
        import numpy as np
        B, T, D, E, H = (4, 512, 256, 4, 8)
        EPS = 1e-05

        def _uniform(k, shape, bound):
            return jax.random.uniform(k, shape, jnp.float32, -bound, bound)

        def _layernorm(x, w, b):
            mu = jnp.mean(x, axis=-1, keepdims=True)
            var = jnp.mean(jnp.square(x - mu), axis=-1, keepdims=True)
            return (x - mu) * jax.lax.rsqrt(var + EPS) * w + b
        e_cnt = router_prob.shape[2]
        b, t, d = x.shape
        n = t // e_cnt
        h = H
        scale = d ** (-0.5)
        qs, ks_, vs = ([], [], [])
        for e in range(e_cnt):
            xe = x[:, e * n:(e + 1) * n, :]
            xn = _layernorm(xe, norm_w, norm_b)
            m = d // 2 ** e
            xm = xn[..., :m]
            qs.append(jnp.einsum('bnm,dm->bnd', xm, q_w[:, :m]) + q_b)
            ks_.append(jnp.einsum('bnm,dm->bnd', xm, k_w[:, :m]) + k_b)
            vs.append(jnp.einsum('bnm,dm->bnd', xm, v_w[:, :m]) + v_b)
        q = jnp.concatenate(qs, axis=1)
        k = jnp.concatenate(ks_, axis=1)
        v = jnp.concatenate(vs, axis=1)
        dh = d // h
        q = q.reshape(b, t, h, dh).transpose(0, 2, 1, 3)
        k = k.reshape(b, t, h, dh).transpose(0, 2, 1, 3)
        v = v.reshape(b, t, h, dh).transpose(0, 2, 1, 3)
        attn = jnp.einsum('bhqd,bhkd->bhqk', q, k) * scale
        attn = jax.nn.softmax(attn, axis=-1)
        attn_out = jnp.einsum('bhqk,bhkd->bhqd', attn, v)
        attn_out = attn_out.transpose(0, 2, 1, 3).reshape(b, t, d)
        outs = []
        for e in range(e_cnt):
            sl = slice(e * n, (e + 1) * n)
            m = d // 2 ** e
            xm = attn_out[:, sl, :m]
            out = jnp.einsum('bnm,om->bno', xm, o_w[:m, :m]) + o_b[:m]
            pad = d - m
            if pad:
                out = jnp.pad(out, ((0, 0), (0, 0), (0, pad)))
            outs.append(out + x[:, sl, :])
        return jnp.concatenate(outs, axis=1)
    x = x + _L0_xattn_ref(_layernorm(x, axis=-1), ctx_512, L0_xattn_ln1_g, L0_xattn_ln1_b, L0_xattn_ln2_g, L0_xattn_ln2_b, L0_xattn_a1_wq, L0_xattn_a1_wk, L0_xattn_a1_wv, L0_xattn_a1_li1_w, L0_xattn_a1_li1_b, L0_xattn_a1_lnx_g, L0_xattn_a1_lnx_b, L0_xattn_a1_lny_g, L0_xattn_a1_lny_b, L0_xattn_a1_ln3_g, L0_xattn_a1_ln3_b, L0_xattn_a1_li2_w, L0_xattn_a1_li2_b, L0_xattn_a1_li3_w, L0_xattn_a1_li3_b, L0_xattn_a2_wq, L0_xattn_a2_wk, L0_xattn_a2_wv, L0_xattn_a2_li1_w, L0_xattn_a2_li1_b, L0_xattn_a2_lnx_g, L0_xattn_a2_lnx_b, L0_xattn_a2_lny_g, L0_xattn_a2_lny_b, L0_xattn_a2_ln3_g, L0_xattn_a2_ln3_b, L0_xattn_a2_li2_w, L0_xattn_a2_li2_b, L0_xattn_a2_li3_w, L0_xattn_a2_li3_b, 0)
    x = x + _L0_attn_ref(_layernorm(x, axis=-1), L0_attn_Wq, L0_attn_Wk, L0_attn_Wv, L0_attn_Wo, L0_attn_lq1, L0_attn_lk1, L0_attn_lq2, L0_attn_lk2, L0_attn_ln_g, L0_attn_ln_b)
    x = x + _L0_ffn_ref(_layernorm(x, axis=-1), L0_ffn_router_W, L0_ffn_router_b, L0_ffn_ln_g, L0_ffn_ln_b, L0_ffn_W1, L0_ffn_b1, L0_ffn_W2, L0_ffn_b2)
    x = x + _L1_xattn_ref(_layernorm(x, axis=-1), ctx_512, ctx_512, L1_xattn_Wq, L1_xattn_bq, L1_xattn_Wk, L1_xattn_bk, L1_xattn_Wv, L1_xattn_bv, L1_xattn_Wo, L1_xattn_bo)
    x = x + _L1_attn_ref(_layernorm(x, axis=-1), L1_attn_norm_w, L1_attn_norm_b, L1_attn_W_in, L1_attn_W_gate, L1_attn_W_dt, L1_attn_b_dt, L1_attn_W_B, L1_attn_W_C, L1_attn_A_log, L1_attn_W_out)
    x = x + _L1_ffn_ref(_layernorm(x, axis=-1), L1_ffn_router_w, L1_ffn_w1_w, L1_ffn_w1_b, L1_ffn_w2_w, L1_ffn_w2_b, L1_ffn_wg_w, L1_ffn_wg_b)
    x = x + _L2_xattn_ref(_layernorm(x, axis=-1), ctx_512, ctx_512, L2_xattn_Wq, L2_xattn_bq, L2_xattn_Wk, L2_xattn_bk, L2_xattn_Wv, L2_xattn_bv)
    x = x + _L2_attn_ref(_layernorm(x, axis=-1), L2_attn_key_w, L2_attn_key_b, L2_attn_vq_w, L2_attn_out_w, L2_attn_out_b)
    x = x + _L2_ffn_ref(_layernorm(x, axis=-1), L2_ffn_W_gate, L2_ffn_W1, L2_ffn_b1, L2_ffn_W2, L2_ffn_b2)
    x = x + _L3_xattn_ref(_layernorm(x, axis=-1), ctx_512, L3_xattn_Wq, L3_xattn_Wkv, L3_xattn_Wo)
    x = x + _L3_attn_ref(_layernorm(x, axis=-1), L3_attn_ln_gamma, L3_attn_ln_beta, L3_attn_w_qkv, L3_attn_w_out, L3_attn_b_out)
    x = x + _L3_ffn_ref(_layernorm(x, axis=-1), L3_ffn_router_prob, L3_ffn_norm_w, L3_ffn_norm_b, L3_ffn_q_w, L3_ffn_q_b, L3_ffn_k_w, L3_ffn_k_b, L3_ffn_v_w, L3_ffn_v_b, L3_ffn_o_w, L3_ffn_o_b)
    return x

_drawn_inputs = setup_inputs


def setup_inputs(seed=0):
    import zlib

    import numpy as np

    out = dict(_drawn_inputs(seed))
    spreads = {'L0_xattn_ln1_g': (1.0, 0.2),
     'L0_xattn_ln1_b': (0.0, 0.1),
     'L0_xattn_ln2_g': (1.0, 0.2),
     'L0_xattn_ln2_b': (0.0, 0.1),
     'L0_xattn_a1_li1_b': (0.0, 0.1),
     'L0_xattn_a1_lnx_g': (1.0, 0.6),
     'L0_xattn_a1_lnx_b': (0.0, 0.8),
     'L0_xattn_a1_lny_g': (1.0, 0.6),
     'L0_xattn_a1_lny_b': (0.0, 0.8),
     'L0_xattn_a1_ln3_g': (1.0, 0.6),
     'L0_xattn_a1_ln3_b': (0.0, 0.561),
     'L0_xattn_a1_li2_b': (0.0, 0.351),
     'L0_xattn_a1_li3_b': (0.0, 0.1),
     'L0_xattn_a2_li1_b': (0.0, 0.1),
     'L0_xattn_a2_lnx_g': (1.0, 0.6),
     'L0_xattn_a2_lnx_b': (0.0, 0.8),
     'L0_xattn_a2_lny_g': (1.0, 0.6),
     'L0_xattn_a2_lny_b': (0.0, 0.8),
     'L0_xattn_a2_ln3_g': (1.0, 0.6),
     'L0_xattn_a2_ln3_b': (0.0, 0.8),
     'L0_xattn_a2_li2_b': (0.0, 0.329),
     'L0_xattn_a2_li3_b': (0.0, 0.1),
     'L0_attn_ln_g': (1.0, 0.2),
     'L0_attn_ln_b': (0.0, 0.1),
     'L0_ffn_router_b': (0.0, 0.1),
     'L0_ffn_ln_g': (1.0, 0.2),
     'L0_ffn_ln_b': (0.0, 0.488),
     'L0_ffn_b1': (0.0, 0.474),
     'L0_ffn_b2': (0.0, 0.332),
     'L1_xattn_bq': (0.0, 0.8),
     'L1_xattn_bk': (0.0, 2.0),
     'L1_xattn_bv': (0.0, 0.1),
     'L1_xattn_bo': (0.0, 0.1),
     'L1_attn_norm_w': (1.0, 0.2),
     'L1_attn_norm_b': (0.0, 0.1),
     'L2_xattn_bq': (0.0, 0.8),
     'L2_xattn_bk': (0.0, 2.0),
     'L2_xattn_bv': (0.0, 0.417),
     'L3_attn_ln_gamma': (1.0, 0.6),
     'L3_attn_ln_beta': (0.0, 0.8),
     'L3_attn_b_out': (0.0, 0.546),
     'L3_ffn_norm_w': (1.0, 0.6),
     'L3_ffn_norm_b': (0.0, 0.8)}
    factors = {'L0_xattn_a1_wq': 8.0,
     'L0_xattn_a1_wk': 8.0,
     'L0_xattn_a1_wv': 4.465,
     'L0_xattn_a1_li1_w': 4.05,
     'L0_xattn_a2_wq': 8.0,
     'L0_xattn_a2_wk': 8.0,
     'L0_attn_lq1': 5.267,
     'L0_attn_lq2': 3.309,
     'L0_attn_lk2': 2.817,
     'L1_attn_b_dt': 8.0,
     'L1_ffn_router_w': 8.0,
     'L1_ffn_w1_w': 8.0,
     'L1_ffn_w1_b': 8.0,
     'L1_ffn_w2_w': 8.0,
     'L1_ffn_w2_b': 8.0,
     'L1_ffn_wg_w': 8.0,
     'L1_ffn_wg_b': 8.0,
     'L2_xattn_Wq': 5.309,
     'L2_xattn_Wk': 5.14,
     'L2_attn_out_b': 8.0,
     'L2_ffn_W_gate': 8.0,
     'L2_ffn_W1': 8.0,
     'L2_ffn_b1': 8.0,
     'L2_ffn_W2': 8.0,
     'L2_ffn_b2': 64.0,
     'L3_attn_w_qkv': 7.38,
     'L3_attn_w_out': 7.147,
     'L3_ffn_q_w': 8.0,
     'L3_ffn_q_b': 8.0,
     'L3_ffn_k_w': 8.0,
     'L3_ffn_k_b': 64.0,
     'L3_ffn_v_w': 8.0,
     'L3_ffn_v_b': 8.0,
     'L3_ffn_o_w': 8.0,
     'L3_ffn_o_b': 64.0}
    for name, (base, spread) in spreads.items():
        noise = np.random.default_rng([zlib.crc32(name.encode()), seed]).standard_normal(out[name].shape)
        drawn = base * np.exp(spread * noise) if base else spread * noise
        out[name] = jnp.asarray(drawn.astype(out[name].dtype))
    for name, factor in factors.items():
        out[name] = (out[name] * factor).astype(out[name].dtype)
    return out
```

```python
from contextlib import ExitStack

import concourse.bass as bass
from concourse import mybir

LAYERS = (0, 1, 2, 3, 4, 5, 6, 7, 8, 9, 10, 11)

F32 = mybir.dt.float32
U32 = mybir.dt.uint32
ALU = mybir.AluOpType
ACT = mybir.ActivationFunctionType
AX_X = mybir.AxisListType.X

P = 128
BATCH, SEQ, DIM = 16, 64, 256
TOKENS = BATCH * SEQ
TILES = TOKENS // P
HALVES = TOKENS // 512
DC = DIM // P
KEYS, CDIM = 1601, 128
KT = -(-KEYS // P)
KLAST = KEYS - (KT - 1) * P
EXPERTS = 8
EPS = 1e-5
BANKS = 8
LAM_INIT = 0.8 - 0.6 * 2.718281828459045 ** (-0.3 * 12)


class Count:

    def __init__(self, sem):
        self.sem = sem
        self.past = 0

    def at(self, n):
        return n + self.past

    def passed(self, n):
        self.past += n


class Core:

    def __init__(self, nc, dram, hold):
        self.nc, self.dram, self.hold = nc, dram, hold
        self.known = {}
        self.serial = 0
        self.PS = hold.enter_context(nc.psum_tensor("PS", [P, BANKS, 512], F32))
        self.X = self.sb(hold, "residual", [P, TILES, DIM])
        self.ident = self.sb(hold, "ident", [P, P])
        self.ones_row = self.sb(hold, "ones_row", [1, P])

    def sb(self, own, name, shape, dtype=F32):
        self.serial += 1
        return own.enter_context(self.nc.sbuf_tensor(f"{name}_{self.serial}", shape, dtype))

    def semaphores(self, name, n):
        return [self.semaphore(f"{name}_{u}") for u in range(n)]

    def semaphore(self, name):
        if name not in self.known:
            self.known[name] = Count(self.hold.enter_context(self.nc.semaphore(name)))
        return self.known[name]


def fetch(core, pairs):
    nc, landed = core.nc, core.semaphore("weights_landed")
    with nc.Block() as block:
        @block.sync
        def _(sp):
            for dst, src in pairs:
                sp.dma_start(dst, src).then_inc(landed.sem, 16)
    landed.passed(16 * len(pairs))


def weights(core, own, **shapes):
    room, pairs = {}, []
    for name, shape in shapes.items():
        t = core.sb(own, name, shape)
        src = core.dram[name]
        if src.shape[0] == 1 and shape[0] > 1:
            src = src[0].partition_broadcast(shape[0])
        room[name] = t
        pairs.append((t[:], src))
    fetch(core, pairs)
    return room


def wait_weights(core, eng):
    landed = core.semaphore("weights_landed")
    eng.wait_ge(landed.sem, landed.past)


def normalize(core, src, dst, gain=None, shift=None):
    nc = core.nc
    step, var_ready, dev_ready = core.semaphore("norm_step"), core.semaphore("variance_ready"), core.semaphore("deviation_ready")
    with ExitStack() as own:
        stats = core.sb(own, "stats", [P, TILES, 6])
        moments = core.sb(own, "moments", [P, TILES, 2])
        dev = core.sb(own, "deviation", [P, TILES])
        rstd = core.sb(own, "rstd", [P, TILES])
        with nc.Block() as block:
            @block.vector
            def _(dve):
                for t in range(TILES):
                    nc.vector.bn_stats(stats[:, t, :], src[:, t, :]).then_inc(step.sem, 1)
                dve.wait_ge(step.sem, step.at(TILES))
                for t in range(TILES):
                    nc.vector.bn_aggr(moments[:, t, :], stats[:, t, :]).then_inc(step.sem, 1)
                dve.wait_ge(step.sem, step.at(2 * TILES))
                nc.vector.tensor_scalar(dev[:], moments[:, :, 1], EPS, None, ALU.add).then_inc(var_ready.sem, 1)
                dve.wait_ge(dev_ready.sem, dev_ready.at(1))
                nc.vector.reciprocal(rstd[:], dev[:]).then_inc(step.sem, 1)
                dve.wait_ge(step.sem, step.at(2 * TILES + 1))
                for t in range(TILES):
                    nc.vector.tensor_scalar(dst[:, t, :], src[:, t, :], moments[:, t, 0:1], rstd[:, t:t + 1],
                                            ALU.subtract, ALU.mult).then_inc(step.sem, 1)
                if gain is not None:
                    wait_weights(core, dve)
                    dve.wait_ge(step.sem, step.at(3 * TILES + 1))
                    nc.vector.tensor_tensor(dst[:], dst[:], gain[:].unsqueeze(1).broadcast_to([P, TILES, DIM]),
                                            ALU.mult).then_inc(step.sem, 1)
                    dve.wait_ge(step.sem, step.at(3 * TILES + 2))
                    nc.vector.tensor_tensor(dst[:], dst[:], shift[:].unsqueeze(1).broadcast_to([P, TILES, DIM]),
                                            ALU.add).then_inc(step.sem, 1)

            @block.scalar
            def _(act):
                act.wait_ge(var_ready.sem, var_ready.at(1))
                nc.scalar.activation(dev[:], dev[:], ACT.Sqrt).then_inc(dev_ready.sem, 1)
    step.passed(3 * TILES + 1 + (2 if gain is not None else 0))
    var_ready.passed(1)
    dev_ready.passed(1)


def evacuate(core, block, fills, ready, by_act, by_dve, act_op, dve_op):
    @block.scalar
    def _(act):
        wait_weights(core, act)
        for f in range(0, fills, 2):
            act.wait_ge(ready.sem, ready.at(f + 1))
            act_op(f).then_inc(by_act.sem, 1)

    @block.vector
    def _(dve):
        wait_weights(core, dve)
        for f in range(1, fills, 2):
            dve.wait_ge(ready.sem, ready.at(f + 1))
            dve_op(f).then_inc(by_dve.sem, 1)


def wait_bank(pe, f, by_act, by_dve):
    if f >= BANKS:
        by = by_act if f % 2 == 0 else by_dve
        pe.wait_ge(by.sem, by.at((f - BANKS) // 2 + 1))


def turn(core, src, chunks, dst, gain=None, shift=None):
    nc, PS = core.nc, core.PS
    ready, by_act, by_dve = core.semaphore("fill_ready"), core.semaphore("fill_taken_act"), core.semaphore("fill_taken_dve")
    fills = chunks * HALVES

    def place(f):
        c, half = f // HALVES, f % HALVES
        return c, dst[:, c, half * 512:(half + 1) * 512], PS[:, f % BANKS, :]

    def act_op(f):
        c, out, bank = place(f)
        return nc.scalar.activation(out, bank, ACT.Identity,
                                    bias=0.0 if shift is None else shift[:, c:c + 1],
                                    scale=1.0 if gain is None else gain[:, c:c + 1])

    def dve_op(f):
        c, out, bank = place(f)
        if gain is None and shift is None:
            return nc.vector.tensor_copy(out, bank)
        return nc.vector.tensor_scalar(out, bank, 1.0 if gain is None else gain[:, c:c + 1],
                                       0.0 if shift is None else shift[:, c:c + 1], ALU.mult, ALU.add)

    with nc.Block() as block:
        @block.tensor
        def _(pe):
            for f in range(fills):
                c, half = f // HALVES, f % HALVES
                wait_bank(pe, f, by_act, by_dve)
                for j in range(4):
                    last = nc.tensor.transpose(PS[:, f % BANKS, j * P:(j + 1) * P],
                                               src[:, half * 4 + j, c * P:(c + 1) * P], core.ident[:])
                last.then_inc(ready.sem, 1)

        evacuate(core, block, fills, ready, by_act, by_dve, act_op, dve_op)
    ready.passed(fills)
    by_act.passed((fills + 1) // 2)
    by_dve.passed(fills // 2)


def linear_turned(core, src, w, dst, bias=None, func=ACT.Identity, rows=P):
    nc, PS = core.nc, core.PS
    ready, by_act, by_dve = core.semaphore("fill_ready"), core.semaphore("fill_taken_act"), core.semaphore("fill_taken_dve")
    kc = src.shape[1]
    fills = dst.shape[1] * HALVES
    plain = func == ACT.Identity

    def place(f):
        m, half = f // HALVES, f % HALVES
        return m, dst[0:rows, m, half * 512:(half + 1) * 512], PS[0:rows, f % BANKS, :]

    def act_op(f):
        m, out, bank = place(f)
        return nc.scalar.activation(out, bank, func, bias=0.0 if bias is None else bias[:, m:m + 1])

    def dve_op(f):
        m, out, bank = place(f)
        if bias is None:
            return nc.vector.tensor_copy(out, bank)
        return nc.vector.tensor_scalar(out, bank, bias[:, m:m + 1], None, ALU.add)

    with nc.Block() as block:
        @block.tensor
        def _(pe):
            wait_weights(core, pe)
            for f in range(fills):
                m, half = f // HALVES, f % HALVES
                if plain:
                    wait_bank(pe, f, by_act, by_dve)
                elif f >= BANKS:
                    pe.wait_ge(by_act.sem, by_act.at(f - BANKS + 1))
                for c in range(kc):
                    last = nc.tensor.matmul(PS[0:rows, f % BANKS, :], w[:, c, m * P:m * P + rows],
                                            src[:, c, half * 512:(half + 1) * 512],
                                            start=(c == 0), stop=(c == kc - 1))
                last.then_inc(ready.sem, 1)

        if plain:
            evacuate(core, block, fills, ready, by_act, by_dve, act_op, dve_op)
        else:
            @block.scalar
            def _(act):
                wait_weights(core, act)
                for f in range(fills):
                    act.wait_ge(ready.sem, ready.at(f + 1))
                    act_op(f).then_inc(by_act.sem, 1)
    ready.passed(fills)
    if plain:
        by_act.passed((fills + 1) // 2)
        by_dve.passed(fills // 2)
    else:
        by_act.passed(fills)


def linear_rows(core, src, w, dst, bias=None, base=None):
    nc, PS = core.nc, core.PS
    ready, taken = core.semaphore("rows_ready"), core.semaphore("rows_taken")
    kc, n_all = src.shape[1], dst.shape[2]
    cuts = [(n, min(512, n_all - n)) for n in range(0, n_all, 512)]
    fills = [(t, n, k) for t in range(TILES) for n, k in cuts]
    with nc.Block() as block:
        @block.tensor
        def _(pe):
            wait_weights(core, pe)
            for f, (t, n, k) in enumerate(fills):
                if f >= BANKS:
                    pe.wait_ge(taken.sem, taken.at(f - BANKS + 1))
                out = PS[:, f % BANKS, 0:k]
                if bias is not None:
                    nc.tensor.matmul(out, core.ones_row[0:1, :], bias[0:1, n:n + k], start=True, stop=False)
                for c in range(kc):
                    last = nc.tensor.matmul(out, src[:, c, t * P:(t + 1) * P], w[:, c, n:n + k],
                                            start=(c == 0 and bias is None), stop=(c == kc - 1))
                last.then_inc(ready.sem, 1)

        @block.vector
        def _(dve):
            for f, (t, n, k) in enumerate(fills):
                dve.wait_ge(ready.sem, ready.at(f + 1))
                if base is None:
                    ins = nc.vector.tensor_copy(dst[:, t, n:n + k], PS[:, f % BANKS, 0:k])
                else:
                    ins = nc.vector.tensor_tensor(dst[:, t, n:n + k], PS[:, f % BANKS, 0:k], base[:, t, n:n + k],
                                                  ALU.add)
                ins.then_inc(taken.sem, 1)
    ready.passed(len(fills))
    taken.passed(len(fills))


def vector_steps(core, steps):
    nc, step = core.nc, core.semaphore("vector_step")
    with nc.Block() as block:
        @block.vector
        def _(dve):
            wait_weights(core, dve)
            for n, run in enumerate(steps):
                if n:
                    dve.wait_ge(step.sem, step.at(n))
                run().then_inc(step.sem, 1)
    step.passed(len(steps))


def add(core, dst, a, b):
    vector_steps(core, [lambda: core.nc.vector.tensor_tensor(dst[:], a[:], b[:], ALU.add)])


def self_attention(core, qT, kT, V, O, heads, d, dv, scale, mask=None, minus_lam=None):
    nc, PS = core.nc, core.PS
    qc = qT.shape[1]
    groups = P // d
    per = heads // groups
    diff = minus_lam is not None
    og = groups // 2 if diff else groups
    squares = og * per
    tfills = squares // 4
    staged = core.semaphores("tile_staged", 2)
    s_ready, shifted = core.semaphore("scores_ready"), core.semaphore("scores_shifted")
    exps, probs = core.semaphore("exps_ready"), core.semaphore("squares_ready")
    turned, t_act = core.semaphore("squares_turned"), core.semaphore("squares_taken_act")
    o_ready, o_taken, step = core.semaphore("out_ready"), core.semaphore("out_taken"), core.semaphore("softmax_step")
    begun = core.semaphore("scores_begun")
    steps = 4 + (1 if diff else 0) + (1 if mask is not None else 0)

    def head_of(pos):
        g, k = pos // per, pos % per
        return k * og + g

    with ExitStack() as own:
        qs = core.sb(own, "q_tile", [P, 2, qc, P])
        ks = core.sb(own, "k_tile", [P, 2, qc, P])
        vs = core.sb(own, "v_tile", [P, 2, V.shape[2]])
        E = core.sb(own, "exps", [P, groups, per, SEQ])
        squares_sb = core.sb(own, "squares", [P, og, per, P])
        turned_sb = core.sb(own, "squares_turned", [P, squares, P])
        top = core.sb(own, "row_max", [P, groups, per])
        total = core.sb(own, "row_sum", [P, groups, per])
        warm = core.sb(own, "warm", [1, 1])
        S = PS[:, 0:groups, 0:per * SEQ].rearrange("p g (k t) -> p g k t", t=SEQ)
        flat = squares_sb[:].rearrange("p g k s -> p (g k) s")
        O_ps = PS[:, 6:8, :].rearrange("p b n -> p (b n)")
        wide = squares * dv
        with nc.Block() as block:
            @block.sync
            def _(sp):
                with sp.Fori(0, TILES // 2) as it:
                    for u in range(2):
                        i = it * 2 + u
                        sp.wait_ge(o_ready.sem, o_ready.at(i + 1))
                        sp.dma_start(qs[:, u], qT[:, :, bass.ds(i * P, P)]).then_inc(staged[u].sem, 16)
                        sp.dma_start(ks[:, u], kT[:, :, bass.ds(i * P, P)]).then_inc(staged[u].sem, 16)
                        sp.dma_start(vs[:, u], V[:, bass.ds(i, 1), :].rearrange("p a n -> p (a n)")).then_inc(staged[u].sem, 16)

            @block.tensor
            def _(pe):
                pe.sem_inc(o_ready.sem, 2)
                with pe.Fori(0, TILES // 2) as it:
                    for u in range(2):
                        i = it * 2 + u
                        pe.wait_ge(staged[u].sem, staged[u].at(it * 48 + 48))
                        pe.wait_ge(shifted.sem, shifted.at(i + 1))
                        if d == 64:
                            pe.sem_inc(begun.sem, 1)
                        for h in range(heads):
                            g, k = h % groups, h // groups
                            for b in range(2):
                                last = nc.tensor.matmul(PS[b * SEQ:(b + 1) * SEQ, g, k * SEQ:(k + 1) * SEQ],
                                                        qs[g * d:(g + 1) * d, u, k, b * SEQ:(b + 1) * SEQ],
                                                        ks[g * d:(g + 1) * d, u, k, b * SEQ:(b + 1) * SEQ],
                                                        start=True, stop=True)
                        last.then_inc(s_ready.sem, 1)
                        pe.wait_ge(probs.sem, probs.at(i * 2 + 2))
                        for j in range(tfills):
                            pe.wait_ge(t_act.sem, t_act.at(i * tfills + j + 1))
                            for m in range(4):
                                last = nc.tensor.transpose(PS[:, 4 + j % 2, m * P:(m + 1) * P], flat[:, 4 * j + m, :],
                                                           core.ident[:])
                            last.then_inc(turned.sem, 1)
                        pe.wait_ge(t_act.sem, t_act.at(i * tfills + tfills + 2))
                        pe.wait_ge(o_taken.sem, o_taken.at(i + 1))
                        for pos in range(squares):
                            h = head_of(pos)
                            last = nc.tensor.matmul(O_ps[:, h * dv:(h + 1) * dv], turned_sb[:, pos, :],
                                                    vs[:, u, h * dv:(h + 1) * dv], start=True, stop=True)
                        last.then_inc(o_ready.sem, 1)

            @block.vector
            def _(dve):
                nc.vector.memset(squares_sb[:], 0.0).then_inc(step.sem, 1)
                dve.wait_ge(step.sem, step.at(1))
                dve.sem_inc(shifted.sem, 1)
                dve.sem_inc(o_taken.sem, 1)
                with dve.Fori(0, TILES) as i:
                    done = [0]

                    def then(ins):
                        done[0] += 1
                        ins.then_inc(step.sem, 1)
                        dve.wait_ge(step.sem, step.at(i * steps + 1 + done[0]))

                    dve.wait_ge(s_ready.sem, s_ready.at(i + 1))
                    then(nc.vector.tensor_reduce(top[:], S, AX_X, ALU.max))
                    nc.vector.tensor_tensor(E[:], S, top[:].unsqueeze(3).broadcast_to([P, groups, per, SEQ]),
                                            ALU.subtract).then_inc(shifted.sem, 1)
                    dve.wait_ge(exps.sem, exps.at(i + 1))
                    then(nc.vector.tensor_reduce(total[:], E[:], AX_X, ALU.add))
                    then(nc.vector.reciprocal(total[:], total[:]))
                    if diff:
                        odd = total[:, 1::2, :]
                        then(nc.vector.tensor_scalar(odd, odd, minus_lam, None, ALU.mult))
                    then(nc.vector.tensor_tensor(E[:], E[:], total[:].unsqueeze(3).broadcast_to([P, groups, per, SEQ]),
                                                 ALU.mult))
                    if mask is not None:
                        Ef = E[:].rearrange("p g k t -> p (g k) t")
                        then(nc.vector.tensor_tensor(Ef, Ef, mask[:].unsqueeze(1).broadcast_to([P, heads, SEQ]), ALU.mult))
                    for b in range(2):
                        rows = slice(b * SEQ, (b + 1) * SEQ)
                        out = squares_sb[rows, :, :, b * SEQ:(b + 1) * SEQ]
                        if diff:
                            ins = nc.vector.tensor_tensor(out, E[rows, 0::2], E[rows, 1::2], ALU.add)
                        else:
                            ins = nc.vector.tensor_copy(out, E[rows])
                        ins.then_inc(probs.sem, 1)
                    dve.wait_ge(o_ready.sem, o_ready.at(i + 3))
                    nc.vector.tensor_copy(O[:, bass.ds(i, 1), :].rearrange("p a n -> p (a n)"),
                                          O_ps[:, 0:wide]).then_inc(o_taken.sem, 1)

            @block.scalar
            def _(act):
                nc.scalar.activation(warm[:], core.ident[0:1, 0:1], ACT.Exp)
                act.sem_inc(t_act.sem, 2)
                with act.Fori(0, TILES) as i:
                    act.wait_ge(shifted.sem, shifted.at(i + 2))
                    nc.scalar.activation(E[:], E[:], ACT.Exp, scale=scale).then_inc(exps.sem, 1)
                    for j in range(tfills):
                        act.wait_ge(turned.sem, turned.at(i * tfills + j + 1))
                        nc.scalar.copy(turned_sb[:, 4 * j:4 * j + 4, :].rearrange("p m s -> p (m s)"),
                                       PS[:, 4 + j % 2, :]).then_inc(t_act.sem, 1)
    for s in staged:
        s.passed(48 * TILES // 2)
    for s in (s_ready, exps):
        s.passed(TILES)
    o_ready.passed(TILES + 2)
    shifted.passed(TILES + 1)
    o_taken.passed(TILES + 1)
    probs.passed(2 * TILES)
    if d == 64:
        begun.passed(TILES)
    turned.passed(tfills * TILES)
    t_act.passed(tfills * TILES + 2)
    step.passed(steps * TILES + 1)


def store(core, pairs):
    nc, stored = core.nc, core.semaphore("stored")
    with nc.Block() as block:
        @block.sync
        def _(sp):
            for dst, src in pairs:
                sp.dma_start(dst, src).then_inc(stored.sem, 16)
            sp.wait_ge(stored.sem, stored.at(16 * len(pairs)))
    stored.passed(16 * len(pairs))


def context_queries(core, qT, wkT, heads, d, gain, name):
    nc, PS = core.nc, core.PS
    ready, by_act, by_dve, stored = (core.semaphore("fill_ready"), core.semaphore("fill_taken_act"),
                                     core.semaphore("fill_taken_dve"), core.semaphore("stored"))
    out = core.dram[name]
    fills = heads * HALVES
    per_chunk = P // d if d <= P else 1
    kc = max(1, d // P)
    with ExitStack() as own:
        room = core.sb(own, "context_q", [P, heads, TOKENS])

        def place(f):
            h, half = f // HALVES, f % HALVES
            return room[:, h, half * 512:(half + 1) * 512], PS[:, f % BANKS, :]

        def act_op(f):
            o, bank = place(f)
            return nc.scalar.activation(o, bank, ACT.Identity, scale=1.0 if gain is None else gain[:, 0:1])

        def dve_op(f):
            o, bank = place(f)
            if gain is None:
                return nc.vector.tensor_copy(o, bank)
            return nc.vector.tensor_scalar(o, bank, gain[:, 0:1], None, ALU.mult)

        with nc.Block() as block:
            @block.tensor
            def _(pe):
                wait_weights(core, pe)
                for f in range(fills):
                    h, half = f // HALVES, f % HALVES
                    wait_bank(pe, f, by_act, by_dve)
                    for c in range(kc):
                        rows = slice((h % per_chunk) * d, (h % per_chunk) * d + d) if d < P else slice(0, P)
                        chunk = h // per_chunk if d < P else c
                        last = nc.tensor.matmul(PS[:, f % BANKS, :], wkT[rows, chunk, :],
                                                qT[rows, chunk, half * 512:(half + 1) * 512],
                                                start=(c == 0), stop=(c == kc - 1))
                    last.then_inc(ready.sem, 1)

            evacuate(core, block, fills, ready, by_act, by_dve, act_op, dve_op)

            @block.sync
            def _(sp):
                for h in range(heads):
                    sp.wait_ge(by_act.sem, by_act.at(h + 1))
                    sp.wait_ge(by_dve.sem, by_dve.at(h + 1))
                    sp.dma_start(out[:, :, h * SEQ:(h + 1) * SEQ].rearrange("b c s -> c b s"),
                                 room[:, h, :].rearrange("c (b s) -> c b s", s=SEQ)).then_inc(stored.sem, 16)
                sp.wait_ge(stored.sem, stored.at(16 * heads))
    ready.passed(fills)
    by_act.passed(fills // 2)
    by_dve.passed(fills // 2)
    stored.passed(16 * heads)


def context_attention(core, name_q, context, wv_of, sums, pairs, rows, per_group, unroll, scale, d_out):
    nc, PS = core.nc, core.PS
    y_landed, q_landed = core.semaphores("context_landed", unroll), core.semaphores("queries_landed", unroll)
    s_ready, m_ready, e_done = core.semaphore("scores_ready"), core.semaphore("max_ready"), core.semaphore("exps_ready")
    turned, t_act, t_dve = core.semaphore("squares_turned"), core.semaphore("squares_taken_act"), core.semaphore("squares_taken_dve")
    o_ready, o_taken = core.semaphore("weighted_ready"), core.semaphore("weighted_taken")
    f_ready, f_taken, step = core.semaphore("out_ready"), core.semaphore("out_taken"), core.semaphore("softmax_step")
    turns = BATCH // unroll
    steps_all = BATCH * pairs
    groups_all = steps_all // per_group
    per_turn = unroll * pairs
    wide = per_group * rows
    heads_in = rows // SEQ
    parts = [list(range(KT))[KT * n // per_group:KT * (n + 1) // per_group] for n in range(per_group)]
    S = PS[0:rows, 0:4, :].rearrange("p b n -> p (b n)")[:, 0:KEYS]
    O_ps = PS[:, 6, 0:wide]
    F_ps = PS[0:rows, 7, 0:per_group * heads_in * d_out].rearrange("p (g a d) -> p g a d", g=per_group, a=heads_in)

    def keys_in(k):
        return KLAST if k == KT - 1 else P

    with ExitStack() as own:
        y = core.sb(own, "context_rows", [P, unroll, KT, CDIM])
        yT = core.sb(own, "context_turned", [P, 2, KEYS])
        qs = core.sb(own, "queries", [P, unroll, pairs * rows])
        probs = core.sb(own, "probs", [P, 2, KEYS])
        probsT = core.sb(own, "probs_turned", [P, 2, KT, wide])
        OT = core.sb(own, "weighted", [P, 2, wide])
        top = core.sb(own, "row_max", [rows, 2])
        bias = core.sb(own, "minus_max", [rows, 2])
        total = core.sb(own, "row_sum", [rows, per_turn])
        warm = core.sb(own, "warm", [1, 1])
        inverse = core.sb(own, "row_scale", [rows, 2, per_group])

        def load(sp, b, u):
            sp.dma_start(y[:, u, 0:KT - 1, :], context[bass.ds(b, 1), 0:(KT - 1) * P, :].rearrange(
                "a (k p) c -> p (a k) c", p=P)).then_inc(y_landed[u].sem, 16)
            sp.dma_start(y[0:KLAST, u, KT - 1, :], context[bass.ds(b, 1), (KT - 1) * P:KEYS, :].rearrange(
                "a p c -> p (a c)")).then_inc(y_landed[u].sem, 16)
            sp.dma_start(qs[:, u, :], core.dram[name_q][bass.ds(b, 1), :, :].rearrange("a c n -> c (a n)")).then_inc(
                q_landed[u].sem, 16)

        def where(it, local):
            return it * per_turn + local, it * unroll + local // pairs, local % pairs

        def set_of(it, local):
            return it * per_turn + local + it * unroll + min(local, per_turn - 1) // pairs

        def fill_waits(pe, j, s):
            if j < 2:
                pe.wait_ge(t_dve.sem, t_dve.at(s * 2 + j + 1))
            else:
                pe.wait_ge(t_act.sem, t_act.at(s * 2 + j - 1))

        def pe_context(pe, it, local):
            n, b, _ = where(it, local)
            u = (local // pairs) % unroll
            s = n - 1 + b if not (isinstance(n, int) and n == 0) else 0
            pe.wait_ge(y_landed[u].sem, y_landed[u].at(it * 32 + 32))
            for j in range(4):
                fill_waits(pe, j, s)
                for k in range(4 * j, min(4 * j + 4, KT)):
                    kk = keys_in(k)
                    last = nc.tensor.transpose(PS[:, 4 + j % 2, (k - 4 * j) * P:(k - 4 * j) * P + kk],
                                               y[0:kk, u, k, :], core.ident[0:kk, 0:kk])
                last.then_inc(turned.sem, 1)
            pe.wait_ge(q_landed[u].sem, q_landed[u].at(it * 16 + 16))
            pe.wait_ge(t_act.sem, t_act.at(s * 2 + 2))

        def pe_context_whole(pe, it, local):
            n, b, _ = where(it, local)
            s = n - 1 + b if not (isinstance(n, int) and n == 0) else 0
            pe.wait_ge(t_dve.sem, t_dve.at(s * 2 + 4))

        def pe_scores(pe, it, local, first):
            n, b, p = where(it, local)
            u = (local // pairs) % unroll
            if not first:
                pe.wait_ge(e_done.sem, e_done.at(n))
            for j in range(4):
                cols = min(512, KEYS - 512 * j)
                last = nc.tensor.matmul(S[:, 512 * j:512 * j + cols], qs[:, u, p * rows:(p + 1) * rows],
                                        yT[:, (local // pairs) % 2, 512 * j:512 * j + cols], start=True, stop=True)
            last.then_inc(s_ready.sem, 1)

        def pe_turn(pe, it, local, js):
            n, s = it * per_turn + local, set_of(it, local)
            if 0 in js:
                pe.wait_ge(e_done.sem, e_done.at(n))
            for j in js:
                fill_waits(pe, j, s)
                for k in range(4 * j, min(4 * j + 4, KT)):
                    kk = keys_in(k)
                    last = nc.tensor.transpose(PS[0:kk, 4 + j % 2, (k - 4 * j) * P:(k - 4 * j + 1) * P],
                                               probs[:, (local - 1) % 2, k * P:k * P + kk], core.ident[:])
                last.then_inc(turned.sem, 1)

        def pe_weighted(pe, it, local):
            n, _, _ = where(it, local)
            part = (local - 1) % per_group
            back = local - 1 - part - per_group
            u = (back // pairs) % unroll
            par = (back // per_group) % 2
            if part == 0:
                s = set_of(it, local - 1)
                pe.wait_ge(t_act.sem, t_act.at(s * 2 + 2))
                pe.wait_ge(t_dve.sem, t_dve.at(s * 2 + 4))
                pe.wait_ge(o_taken.sem, o_taken.at(it * (per_turn // per_group) + back // per_group + 1))
            for k in parts[part]:
                kk = keys_in(k)
                last = nc.tensor.matmul(O_ps, y[0:kk, u, k, :], probsT[0:kk, par, k, :], start=(k == 0),
                                        stop=(k == KT - 1))
            if part == per_group - 1:
                last.then_inc(o_ready.sem, 1)

        def pe_out(pe, it, local):
            back = local - 1 - 2 * per_group
            g = it * (per_turn // per_group) + back // per_group
            par = (back // per_group) % 2
            pe.wait_ge(o_taken.sem, o_taken.at(g + 2))
            pe.wait_ge(f_taken.sem, f_taken.at(g * heads_in + heads_in))
            for m in range(per_group):
                pair = (back + m) % pairs
                last = nc.tensor.matmul(F_ps[:, m], OT[:, par, m * rows:(m + 1) * rows], wv_of(pair), start=True, stop=True)
            last.then_inc(f_ready.sem, 1)

        def act_step(act, it, local, first, tail=False):
            n, b, p = where(it, local)
            if p == 0 and not tail:
                s = 0 if first else n - 1 + b
                for j in range(2):
                    act.wait_ge(turned.sem, turned.at(s * 4 + j + 1))
                    nc.scalar.copy(yT[:, (local // pairs) % 2, 512 * j:512 * j + 512], PS[:, 4 + j, :]).then_inc(t_act.sem, 1)
            return n, b, p

        def act_turn(act, it, local):
            s = set_of(it, local)
            gl = (local - 1) // per_group
            m = (local - 1) % per_group
            for j in range(2):
                act.wait_ge(turned.sem, turned.at(s * 4 + j + 1))
                nc.scalar.copy(probsT[:, gl % 2, 4 * j:4 * j + 4, m * rows:(m + 1) * rows],
                               PS[:, 4 + j, :].rearrange("p (k r) -> p k r", r=P)[:, :, 0:rows]).then_inc(t_act.sem, 1)

        def act_exp(act, it, local):
            n, _, _ = where(it, local)
            act.wait_ge(m_ready.sem, m_ready.at(n + 1))
            nc.scalar.activation(probs[0:rows, local % 2, :], S, ACT.Exp, bias=bias[:, local % 2:local % 2 + 1], scale=scale,
                                 accum_out=total[:, local % per_turn:local % per_turn + 1]).then_inc(e_done.sem, 1)

        def act_weighted(act, it, local):
            back = local - 2 * per_group
            g = it * (per_turn // per_group) + back // per_group
            act.wait_ge(o_ready.sem, o_ready.at(g + 1))
            nc.scalar.copy(OT[:, (back // per_group) % 2, :], O_ps).then_inc(o_taken.sem, 1)

        def dve_context(dve, it, local):
            n, b, _ = where(it, local)
            s = n - 1 + b if not (isinstance(n, int) and n == 0) else 0
            for j in (2, 3):
                cols = min(512, KEYS - 512 * j)
                dve.wait_ge(turned.sem, turned.at(s * 4 + j + 1))
                nc.vector.tensor_copy(yT[:, (local // pairs) % 2, 512 * j:512 * j + cols],
                                      PS[:, 2 + j, 0:cols]).then_inc(t_dve.sem, 1)

        def dve_turn(dve, it, local):
            s = set_of(it, local)
            gl = (local - 1) // per_group
            m = (local - 1) % per_group
            for j in (2, 3):
                k0, k1 = 4 * j, min(4 * j + 4, KT)
                kk = P if j == 2 else KLAST
                dve.wait_ge(turned.sem, turned.at(s * 4 + j + 1))
                nc.vector.tensor_copy(probsT[0:kk, gl % 2, k0:k1, m * rows:(m + 1) * rows],
                                      PS[0:kk, 2 + j, 0:(k1 - k0) * P].rearrange("p (k r) -> p k r", r=P)[:, :, 0:rows]).then_inc(
                                          t_dve.sem, 1)

        def dve_max(dve, it, local):
            n, _, _ = where(it, local)
            q = local % 2
            dve.wait_ge(s_ready.sem, s_ready.at(n + 1))
            nc.vector.tensor_reduce(top[:, q:q + 1], S, AX_X, ALU.max).then_inc(step.sem, 1)
            g_done = n + 1
            dve.wait_ge(step.sem, step.at(g_done))
            nc.vector.tensor_scalar(bias[:, q:q + 1], top[:, q:q + 1], -scale, None, ALU.mult).then_inc(m_ready.sem, 1)

        inv_done = core.semaphore("row_scale_ready")

        def dve_out(dve, it, local):
            back = local - 1 - 2 * per_group
            g = it * (per_turn // per_group) + back // per_group
            pair0 = back % pairs
            b = it * unroll + back // pairs
            slot = back % per_turn
            inv = inverse[:, (back // per_group) % 2, :]
            nc.vector.reciprocal(inv, total[:, slot:slot + per_group]).then_inc(inv_done.sem, 1)
            dve.wait_ge(inv_done.sem, inv_done.at(g + 1))
            dve.wait_ge(f_ready.sem, f_ready.at(g + 1))
            for a in range(heads_in):
                r = slice(a * SEQ, (a + 1) * SEQ)
                nc.vector.tensor_tensor(sums[r, bass.ds(b, 1), pair0:pair0 + per_group, :].rearrange("p x g d -> p (x g) d"),
                                        F_ps[r, :, a, :],
                                        inv[r, :].unsqueeze(2).broadcast_to([SEQ, per_group, d_out]),
                                        ALU.mult).then_inc(f_taken.sem, 1)

        def pe_step(pe, it, local, first, tail):
            p = local % pairs
            live = lambda back: not first or local >= back
            if not tail and p == 0:
                pe_context(pe, it, local)
            if not tail and p:
                pe_scores(pe, it, local, first and local == 0)
            if live(1) and not (tail and local > per_turn_end):
                pe_turn(pe, it, local, (0, 1))
            if (local - 1) % per_group == 0 and live(2 * per_group + 1):
                pe_out(pe, it, local)
            if live(per_group + 1) and not (tail and local > per_turn_end + per_group):
                pe_weighted(pe, it, local)
            if live(1) and not (tail and local > per_turn_end):
                pe_turn(pe, it, local, (2, 3))
            if not tail and p == 0:
                pe_context_whole(pe, it, local)
                pe_scores(pe, it, local, first and local == 0)

        def act_all(act, it, local, first, tail):
            p = local % pairs
            live = lambda back: not first or local >= back
            if not tail and p == 0:
                act_step(act, it, local, first and local == 0)
            if live(1) and not (tail and local > per_turn_end):
                act_turn(act, it, local)
            if not tail:
                act_exp(act, it, local)
            if local % per_group == 0 and live(2 * per_group) and not (tail and local > per_turn_end + per_group):
                act_weighted(act, it, local)

        def dve_all(dve, it, local, first, tail):
            p = local % pairs
            live = lambda back: not first or local >= back
            if not tail and p == 0:
                dve_context(dve, it, local)
            if not tail and p:
                dve_max(dve, it, local)
            if live(1) and not (tail and local > per_turn_end):
                dve_turn(dve, it, local)
            if not tail and p == 0:
                dve_max(dve, it, local)
            if (local - 1) % per_group == 0 and live(2 * per_group + 1):
                dve_out(dve, it, local)

        per_turn_end = per_turn

        def run(eng, one):
            for local in range(per_turn):
                one(eng, 0, local, True, False)
            with eng.Fori(1, turns) as it:
                for local in range(per_turn):
                    one(eng, it, local, False, False)
            for local in range(per_turn, per_turn + 2 * per_group + 2):
                if local - 1 - 2 * per_group < per_turn:
                    one(eng, turns - 1, local, False, True)

        with nc.Block() as block:
            @block.sync
            def _(sp):
                for u in range(unroll):
                    load(sp, u, u)
                with sp.Fori(1, turns) as it:
                    for u in range(unroll):
                        sp.wait_ge(o_ready.sem, o_ready.at(((it - 1) * unroll + u + 1) * (pairs // per_group)))
                        load(sp, it * unroll + u, u)

            @block.tensor
            def _(pe):
                wait_weights(core, pe)
                run(pe, pe_step)

            @block.scalar
            def _(act):
                act.sem_inc(o_taken.sem, 1)
                nc.scalar.activation(warm[:], core.ident[0:1, 0:1], ACT.Exp)
                run(act, act_all)

            @block.vector
            def _(dve):
                if rows < P:
                    nc.vector.memset(probs[rows:P], 0.0)
                dve.sem_inc(t_dve.sem, 2)
                dve.sem_inc(f_taken.sem, heads_in)
                run(dve, dve_all)
    for u in range(unroll):
        y_landed[u].passed(32 * turns)
        q_landed[u].passed(16 * turns)
    for s in (s_ready, m_ready, e_done, step):
        s.passed(steps_all)
    turned.passed(4 * (steps_all + BATCH))
    t_act.passed(2 * (steps_all + BATCH))
    t_dve.passed(2 * (steps_all + BATCH) + 2)
    o_ready.passed(groups_all)
    o_taken.passed(groups_all + 1)
    f_ready.passed(groups_all)
    f_taken.passed(groups_all * heads_in + heads_in)
    inv_done.passed(groups_all)


def turn_sums(core, sums, pairs, d, dst, shift):
    nc, PS = core.nc, core.PS
    ready, by_act, by_dve = core.semaphore("fill_ready"), core.semaphore("fill_taken_act"), core.semaphore("fill_taken_dve")
    chunks = pairs * d // P
    flat = sums[:].rearrange("p b h d -> p b (h d)")
    fills = chunks * (BATCH // 4)

    def place(f, half):
        c, b4 = f // (BATCH // 4), f % (BATCH // 4)
        k = half * chunks + c
        out = dst[:, k, b4 * 4 * SEQ:(b4 + 1) * 4 * SEQ].rearrange("p (b s) -> p b s", s=SEQ)
        bank = PS[:, f % BANKS, :].rearrange("p (b a s) -> p b a s", b=4, a=2)[:, :, half, :]
        return out, bank, shift[:, k:k + 1]

    with nc.Block() as block:
        @block.tensor
        def _(pe):
            for f in range(fills):
                c, b4 = f // (BATCH // 4), f % (BATCH // 4)
                if f >= BANKS:
                    by = by_act if f % 2 == 0 else by_dve
                    pe.wait_ge(by.sem, by.at(2 * ((f - BANKS) // 2 + 1)))
                for j in range(4):
                    last = nc.tensor.transpose(PS[:, f % BANKS, j * P:(j + 1) * P],
                                               flat[:, b4 * 4 + j, c * P:(c + 1) * P], core.ident[:])
                last.then_inc(ready.sem, 1)

        @block.scalar
        def _(act):
            wait_weights(core, act)
            for f in range(0, fills, 2):
                act.wait_ge(ready.sem, ready.at(f + 1))
                for half in range(2):
                    out, bank, bias = place(f, half)
                    nc.scalar.activation(out, bank, ACT.Identity, bias=bias).then_inc(by_act.sem, 1)

        @block.vector
        def _(dve):
            wait_weights(core, dve)
            for f in range(1, fills, 2):
                dve.wait_ge(ready.sem, ready.at(f + 1))
                for half in range(2):
                    out, bank, bias = place(f, half)
                    nc.vector.tensor_scalar(out, bank, bias, None, ALU.add).then_inc(by_dve.sem, 1)
    for s in (ready, by_act, by_dve):
        s.passed(fills)


def normalize_context(core):
    nc = core.nc
    src, dst = core.dram["ctx_512"], core.dram["context_norm"]
    landed, stored = core.semaphores("context_landed", 2), core.semaphores("context_stored", 2)
    m_step, p_step = core.semaphore("norm_step"), core.semaphore("pool_step")
    centred, squared, var_ready, dev_ready, scaled = (core.semaphore("centred"), core.semaphore("squared"), core.semaphore("variance_ready"),
                                                      core.semaphore("deviation_ready"), core.semaphore("context_scaled"))
    per = BATCH * KEYS // P
    left = BATCH * KEYS - per * P
    cut = 25
    cuts = per // cut
    flat_in = src.rearrange("b k c -> (b k) c")
    flat_out = dst.rearrange("b k c -> (b k) c")
    body_in = flat_in[0:per * P, :].rearrange("(p r) c -> p r c", p=P)
    body_out = flat_out[0:per * P, :].rearrange("(p r) c -> p r c", p=P)
    with ExitStack() as own:
        rows = core.sb(own, "rows", [P, 2, cut, CDIM])
        sq = core.sb(own, "squares", [P, 2, cut, CDIM])
        mean = core.sb(own, "mean", [P, 2, cut])
        var = core.sb(own, "variance", [P, 2, cut])

        def moves(n):
            if n < cuts:
                return body_in[:, n * cut:(n + 1) * cut, :], body_out[:, n * cut:(n + 1) * cut, :], P, cut
            return flat_in[per * P:, :].unsqueeze(1), flat_out[per * P:, :].unsqueeze(1), left, 1

        with nc.Block() as block:
            @block.sync
            def _(sp):
                for n in range(cuts + 1):
                    a, _, p, r = moves(n)
                    if n >= 2:
                        sp.wait_ge(stored[n % 2].sem, stored[n % 2].at(16 * (n // 2)))
                    sp.dma_start(rows[0:p, n % 2, 0:r, :], a).then_inc(landed[n % 2].sem, 16)
                    if n >= 1:
                        _, b, p, r = moves(n - 1)
                        sp.wait_ge(scaled.sem, scaled.at(n))
                        sp.dma_start(b, rows[0:p, (n - 1) % 2, 0:r, :]).then_inc(stored[(n - 1) % 2].sem, 16)
                _, b, p, r = moves(cuts)
                sp.wait_ge(scaled.sem, scaled.at(cuts + 1))
                sp.dma_start(b, rows[0:p, cuts % 2, 0:r, :]).then_inc(stored[cuts % 2].sem, 16)
                for q in range(2):
                    sp.wait_ge(stored[q].sem, stored[q].at(16 * ((cuts + 2 - q) // 2)))

            @block.vector
            def _(dve):
                for n in range(cuts + 1):
                    _, _, p, r = moves(n)
                    x, q = rows[0:p, n % 2, 0:r, :], n % 2
                    m, v = mean[0:p, q, 0:r], var[0:p, q, 0:r]
                    dve.wait_ge(landed[q].sem, landed[q].at(16 * (n // 2) + 16))
                    nc.vector.tensor_reduce(m, x, AX_X, ALU.add).then_inc(m_step.sem, 1)
                    dve.wait_ge(m_step.sem, m_step.at(3 * n + 1))
                    nc.vector.tensor_scalar(m, m, 1.0 / CDIM, None, ALU.mult).then_inc(m_step.sem, 1)
                    dve.wait_ge(m_step.sem, m_step.at(3 * n + 2))
                    nc.vector.tensor_tensor(x, x, m.unsqueeze(2).broadcast_to([p, r, CDIM]), ALU.subtract).then_inc(centred.sem, 1)
                    dve.wait_ge(squared.sem, squared.at(n + 1))
                    nc.vector.tensor_reduce(v, sq[0:p, q, 0:r, :], AX_X, ALU.add).then_inc(m_step.sem, 1)
                    dve.wait_ge(m_step.sem, m_step.at(3 * n + 3))
                    nc.vector.tensor_scalar(v, v, 1.0 / CDIM, EPS, ALU.mult, ALU.add).then_inc(var_ready.sem, 1)
                    dve.wait_ge(dev_ready.sem, dev_ready.at(n + 1))
                    nc.vector.reciprocal(v, v).then_inc(p_step.sem, 1)

            @block.scalar
            def _(act):
                for n in range(cuts + 1):
                    _, _, p, r = moves(n)
                    act.wait_ge(centred.sem, centred.at(n + 1))
                    nc.scalar.activation(sq[0:p, n % 2, 0:r, :], rows[0:p, n % 2, 0:r, :], ACT.Square).then_inc(squared.sem, 1)
                    act.wait_ge(var_ready.sem, var_ready.at(n + 1))
                    v = var[0:p, n % 2, 0:r]
                    nc.scalar.activation(v, v, ACT.Sqrt).then_inc(dev_ready.sem, 1)

            @block.gpsimd
            def _(pool):
                for n in range(cuts + 1):
                    _, _, p, r = moves(n)
                    x = rows[0:p, n % 2, 0:r, :]
                    pool.wait_ge(p_step.sem, p_step.at(n + 1))
                    nc.gpsimd.tensor_tensor(x, x, var[0:p, n % 2, 0:r].unsqueeze(2).broadcast_to([p, r, CDIM]),
                                            ALU.mult).then_inc(scaled.sem, 1)
    k = cuts + 1
    for q in range(2):
        landed[q].passed(16 * ((k + 1 - q) // 2))
        stored[q].passed(16 * ((k + 1 - q) // 2))
    m_step.passed(3 * k)
    for s in (p_step, centred, squared, var_ready, dev_ready, scaled):
        s.passed(k)


def mlp(core, own, rows, ln_g, ln_b, w2, b2, w3, b3):
    with ExitStack() as own:
        hat = core.sb(own, "hat", [P, TILES, DIM])
        hatT = core.sb(own, "hat_turned", [P, DC, TOKENS])
        inner = core.sb(own, "inner", [P, w3.shape[1], TOKENS])
        normalize(core, rows, hat)
        turn(core, hat, DC, hatT, ln_g, ln_b)
        linear_turned(core, hatT, w2, inner, b2, ACT.Gelu)
        linear_rows(core, inner, w3, rows, b3, rows)


def l0_xattn(core):
    X, nc = core.X, core.nc
    normalize_context(core)
    with ExitStack() as layer:
        U = core.sb(layer, "u", [P, TILES, DIM])
        R = core.sb(layer, "r", [P, TILES, DIM])
        ln = weights(core, layer, L0_xattn_ln1_g=[P, DIM], L0_xattn_ln1_b=[P, DIM], L0_xattn_ln2_g=[P, DIM],
                     L0_xattn_ln2_b=[P, DIM], causal=[P, SEQ])
        normalize(core, X, U)
        normalize(core, U, U, ln["L0_xattn_ln1_g"], ln["L0_xattn_ln1_b"])
        for a, heads, d in (("a1", 16, 32), ("a2", 16, 32)):
            inner = heads * d
            pre = f"L0_xattn_{a}_"
            with ExitStack() as own:
                cy = DIM if a == "a1" else CDIM
                shapes = {"wq": [P, DC, inner], "wv": [P, cy // P, inner], "li1_w": [P, inner // P, DIM], "li1_b": [1, DIM],
                          "lnx_g": [P, DC], "lnx_b": [P, DC], "lny_g": [P, cy // P], "lny_b": [P, cy // P],
                          "ln3_g": [P, DC], "ln3_b": [P, DC], "li2_w": [P, DC, 4 * DIM], "li2_b": [P, 4 * DC],
                          "li3_w": [P, 4 * DC, DIM], "li3_b": [1, DIM]}
                if a == "a1":
                    shapes["wk"] = [P, DC, inner]
                else:
                    shapes["wkT"] = [P, inner // P, CDIM]
                w = {k[len(pre):]: v for k, v in weights(core, own, **{pre + k: s for k, s in shapes.items()}).items()}
                if a == "a1":
                    with ExitStack() as work:
                        hat = core.sb(work, "hat", [P, TILES, DIM])
                        normT = core.sb(work, "norm_turned", [P, DC, TOKENS])
                        qT = core.sb(work, "qT", [P, inner // P, TOKENS])
                        kT = core.sb(work, "kT", [P, inner // P, TOKENS])
                        V = core.sb(work, "v", [P, TILES, inner])
                        O = core.sb(work, "o", [P, TILES, inner])
                        normalize(core, U, hat)
                        turn(core, hat, DC, normT, w["lnx_g"], w["lnx_b"])
                        linear_turned(core, normT, w["wq"], qT)
                        turn(core, hat, DC, normT, w["lny_g"], w["lny_b"])
                        linear_turned(core, normT, w["wk"], kT)
                        linear_rows(core, normT, w["wv"], V)
                        self_attention(core, qT, kT, V, O, heads, d, d, d ** -0.5, mask=ln["causal"])
                        turn(core, O, inner // P, qT)
                        linear_rows(core, qT, w["li1_w"], R, w["li1_b"], U)
                else:
                    with ExitStack() as work:
                        sums = core.sb(work, "sums", [P, BATCH, heads // 2, d])
                        vb = core.sb(work, "v_bias", [P, inner // P])
                        wv = core.sb(work, "wv_scaled", [P, inner])
                        with ExitStack() as front:
                            hat = core.sb(front, "hat", [P, TILES, DIM])
                            normT = core.sb(front, "norm_turned", [P, DC, TOKENS])
                            qT = core.sb(front, "qT", [P, inner // P, TOKENS])
                            normalize(core, U, hat)
                            turn(core, hat, DC, normT, w["lnx_g"], w["lnx_b"])
                            linear_turned(core, normT, w["wq"], qT)
                            context_queries(core, qT, w["wkT"], heads, d, w["lny_g"], "context_q16")
                        value_affine(core, w["wv"], w["lny_g"], w["lny_b"], wv, vb)
                        wv5 = wv[:].rearrange("c (a p d) -> c p a d", a=2, d=d)
                        context_attention(core, "context_q16", core.dram["context_norm"], lambda pair: wv5[:, pair],
                                          sums, heads // 2, P, 4, 2, d ** -0.5, d)
                        oT = core.sb(work, "oT", [P, inner // P, TOKENS])
                        turn_sums(core, sums, heads // 2, d, oT, vb)
                        linear_rows(core, oT, w["li1_w"], R, w["li1_b"], U)
                mlp(core, own, R, w["ln3_g"], w["ln3_b"], w["li2_w"], w["li2_b"], w["li3_w"], w["li3_b"])
                if a == "a1":
                    add(core, U, U, R)
                    normalize(core, U, U, ln["L0_xattn_ln2_g"], ln["L0_xattn_ln2_b"])
        vector_steps(core, [lambda: nc.vector.tensor_tensor(R[:], R[:], U[:], ALU.add),
                            lambda: nc.vector.tensor_tensor(X[:], X[:], R[:], ALU.add)])


def value_affine(core, wv, gain, shift, scaled, bias):
    nc, PS = core.nc, core.PS
    ready, step = core.semaphore("rows_ready"), core.semaphore("vector_step")
    chunks = bias.shape[1]
    with nc.Block() as block:
        @block.tensor
        def _(pe):
            wait_weights(core, pe)
            for k in range(chunks):
                last = nc.tensor.matmul(PS[:, k, 0:1], wv[:, 0, k * P:(k + 1) * P], shift[:, 0:1], start=True, stop=True)
            last.then_inc(ready.sem, 1)

        @block.vector
        def _(dve):
            wait_weights(core, dve)
            nc.vector.tensor_scalar(scaled[:], wv[:, 0, :], gain[:, 0:1], None, ALU.mult).then_inc(step.sem, 1)
            dve.wait_ge(ready.sem, ready.at(1))
            nc.vector.tensor_copy(bias[:], PS[:, 0:chunks, 0]).then_inc(step.sem, 1)
    ready.passed(1)
    step.passed(2)


def l0_attn(core):
    nc, X = core.nc, core.X
    heads, d, dv, pad = 8, 16, 32, 32
    with ExitStack() as own:
        w = weights(core, own, L0_attn_Wq=[P, DC, 2 * heads * pad], L0_attn_Wk=[P, DC, 2 * heads * pad],
                    L0_attn_Wv=[P, DC, DIM], L0_attn_Wo=[P, DC, DIM], L0_attn_lq1=[P, d], L0_attn_lk1=[P, d],
                    L0_attn_lq2=[P, d], L0_attn_lk2=[P, d], L0_attn_ln_g=[P, dv], L0_attn_ln_b=[P, dv])
        U = core.sb(own, "u", [P, TILES, DIM])
        uT = core.sb(own, "uT", [P, DC, TOKENS])
        qT = core.sb(own, "qT", [P, 4, TOKENS])
        kT = core.sb(own, "kT", [P, 4, TOKENS])
        V = core.sb(own, "v", [P, TILES, DIM])
        O = core.sb(own, "o", [P, TILES, DIM])
        lam = core.sb(own, "lam", [P, 4])
        normalize(core, X, U)
        turn(core, U, DC, uT)
        linear_turned(core, uT, w["L0_attn_Wq"], qT)
        linear_turned(core, uT, w["L0_attn_Wk"], kT)
        linear_rows(core, uT, w["L0_attn_Wv"], V)
        v = nc.vector
        vector_steps(core, [
            lambda: v.tensor_tensor(w["L0_attn_lq1"][:], w["L0_attn_lq1"][:], w["L0_attn_lk1"][:], ALU.mult),
            lambda: v.tensor_reduce(lam[:, 0:1], w["L0_attn_lq1"][:], AX_X, ALU.add),
            lambda: v.tensor_tensor(w["L0_attn_lq2"][:], w["L0_attn_lq2"][:], w["L0_attn_lk2"][:], ALU.mult),
            lambda: v.tensor_reduce(lam[:, 1:2], w["L0_attn_lq2"][:], AX_X, ALU.add)])
        scalar_step(core, lambda: nc.scalar.activation(lam[:, 0:2], lam[:, 0:2], ACT.Exp))
        vector_steps(core, [
            lambda: v.tensor_tensor(lam[:, 2:3], lam[:, 1:2], lam[:, 0:1], ALU.subtract),
            lambda: v.tensor_scalar(lam[:, 2:3], lam[:, 2:3], -LAM_INIT, None, ALU.add)])
        self_attention(core, qT, kT, V, O, 2 * heads, pad, dv, d ** -0.5, minus_lam=lam[:, 2:3])
        rows = TILES * heads
        O4 = O[:].rearrange("p t (h d) -> p (t h) d", d=dv)
        U4 = U[:].rearrange("p t (h d) -> p (t h) d", d=dv)
        mean = core.sb(own, "mean", [P, rows])
        var = core.sb(own, "variance", [P, rows])
        over = lambda a: a[:].unsqueeze(2).broadcast_to([P, rows, dv])
        along = lambda a: a[:].unsqueeze(1).broadcast_to([P, rows, dv])
        vector_steps(core, [
            lambda: v.tensor_reduce(mean[:], O4, AX_X, ALU.add),
            lambda: v.tensor_scalar(mean[:], mean[:], 1.0 / dv, None, ALU.mult),
            lambda: v.tensor_tensor(O4, O4, over(mean), ALU.subtract),
            lambda: v.tensor_tensor(U4, O4, O4, ALU.mult),
            lambda: v.tensor_reduce(var[:], U4, AX_X, ALU.add),
            lambda: v.tensor_scalar(var[:], var[:], 1.0 / dv, EPS, ALU.mult, ALU.add)])
        scalar_step(core, lambda: nc.scalar.activation(var[:], var[:], ACT.Sqrt))
        vector_steps(core, [
            lambda: v.reciprocal(var[:], var[:]),
            lambda: v.tensor_tensor(O4, O4, over(var), ALU.mult),
            lambda: v.tensor_tensor(O4, O4, along(w["L0_attn_ln_g"]), ALU.mult),
            lambda: v.tensor_tensor(O4, O4, along(w["L0_attn_ln_b"]), ALU.add)])
        turn(core, O, DC, uT)
        linear_rows(core, uT, w["L0_attn_Wo"], X, None, X)


def scalar_step(core, run):
    nc, step = core.nc, core.semaphore("scalar_step")
    with nc.Block() as block:
        @block.scalar
        def _(act):
            wait_weights(core, act)
            run().then_inc(step.sem, 1)
    step.passed(1)


def top_two(core, own, scores):
    nc, step = core.nc, core.semaphore("vector_step")
    best = core.sb(own, "best", [P, TILES, 8])
    place = core.sb(own, "place", [P, TILES, 8], U32)
    placef = core.sb(own, "place_f", [P, TILES, 8])
    first = core.sb(own, "first", [P, TILES, EXPERTS])
    second = core.sb(own, "second", [P, TILES, EXPERTS])
    iota = weights(core, own, iota8=[P, EXPERTS])["iota8"]
    with nc.Block() as block:
        @block.vector
        def _(dve):
            for t in range(TILES):
                nc.vector.max(best[:, t, :], scores[:, t, :]).then_inc(step.sem, 1)
            dve.wait_ge(step.sem, step.at(TILES))
            for t in range(TILES):
                nc.vector.max_index(place[:, t, :], best[:, t, :], scores[:, t, :]).then_inc(step.sem, 1)
            dve.wait_ge(step.sem, step.at(2 * TILES))
            nc.vector.tensor_copy(placef[:], place[:]).then_inc(step.sem, 1)
            dve.wait_ge(step.sem, step.at(2 * TILES + 1))
            wait_weights(core, dve)
            for n, out in enumerate((first, second)):
                nc.vector.tensor_tensor(out[:], iota[:].unsqueeze(1).broadcast_to([P, TILES, EXPERTS]),
                                        placef[:, :, n:n + 1].broadcast_to([P, TILES, EXPERTS]),
                                        ALU.is_equal).then_inc(step.sem, 1)
    step.passed(2 * TILES + 3)
    return best, first, second


def spread(a):
    return a.broadcast_to([P, TILES, EXPERTS])


def gate_bias(core, gates, b2, acc):
    nc, PS = core.nc, core.PS
    ready, taken, rows_ready, rows_taken = (core.semaphore("fill_ready"), core.semaphore("fill_taken_act"),
                                            core.semaphore("rows_ready"), core.semaphore("rows_taken"))
    with ExitStack() as own:
        gT = core.sb(own, "gates_turned", [EXPERTS, TILES, P])
        with nc.Block() as block:
            @block.tensor
            def _(pe):
                wait_weights(core, pe)
                for t in range(TILES):
                    last = nc.tensor.transpose(PS[0:EXPERTS, t // 4, (t % 4) * P:(t % 4 + 1) * P], gates[:, t, :], core.ident[:])
                last.then_inc(ready.sem, 1)
                pe.wait_ge(taken.sem, taken.at(1))
                for t in range(TILES):
                    last = nc.tensor.matmul(PS[:, 2 + t // 2, (t % 2) * DIM:(t % 2 + 1) * DIM], gT[:, t, :], b2[:], start=True, stop=True)
                last.then_inc(rows_ready.sem, 1)

            @block.scalar
            def _(act):
                act.wait_ge(ready.sem, ready.at(1))
                nc.scalar.copy(gT[:].rearrange("e t p -> e (t p)"),
                               PS[0:EXPERTS, 0:2, :].rearrange("e b n -> e (b n)")).then_inc(taken.sem, 1)

            @block.vector
            def _(dve):
                dve.wait_ge(rows_ready.sem, rows_ready.at(1))
                nc.vector.tensor_copy(acc[:].rearrange("p t d -> p (t d)"),
                                      PS[:, 2:6, :].rearrange("p b n -> p (b n)")).then_inc(rows_taken.sem, 1)
    for s in (ready, taken, rows_ready, rows_taken):
        s.passed(1)


def experts(core, xT, gates, acc, w1, b1, w2, func, gain=None, shift=None, wm=None, bm=None):
    nc, PS = core.nc, core.PS
    hidden = 4 * DIM
    FC = hidden // P
    mult, affine = wm is not None, gain is not None
    landed = core.semaphores("expert_landed", 2)
    up_ready, up_act, up_dve = core.semaphore("up_ready"), core.semaphore("up_taken_act"), core.semaphore("up_taken_dve")
    down_ready, down_taken, h_ready = core.semaphore("down_ready"), core.semaphore("down_taken"), core.semaphore("input_ready")
    loads = 3 + (2 if mult else 0) + (2 if affine else 0)
    ups = FC * HALVES
    ring = 2 if mult else 4
    dr = 4
    with ExitStack() as own:
        w1s = core.sb(own, "w1", [P, 2, DC, hidden])
        w2s = core.sb(own, "w2", [P, 2, FC, DIM])
        b1s = core.sb(own, "b1", [P, 2, FC])
        if mult:
            wms, bms = core.sb(own, "wm", [P, 2, DC, hidden]), core.sb(own, "bm", [P, 2, FC])
        if affine:
            gs, ss = core.sb(own, "gain", [P, 2, DC]), core.sb(own, "shift", [P, 2, DC])
            h = core.sb(own, "h", [P, DC, TOKENS])
        else:
            h = xT
        aT = core.sb(own, "hidden", [P, FC, TOKENS])
        warm = core.sb(own, "warm", [1, 1])
        with nc.Block() as block:
            @block.sync
            def _(sp):
                with sp.Fori(0, EXPERTS // 2) as it:
                    for u in range(2):
                        e = it * 2 + u
                        sp.wait_ge(down_ready.sem, down_ready.at(e * TILES + TILES))
                        todo = [(w1s[:, u], w1), (b1s[:, u], b1), (w2s[:, u], w2)]
                        if mult:
                            todo += [(wms[:, u], wm), (bms[:, u], bm)]
                        if affine:
                            todo += [(gs[:, u], gain), (ss[:, u], shift)]
                        for dst, src in todo:
                            sp.dma_start(dst, src[bass.ds(e, 1)].squeeze(0)).then_inc(landed[u].sem, 16)

            @block.tensor
            def _(pe):
                pe.sem_inc(down_ready.sem, 2 * TILES)
                pe.sem_inc(up_ready.sem, 1)
                with pe.Fori(0, EXPERTS // 2) as it:
                    for u in range(2):
                        e = it * 2 + u
                        pe.wait_ge(landed[u].sem, landed[u].at(it * 16 * loads + 16 * loads))
                        if affine:
                            pe.wait_ge(h_ready.sem, h_ready.at(e * DC + DC))
                        for f in range(FC):
                            for half in range(HALVES):
                                k = f * HALVES + half
                                pe.wait_ge(up_act.sem, up_act.at(e * ups + k + 1))
                                if mult:
                                    pe.wait_ge(up_dve.sem, up_dve.at(e * ups + k + 1))
                                for x, ws in enumerate((w1s, wms) if mult else (w1s,)):
                                    for c in range(DC):
                                        last = nc.tensor.matmul(PS[:, k % ring + 2 * x, :], ws[:, u, c, f * P:(f + 1) * P],
                                                                h[:, c, half * 512:(half + 1) * 512],
                                                                start=(c == 0), stop=(c == DC - 1))
                                last.then_inc(up_ready.sem, 1)
                        if mult:
                            pe.wait_ge(up_dve.sem, up_dve.at(e * ups + ups + ring))
                        else:
                            pe.wait_ge(up_act.sem, up_act.at(e * ups + ups + ring))
                        for t in range(TILES):
                            pe.wait_ge(down_taken.sem, down_taken.at(e * TILES + t + 1))
                            for f in range(FC):
                                last = nc.tensor.matmul(PS[:, 4 + t % dr, 0:DIM], aT[:, f, t * P:(t + 1) * P], w2s[:, u, f, :],
                                                        start=(f == 0), stop=(f == FC - 1))
                            last.then_inc(down_ready.sem, 1)

            @block.scalar
            def _(act):
                nc.scalar.activation(warm[:], core.ident[0:1, 0:1], func)
                act.sem_inc(up_act.sem, ring)
                with act.Fori(0, EXPERTS // 2) as it:
                    for u in range(2):
                        e = it * 2 + u
                        for f in range(FC):
                            for half in range(HALVES):
                                k = f * HALVES + half
                                act.wait_ge(up_ready.sem, up_ready.at(e * ups + k + 2))
                                nc.scalar.activation(aT[:, f, half * 512:(half + 1) * 512], PS[:, k % ring, :], func,
                                                     bias=b1s[:, u, f:f + 1]).then_inc(up_act.sem, 1)

            @block.vector
            def _(dve):
                dve.sem_inc(down_taken.sem, dr)
                if mult:
                    dve.sem_inc(up_dve.sem, ring)
                with dve.Fori(0, EXPERTS // 2) as it:
                    for u in range(2):
                        e = it * 2 + u
                        if affine:
                            dve.wait_ge(landed[u].sem, landed[u].at(it * 16 * loads + 16 * loads))
                            dve.wait_ge(up_ready.sem, up_ready.at(e * ups + 1))
                            for c in range(DC):
                                nc.vector.tensor_scalar(h[:, c, :], xT[:, c, :], gs[:, u, c:c + 1], ss[:, u, c:c + 1],
                                                        ALU.mult, ALU.add).then_inc(h_ready.sem, 1)
                        if mult:
                            for f in range(FC):
                                for half in range(HALVES):
                                    k = f * HALVES + half
                                    a = aT[:, f, half * 512:(half + 1) * 512]
                                    dve.wait_ge(up_act.sem, up_act.at(e * ups + k + 1 + ring))
                                    nc.vector.scalar_tensor_tensor(a, PS[:, k % ring + 2, :], bms[:, u, f:f + 1], a,
                                                                   ALU.add, ALU.mult).then_inc(up_dve.sem, 1)
                        for t in range(TILES):
                            dve.wait_ge(down_ready.sem, down_ready.at(e * TILES + t + 1 + 2 * TILES))
                            nc.vector.scalar_tensor_tensor(
                                acc[:, t, :], PS[:, 4 + t % dr, 0:DIM], gates[:, t, bass.ds(e, 1)], acc[:, t, :],
                                ALU.mult, ALU.add).then_inc(down_taken.sem, 1)
    for s in landed:
        s.passed(16 * loads * EXPERTS // 2)
    up_ready.passed(ups * EXPERTS + 1)
    up_act.passed(ups * EXPERTS + ring)
    down_ready.passed(TILES * EXPERTS + 2 * TILES)
    down_taken.passed(TILES * EXPERTS + dr)
    if mult:
        up_dve.passed(ups * EXPERTS + ring)
    if affine:
        h_ready.passed(DC * EXPERTS)


def l0_ffn(core):
    nc, X = core.nc, core.X
    v = nc.vector
    with ExitStack() as own:
        w = weights(core, own, L0_ffn_router_W=[P, DC, EXPERTS], L0_ffn_router_b=[1, EXPERTS], L0_ffn_b2=[EXPERTS, DIM])
        U = core.sb(own, "u", [P, TILES, DIM])
        hat = core.sb(own, "hat", [P, TILES, DIM])
        uT = core.sb(own, "uT", [P, DC, TOKENS])
        logits = core.sb(own, "logits", [P, TILES, EXPERTS])
        gates = core.sb(own, "gates", [P, TILES, EXPERTS])
        acc = core.sb(own, "acc", [P, TILES, DIM])
        share = core.sb(own, "share", [P, TILES, 2])
        whole = core.sb(own, "gate_sum", [P, TILES])
        normalize(core, X, U)
        turn(core, U, DC, uT)
        linear_rows(core, uT, w["L0_ffn_router_W"], logits, w["L0_ffn_router_b"])
        best, first, second = top_two(core, own, logits)
        vector_steps(core, [lambda: v.tensor_tensor(share[:], best[:, :, 0:2], best[:, :, 0:1].broadcast_to([P, TILES, 2]), ALU.subtract)])
        scalar_step(core, lambda: nc.scalar.activation(share[:], share[:], ACT.Exp))
        vector_steps(core, [
            lambda: v.tensor_reduce(whole[:], share[:], AX_X, ALU.add),
            lambda: v.reciprocal(whole[:], whole[:]),
            lambda: v.tensor_tensor(share[:], share[:], whole[:].unsqueeze(2).broadcast_to([P, TILES, 2]), ALU.mult),
            lambda: v.tensor_tensor(first[:], first[:], spread(share[:, :, 0:1]), ALU.mult),
            lambda: v.tensor_tensor(second[:], second[:], spread(share[:, :, 1:2]), ALU.mult),
            lambda: v.tensor_tensor(gates[:], first[:], second[:], ALU.add)])
        gate_bias(core, gates, w["L0_ffn_b2"], acc)
        vector_steps(core, [
            lambda: v.tensor_reduce(whole[:], gates[:], AX_X, ALU.add),
            lambda: v.tensor_tensor(hat[:], U[:], whole[:].unsqueeze(2).broadcast_to([P, TILES, DIM]), ALU.mult),
            lambda: v.tensor_tensor(acc[:], acc[:], hat[:], ALU.add)])
        normalize(core, U, hat)
        turn(core, hat, DC, uT)
        d = core.dram
        experts(core, uT, gates, acc, d["L0_ffn_W1"], d["L0_ffn_b1"], d["L0_ffn_W2"], ACT.Gelu,
                gain=d["L0_ffn_ln_g"], shift=d["L0_ffn_ln_b"])
        add(core, X, X, acc)


def l1_ffn(core):
    nc, X = core.nc, core.X
    v = nc.vector
    with ExitStack() as own:
        w = weights(core, own, L1_ffn_router_w=[P, DC, EXPERTS], L1_ffn_w2_b=[EXPERTS, DIM])
        U = core.sb(own, "u", [P, TILES, DIM])
        uT = core.sb(own, "uT", [P, DC, TOKENS])
        probs = core.sb(own, "probs", [P, TILES, EXPERTS])
        gates = core.sb(own, "gates", [P, TILES, EXPERTS])
        acc = core.sb(own, "acc", [P, TILES, DIM])
        top = core.sb(own, "top", [P, TILES])
        normalize(core, X, U)
        turn(core, U, DC, uT)
        linear_rows(core, uT, w["L1_ffn_router_w"], probs)
        softmax_experts(core, probs, top, None)
        best, first, second = top_two(core, own, probs)
        vector_steps(core, [
            lambda: v.tensor_tensor(first[:], first[:], spread(best[:, :, 0:1]), ALU.mult),
            lambda: v.tensor_tensor(second[:], second[:], spread(best[:, :, 1:2]), ALU.mult),
            lambda: v.tensor_tensor(gates[:], first[:], second[:], ALU.add)])
        gate_bias(core, gates, w["L1_ffn_w2_b"], acc)
        d = core.dram
        experts(core, uT, gates, acc, d["L1_ffn_wg_w"], d["L1_ffn_wg_b"], d["L1_ffn_w2_w"], ACT.Gelu,
                wm=d["L1_ffn_w1_w"], bm=d["L1_ffn_w1_b"])
        add(core, X, X, acc)


def softmax_experts(core, scores, top, keep):
    nc = core.nc
    v = nc.vector
    wide = lambda a: a[:].unsqueeze(2).broadcast_to([P, TILES, EXPERTS])
    vector_steps(core, [
        lambda: v.tensor_reduce(top[:], scores[:], AX_X, ALU.max),
        lambda: v.tensor_tensor(scores[:], scores[:], wide(top), ALU.subtract)])
    scalar_step(core, lambda: nc.scalar.activation(scores[:], scores[:], ACT.Exp))
    vector_steps(core, ([lambda: v.tensor_tensor(scores[:], scores[:], keep[:], ALU.mult)] if keep is not None else []) + [
        lambda: v.tensor_reduce(top[:], scores[:], AX_X, ALU.add),
        lambda: v.reciprocal(top[:], top[:]),
        lambda: v.tensor_tensor(scores[:], scores[:], wide(top), ALU.mult)])


def l2_ffn(core):
    nc, X = core.nc, core.X
    v = nc.vector
    with ExitStack() as own:
        w = weights(core, own, L2_ffn_W_gate=[P, DC, EXPERTS], L2_ffn_b2=[EXPERTS, DIM])
        U = core.sb(own, "u", [P, TILES, DIM])
        uT = core.sb(own, "uT", [P, DC, TOKENS])
        gates = core.sb(own, "gates", [P, TILES, EXPERTS])
        keep = core.sb(own, "keep", [P, TILES, EXPERTS])
        best = core.sb(own, "best", [P, TILES, 8])
        acc = core.sb(own, "acc", [P, TILES, DIM])
        top = core.sb(own, "top", [P, TILES])
        normalize(core, X, U)
        turn(core, U, DC, uT)
        linear_rows(core, uT, w["L2_ffn_W_gate"], gates)
        vector_steps(core, [(lambda t: lambda: v.max(best[:, t, :], gates[:, t, :]))(t) for t in range(TILES)] + [
            lambda: v.tensor_tensor(keep[:], gates[:], spread(best[:, :, 1:2]), ALU.is_ge)])
        softmax_experts(core, gates, top, keep)
        vector_steps(core, [lambda: v.tensor_scalar(gates[:], gates[:], 1.0 / EXPERTS, None, ALU.mult)])
        gate_bias(core, gates, w["L2_ffn_b2"], acc)
        d = core.dram
        experts(core, uT, gates, acc, d["L2_ffn_W1"], d["L2_ffn_b1"], d["L2_ffn_W2"], ACT.Relu)
        add(core, X, X, acc)


def l1_xattn(core):
    small_xattn(core, "L1_xattn_", True)


def l3_xattn(core):
    small_xattn(core, "L3_xattn_", False)


def small_xattn(core, pre, biased):
    heads, d, pad = 16, 16, 32
    X = core.X
    with ExitStack() as own:
        shapes = {"Wq": [P, DC, heads * pad], "WkT": [P, heads * pad // P, CDIM], "Wv": [P, DIM], "Wo": [P, DC, DIM],
                  "bv": [P, DC]}
        if biased:
            shapes.update({"bq": [P, heads * pad // P], "bo": [1, DIM]})
        w = {k[len(pre):]: t for k, t in weights(core, own, **{pre + k: s for k, s in shapes.items()}).items()}
        sums = core.sb(own, "sums", [P, BATCH, heads // 2, d])
        with ExitStack() as front:
            U = core.sb(front, "u", [P, TILES, DIM])
            uT = core.sb(front, "uT", [P, DC, TOKENS])
            qT = core.sb(front, "qT", [P, heads * pad // P, TOKENS])
            normalize(core, X, U)
            turn(core, U, DC, uT)
            linear_turned(core, uT, w["Wq"], qT, w["bq"] if biased else None)
            context_queries(core, qT, w["WkT"], heads, pad, None, "context_q16")
        wv4 = w["Wv"][:].rearrange("c (a p d) -> c p a d", a=2, d=d)
        context_attention(core, "context_q16", core.dram["ctx_512"], lambda pair: wv4[:, pair], sums, heads // 2, P, 4, 2,
                          d ** -0.5, d)
        oT = core.sb(own, "oT", [P, DC, TOKENS])
        turn_sums(core, sums, heads // 2, d, oT, w["bv"])
        linear_rows(core, oT, w["Wo"], X, w["bo"] if biased else None, X)


def l2_xattn(core):
    X, nc = core.X, core.nc
    with ExitStack() as own:
        w = weights(core, own, L2_xattn_Wq=[P, DC, DIM], L2_xattn_bq=[P, DC], L2_xattn_WkT=[P, DC, CDIM],
                    L2_xattn_Wv=[P, DIM], L2_xattn_bv=[P, DIM])
        sums = core.sb(own, "sums", [SEQ, BATCH, 1, DIM])
        with ExitStack() as front:
            U = core.sb(front, "u", [P, TILES, DIM])
            uT = core.sb(front, "uT", [P, DC, TOKENS])
            qT = core.sb(front, "qT", [P, DC, TOKENS])
            normalize(core, X, U)
            turn(core, U, DC, uT)
            linear_turned(core, uT, w["L2_xattn_Wq"], qT, w["L2_xattn_bq"])
            context_queries(core, qT, w["L2_xattn_WkT"], 1, DIM, None, "context_q1")
        context_attention(core, "context_q1", core.dram["ctx_512"], lambda pair: w["L2_xattn_Wv"][:].unsqueeze(1), sums, 1, SEQ,
                          1, 4, 1.0, DIM)
        out = core.sb(own, "out", [P, TILES, DIM])
        s5 = sums[:].rearrange("s (t a) x d -> s t a (x d)", a=2)
        store(core, [(out[a * SEQ:(a + 1) * SEQ], s5[:, :, a, :]) for a in range(2)])
        v = nc.vector
        vector_steps(core, [
            lambda: v.tensor_tensor(out[:], out[:], w["L2_xattn_bv"][:].unsqueeze(1).broadcast_to([P, TILES, DIM]), ALU.add),
            lambda: v.tensor_tensor(X[:], X[:], out[:], ALU.add)])


def l1_attn(core):
    nc, X, PS = core.nc, core.X, core.PS
    v = nc.vector
    inner, states = 512, 16
    C = inner // P
    with ExitStack() as own:
        w = weights(core, own, L1_attn_norm_w=[P, DC], L1_attn_norm_b=[P, DC], L1_attn_W_in=[P, DC, inner],
                    L1_attn_W_gate=[P, DC, inner], L1_attn_W_dt=[P, C, inner], L1_attn_b_dt=[P, C],
                    L1_attn_W_BC=[P, C, 2 * states], L1_attn_A_log=[P, C, states], L1_attn_W_out=[P, C, DIM])
        zT = core.sb(own, "zT", [P, C, TOKENS])
        gateT = core.sb(own, "gateT", [P, C, TOKENS])
        dtT = core.sb(own, "dtT", [P, C, TOKENS])
        A = w["L1_attn_A_log"]
        with ExitStack() as front:
            U = core.sb(front, "u", [P, TILES, DIM])
            uT = core.sb(front, "uT", [P, DC, TOKENS])
            bcT = core.sb(front, "bcT", [2 * states, 1, TOKENS])
            e = core.sb(front, "e", [P, C, TOKENS])
            normalize(core, X, U)
            add(core, X, X, U)
            normalize(core, U, U)
            turn(core, U, DC, uT, w["L1_attn_norm_w"], w["L1_attn_norm_b"])
            linear_turned(core, uT, w["L1_attn_W_in"], zT)
            linear_turned(core, uT, w["L1_attn_W_gate"], gateT, None, ACT.Silu)
            linear_turned(core, zT, w["L1_attn_W_dt"], dtT, w["L1_attn_b_dt"])
            linear_turned(core, zT, w["L1_attn_W_BC"], bcT, rows=2 * states)
            store(core, [(core.dram["bc_turned"], bcT[:, 0, :])])
            scalar_step(core, lambda: nc.scalar.activation(e[:], dtT[:], ACT.Abs))
            scalar_step(core, lambda: nc.scalar.activation(e[:], e[:], ACT.Exp, scale=-1.0))
            scalar_step(core, lambda: nc.scalar.activation(A[:], A[:], ACT.Exp))
            scalar_step(core, lambda: nc.scalar.activation(e[:], e[:], ACT.Ln, bias=1.0))
            vector_steps(core, [
                lambda: v.scalar_tensor_tensor(dtT[:], dtT[:], 0.0, e[:], ALU.max, ALU.add),
                lambda: v.tensor_scalar(dtT[:], dtT[:], 0.001, 1.0, ALU.max, ALU.min),
                lambda: v.tensor_tensor(zT[:], zT[:], dtT[:], ALU.mult),
                lambda: v.tensor_scalar(A[:], A[:], 1e-6, 1.0, ALU.max, ALU.min),
                lambda: v.tensor_scalar(A[:], A[:], -1.0, None, ALU.mult),
                lambda: v.memset(dtT[:].rearrange("p c (b s) -> p c b s", s=SEQ)[:, :, :, 0:1], 1e30)])
        selective_scan(core, zT, dtT, A, C, states)
        y = dtT
        vector_steps(core, [lambda: v.tensor_tensor(y[:].rearrange("p c n -> p (c n)"), PS[:].rearrange("p b n -> p (b n)"),
                                                    gateT[:].rearrange("p c n -> p (c n)"), ALU.mult)])
        linear_rows(core, y, w["L1_attn_W_out"], X, None, X)


def selective_scan(core, dtz, dt, A, C, states):
    nc, PS = core.nc, core.PS
    landed = core.semaphores("rows_landed", 2)
    decay_ready, in_ready, h_ready, w_ready, summed = (core.semaphore("decay_ready"), core.semaphore("scan_in_ready"),
                                                       core.semaphore("state_ready"), core.semaphore("product_ready"),
                                                       core.semaphore("product_summed"))
    zero_ready = core.semaphore("zero_ready")
    bc = core.dram["bc_turned"]
    with ExitStack() as own:
        Bb = core.sb(own, "b_all", [P, 2, TOKENS])
        Cb = core.sb(own, "c_all", [P, 2, TOKENS])
        decay = core.sb(own, "decay", [P, 2, TOKENS])
        fresh = core.sb(own, "fresh", [P, 2, TOKENS])
        state = core.sb(own, "state", [P, 2, TOKENS])
        prod = core.sb(own, "prod", [P, 2, TOKENS])
        zeros = core.sb(own, "zeros", [P, 512])
        warm = core.sb(own, "warm", [1, 1])
        with nc.Block() as block:
            @block.sync
            def _(sp):
                with sp.Fori(0, states // 2) as it:
                    for u in range(2):
                        s = it * 2 + u
                        sp.wait_ge(w_ready.sem, w_ready.at(s * C + C))
                        sp.dma_start(Bb[:, u, :], bc[bass.ds(s, 1), :].broadcast_to([P, TOKENS])).then_inc(landed[u].sem, 16)
                        sp.dma_start(Cb[:, u, :], bc[bass.ds(s + states, 1), :].broadcast_to([P, TOKENS])).then_inc(landed[u].sem, 16)

            @block.scalar
            def _(act):
                nc.scalar.activation(warm[:], core.ident[0:1, 0:1], ACT.Exp)
                with act.Fori(0, states // 2) as it:
                    for u in range(2):
                        for c in range(C):
                            n = (it * 2 + u) * C + c
                            act.wait_ge(h_ready.sem, h_ready.at(n + 1))
                            nc.scalar.activation(decay[:, c % 2, :], dt[:, c, :], ACT.Exp,
                                                 scale=A[:, c, bass.ds(it * 2 + u, 1)]).then_inc(decay_ready.sem, 1)

            @block.gpsimd
            def _(pool):
                with pool.Fori(0, states // 2) as it:
                    for u in range(2):
                        pool.wait_ge(landed[u].sem, landed[u].at(it * 32 + 32))
                        for c in range(C):
                            n = (it * 2 + u) * C + c
                            pool.wait_ge(h_ready.sem, h_ready.at(n + 1))
                            nc.gpsimd.tensor_tensor(fresh[:, c % 2, :], dtz[:, c, :], Bb[:, u, :], ALU.mult).then_inc(in_ready.sem, 1)

            @block.vector
            def _(dve):
                nc.vector.memset(zeros[:], 0.0).then_inc(zero_ready.sem, 1)
                dve.sem_inc(h_ready.sem, 2)
                dve.sem_inc(w_ready.sem, 2 * C)
                with dve.Fori(0, states // 2) as it:
                    for u in range(2):
                        dve.wait_ge(landed[u].sem, landed[u].at(it * 32 + 32))
                        for c in range(C):
                            n = (it * 2 + u) * C + c
                            dve.wait_ge(decay_ready.sem, decay_ready.at(n + 1))
                            dve.wait_ge(in_ready.sem, in_ready.at(n + 1))
                            nc.vector.tensor_tensor_scan(state[:, c % 2, :], decay[:, c % 2, :], fresh[:, c % 2, :], 0.0,
                                                         ALU.mult, ALU.add).then_inc(h_ready.sem, 1)
                            dve.wait_ge(h_ready.sem, h_ready.at(n + 3))
                            dve.wait_ge(summed.sem, summed.at(n + 1))
                            nc.vector.tensor_tensor(prod[:, c % 2, :], state[:, c % 2, :], Cb[:, u, :], ALU.mult).then_inc(w_ready.sem, 1)

            @block.tensor
            def _(pe):
                pe.sem_inc(summed.sem, 2)
                pe.wait_ge(zero_ready.sem, zero_ready.at(1))
                for k in range(BANKS):
                    nc.tensor.matmul(PS[:, k, :], core.ident[:], zeros[:], start=True, stop=False, skip_group_check=True)
                with pe.Fori(0, states // 2) as it:
                    for u in range(2):
                        for c in range(C):
                            n = (it * 2 + u) * C + c
                            pe.wait_ge(w_ready.sem, w_ready.at(n + 1 + 2 * C))
                            for half in range(HALVES):
                                last = nc.tensor.matmul(PS[:, c * HALVES + half, :], core.ident[:],
                                                        prod[:, c % 2, half * 512:(half + 1) * 512], start=False, stop=False,
                                                        skip_group_check=True)
                            last.then_inc(summed.sem, 1)
                for k in range(BANKS):
                    last = nc.tensor.matmul(PS[:, k, :], core.ident[:], zeros[:], start=False, stop=True, skip_group_check=True)
                last.then_inc(summed.sem, 1)
                pe.wait_ge(summed.sem, summed.at(states * C + 3))
    n = states * C
    for s in landed:
        s.passed(32 * states // 2)
    decay_ready.passed(n)
    in_ready.passed(n)
    h_ready.passed(n + 2)
    w_ready.passed(n + 2 * C)
    summed.passed(n + 3)
    zero_ready.passed(1)


def l2_attn(core):
    nc, X = core.nc, core.X
    v = nc.vector
    heads, d = 16, 16
    with ExitStack() as own:
        w = weights(core, own, L2_attn_key_w=[P, DC, DIM], L2_attn_key_b=[P, DC], L2_attn_v_w=[P, DC, DIM],
                    L2_attn_q_w=[P, DC, DIM], L2_attn_out_w=[P, DC, DIM], L2_attn_out_b=[1, DIM], gather_rows=[P, d, P])
        kT = core.sb(own, "kT", [P, DC, TOKENS])
        freshT = core.sb(own, "freshT", [P, DC, TOKENS])
        qT = core.sb(own, "qT", [P, DC, TOKENS])
        vT = core.sb(own, "vT", [P, DC, TOKENS])
        U = core.sb(own, "u", [P, TILES, DIM])
        uT = core.sb(own, "uT", [P, DC, TOKENS])
        normalize(core, X, U)
        turn(core, U, DC, uT)
        linear_turned(core, uT, w["L2_attn_v_w"], vT)
        store(core, [(core.dram["v_turned"].rearrange("(c p) n -> p c n", p=P), vT[:])])
        linear_turned(core, uT, w["L2_attn_q_w"], qT)
        linear_turned(core, uT, w["L2_attn_key_w"], kT, w["L2_attn_key_b"], ACT.Sigmoid)
        vector_steps(core, [
            lambda: v.tensor_scalar(freshT[:], kT[:], -1.0, 1.0, ALU.mult, ALU.add),
            lambda: v.memset(kT[:].rearrange("p c (b s) -> p c b s", s=SEQ)[:, :, :, 0:1], 0.0)])
        memory_scan(core, kT, freshT, qT, w["gather_rows"], uT, d)
        linear_rows(core, uT, w["L2_attn_out_w"], X, w["L2_attn_out_b"], X)


def memory_scan(core, kT, freshT, qT, gather, dst, d):
    nc, PS = core.nc, core.PS
    landed, used = core.semaphores("rows_landed", DC), core.semaphore("rows_used")
    in_ready, h_ready, w_ready, summed = (core.semaphore("scan_in_ready"), core.semaphore("state_ready"),
                                          core.semaphore("product_ready"), core.semaphore("product_summed"))
    taken = core.semaphore("rows_taken")
    per = P // d
    vrows = core.dram["v_turned"].rearrange("(c h e) n -> c h e n", c=DC, e=d)
    with ExitStack() as own:
        Vb = core.sb(own, "v_all", [P, DC, TOKENS])
        fresh = core.sb(own, "fresh", [P, DC, TOKENS])
        state = core.sb(own, "state", [P, DC, TOKENS])
        prod = core.sb(own, "prod", [P, DC, TOKENS])
        with nc.Block() as block:
            @block.sync
            def _(sp):
                with sp.Fori(0, d) as e:
                    for c in range(DC):
                        sp.wait_ge(used.sem, used.at(e * DC + c + 1))
                        for h in range(per):
                            sp.dma_start(Vb[h * d:(h + 1) * d, c, :],
                                         vrows[c, h, bass.ds(e, 1), :].broadcast_to([d, TOKENS])).then_inc(landed[c].sem, 16)

            @block.gpsimd
            def _(pool):
                pool.sem_inc(used.sem, DC)
                with pool.Fori(0, d) as e:
                    for c in range(DC):
                        n = e * DC + c
                        pool.wait_ge(landed[c].sem, landed[c].at(e * 16 * per + 16 * per))
                        pool.wait_ge(h_ready.sem, h_ready.at(n + 1))
                        nc.gpsimd.tensor_tensor(fresh[:, c, :], freshT[:, c, :], Vb[:, c, :], ALU.mult).then_inc(in_ready.sem, 1)
                        pool.wait_ge(in_ready.sem, in_ready.at(n + 1))
                        pool.sem_inc(used.sem, 1)

            @block.vector
            def _(dve):
                dve.sem_inc(h_ready.sem, DC)
                with dve.Fori(0, d) as e:
                    for c in range(DC):
                        n = e * DC + c
                        dve.wait_ge(in_ready.sem, in_ready.at(n + 1))
                        nc.vector.tensor_tensor_scan(state[:, c, :], kT[:, c, :], fresh[:, c, :], 0.0,
                                                     ALU.mult, ALU.add).then_inc(h_ready.sem, 1)
                        dve.wait_ge(h_ready.sem, h_ready.at(n + DC + 1))
                        dve.wait_ge(summed.sem, summed.at(n + 1))
                        nc.vector.tensor_tensor(prod[:, c, :], state[:, c, :], qT[:, c, :], ALU.mult).then_inc(w_ready.sem, 1)
                dve.wait_ge(summed.sem, summed.at(d * DC + DC))
                nc.vector.tensor_copy(dst[:].rearrange("p c n -> p (c n)"),
                                      PS[:, 0:DC * HALVES, :].rearrange("p b n -> p (b n)")).then_inc(taken.sem, 1)

            @block.tensor
            def _(pe):
                wait_weights(core, pe)
                pe.sem_inc(summed.sem, DC)
                for e in range(d):
                    for c in range(DC):
                        pe.wait_ge(w_ready.sem, w_ready.at(e * DC + c + 1))
                        for half in range(HALVES):
                            last = nc.tensor.matmul(PS[:, c * HALVES + half, :], gather[:, e, :],
                                                    prod[:, c, half * 512:(half + 1) * 512], start=(e == 0), stop=(e == d - 1),
                                                    skip_group_check=True)
                        last.then_inc(summed.sem, 1)
    n = d * DC
    for s in landed:
        s.passed(16 * per * d)
    used.passed(n + DC)
    in_ready.passed(n)
    h_ready.passed(n + DC)
    w_ready.passed(n)
    summed.passed(n + DC)
    taken.passed(1)


def rotate(core, xT, swap, cos, sin):
    nc, PS = core.nc, core.PS
    ready, taken, step = core.semaphore("fill_ready"), core.semaphore("fill_taken_dve"), core.semaphore("norm_step")
    cos_done = core.semaphore("cos_done")
    fills = xT.shape[1] * HALVES
    nb = 512 // SEQ
    wide = lambda a: a[:].unsqueeze(1).broadcast_to([P, nb, SEQ])
    with ExitStack() as own:
        part = core.sb(own, "part", [P, 2, 512])
        with nc.Block() as block:
            @block.tensor
            def _(pe):
                wait_weights(core, pe)
                for f in range(fills):
                    c, half = f // HALVES, f % HALVES
                    if f >= BANKS:
                        pe.wait_ge(step.sem, step.at(f - BANKS + 1))
                    nc.tensor.matmul(PS[:, f % BANKS, :], swap[:], xT[:, c, half * 512:(half + 1) * 512],
                                     start=True, stop=True).then_inc(ready.sem, 1)

            @block.gpsimd
            def _(pool):
                wait_weights(core, pool)
                for f in range(fills):
                    c, half = f // HALVES, f % HALVES
                    x = xT[:, c, half * 512:(half + 1) * 512].rearrange("p (b s) -> p b s", s=SEQ)
                    pool.wait_ge(ready.sem, ready.at(f + 1))
                    nc.gpsimd.tensor_tensor(x, x, wide(cos), ALU.mult).then_inc(cos_done.sem, 1)

            @block.vector
            def _(dve):
                wait_weights(core, dve)
                for f in range(fills):
                    c, half = f // HALVES, f % HALVES
                    x = xT[:, c, half * 512:(half + 1) * 512]
                    dve.wait_ge(ready.sem, ready.at(f + 1))
                    nc.vector.tensor_tensor(part[:, f % 2, :].rearrange("p (b s) -> p b s", s=SEQ),
                                            PS[:, f % BANKS, :].rearrange("p (b s) -> p b s", s=SEQ), wide(sin),
                                            ALU.mult).then_inc(step.sem, 1)
                    dve.wait_ge(step.sem, step.at(f + 1))
                    dve.wait_ge(cos_done.sem, cos_done.at(f + 1))
                    nc.vector.tensor_tensor(x, x, part[:, f % 2, :], ALU.add).then_inc(taken.sem, 1)
    for s in (ready, taken, step, cos_done):
        s.passed(fills)


def l3_attn(core):
    heads, hd = 16, 64
    inner = heads * hd
    C = inner // P
    X = core.X
    with ExitStack() as own:
        w = weights(core, own, L3_attn_ln_gamma=[P, DC], L3_attn_ln_beta=[P, DC], L3_attn_w_out=[P, C, DIM],
                    L3_attn_b_out=[1, DIM], rope_cos=[P, SEQ], rope_sin=[P, SEQ], rope_swap=[P, P])
        qT = core.sb(own, "qT", [P, C, TOKENS])
        V = core.sb(own, "v", [P, TILES, inner])
        with ExitStack() as keys:
            kT = core.sb(keys, "kT", [P, C, TOKENS])
            with ExitStack() as front:
                wqkv = weights(core, front, L3_attn_w_qkv=[P, DC, 3 * inner])["L3_attn_w_qkv"]
                U = core.sb(front, "u", [P, TILES, DIM])
                uT = core.sb(front, "uT", [P, DC, TOKENS])
                normalize(core, X, U)
                normalize(core, U, U)
                turn(core, U, DC, uT, w["L3_attn_ln_gamma"], w["L3_attn_ln_beta"])
                linear_turned(core, uT, wqkv[:, :, 0:inner], qT)
                linear_turned(core, uT, wqkv[:, :, inner:2 * inner], kT)
                linear_rows(core, uT, wqkv[:, :, 2 * inner:3 * inner], V)
            rotate(core, qT, w["rope_swap"], w["rope_cos"], w["rope_sin"])
            rotate(core, kT, w["rope_swap"], w["rope_cos"], w["rope_sin"])
            self_attention(core, qT, kT, V, V, heads, hd, hd, hd ** -0.5)
        turn(core, V, C, qT)
        linear_rows(core, qT, w["L3_attn_w_out"], X, w["L3_attn_b_out"], X)


def l3_ffn(core):
    heads, d = 8, 32
    nc, X = core.nc, core.X
    v = nc.vector
    pre = "L3_ffn_"
    with ExitStack() as own:
        shapes = {"norm_w": [P, DC], "norm_b": [P, DC], "q_w": [P, DC, DIM], "k_w": [P, DC, DIM], "v_w": [P, DC, DIM],
                  "o_w": [P, DC, DIM], "q_b": [P, DC], "k_b": [P, DC], "v_b": [1, DIM], "o_b": [1, DIM]}
        w = {k[len(pre):]: t for k, t in weights(core, own, **{pre + k: s for k, s in shapes.items()}).items()}
        masks = weights(core, own, width_turned=[P, DC, SEQ], width_rows=[P, DIM])
        U = core.sb(own, "u", [P, TILES, DIM])
        hat = core.sb(own, "hat", [P, TILES, DIM])
        uT = core.sb(own, "uT", [P, DC, TOKENS])
        qT = core.sb(own, "qT", [P, DC, TOKENS])
        kT = core.sb(own, "kT", [P, DC, TOKENS])
        V = core.sb(own, "v", [P, TILES, DIM])
        O = core.sb(own, "o", [P, TILES, DIM])
        normalize(core, X, U)
        normalize(core, U, hat)
        turn(core, hat, DC, uT, w["norm_w"], w["norm_b"])

        def cut(c):
            x = uT[:, c, :].rearrange("p (b s) -> p b s", s=SEQ)
            return v.tensor_tensor(x, x, masks["width_turned"][:, c, :].unsqueeze(1).broadcast_to([P, BATCH, SEQ]), ALU.mult)

        vector_steps(core, [(lambda c: lambda: cut(c))(c) for c in range(DC)])
        linear_turned(core, uT, w["q_w"], qT, w["q_b"])
        linear_turned(core, uT, w["k_w"], kT, w["k_b"])
        linear_rows(core, uT, w["v_w"], V, w["v_b"])
        self_attention(core, qT, kT, V, O, heads, d, d, DIM ** -0.5)
        rows_mask = masks["width_rows"][:].unsqueeze(1).broadcast_to([P, TILES, DIM])
        vector_steps(core, [lambda: v.tensor_tensor(O[:], O[:], rows_mask, ALU.mult)])
        turn(core, O, DC, uT)
        linear_rows(core, uT, w["o_w"], O, w["o_b"])
        vector_steps(core, [lambda: v.tensor_tensor(O[:], O[:], rows_mask, ALU.mult),
                            lambda: v.tensor_tensor(O[:], O[:], U[:], ALU.add),
                            lambda: v.tensor_tensor(X[:], X[:], O[:], ALU.add)])


def perceiver(nc, dram):
    sublayers = (l0_xattn, l0_attn, l0_ffn, l1_xattn, l1_attn, l1_ffn, l2_xattn, l2_attn, l2_ffn, l3_xattn, l3_attn, l3_ffn)
    with ExitStack() as hold:
        core = Core(nc, dram, hold)
        first = core.semaphore("vector_step")
        with nc.Block() as block:
            @block.vector
            def _(dve):
                nc.vector.memset(core.ones_row[:], 1.0).then_inc(first.sem, 1)
        first.passed(1)
        fetch(core, [(core.X[:], dram["x"].rearrange("(t p) d -> p t d", p=P)), (core.ident[:], dram["ident"])])
        with nc.Block() as block:
            @block.vector
            def _(dve):
                wait_weights(core, dve)

            @block.tensor
            def _(pe):
                wait_weights(core, pe)

            @block.scalar
            def _(act):
                wait_weights(core, act)
        for n in LAYERS:
            sublayers[n](core)
        store(core, [(dram["out"].rearrange("(t p) d -> p t d", p=P), core.X[:])])




def layouts(inputs):
    import numpy as np

    a = {k: np.asarray(v) for k, v in inputs.items()}
    out = {}

    def chunked(w):
        return w.reshape(-1, P, w.shape[-1]).transpose(1, 0, 2)

    def column(b):
        return b.reshape(-1, P).T

    def pad_heads(w, d, to):
        k = w.shape[0]
        r = np.zeros((k, w.shape[1] // d, to), w.dtype)
        r[:, :, :d] = w.reshape(k, -1, d)
        return r.reshape(k, -1)

    def halves_first(w, d):
        return w.reshape(-1, 2, d, w.shape[-1]).transpose(1, 0, 2, 3).reshape(w.shape)

    out["x"] = a["x"].reshape(TOKENS, DIM)
    out["ctx_512"] = a["ctx_512"]
    for n in ("ln1_g", "ln1_b", "ln2_g", "ln2_b"):
        out[f"L0_xattn_{n}"] = a[f"L0_xattn_{n}"][None]
    for p in ("L0_xattn_a1_", "L0_xattn_a2_"):
        cols = lambda w: w.transpose(1, 0, 2).reshape(w.shape[1], -1)
        out[p + "wq"] = chunked(cols(a[p + "wq"]))
        if "a1" in p:
            out[p + "wk"] = chunked(cols(a[p + "wk"]))
            out[p + "wv"] = chunked(cols(a[p + "wv"]))
            out[p + "li1_w"] = chunked(a[p + "li1_w"])
        else:
            out[p + "wkT"] = chunked(cols(a[p + "wk"]).T)
            out[p + "wv"] = chunked(halves_first(cols(a[p + "wv"]).T, 32).T)
            out[p + "li1_w"] = chunked(halves_first(a[p + "li1_w"], 32))
        for n in ("li2_w", "li3_w"):
            out[p + n] = chunked(a[p + n])
        for n in ("lnx_g", "lnx_b", "lny_g", "lny_b", "ln3_g", "ln3_b", "li2_b"):
            out[p + n] = column(a[p + n])
        for n in ("li1_b", "li3_b"):
            out[p + n] = a[p + n][None]
    for n in ("Wq", "Wk"):
        out["L0_attn_" + n] = chunked(pad_heads(a["L0_attn_" + n], 16, 32))
    for n in ("Wv", "Wo"):
        out["L0_attn_" + n] = chunked(a["L0_attn_" + n])
    for n in ("lq1", "lk1", "lq2", "lk2", "ln_g", "ln_b"):
        out["L0_attn_" + n] = a["L0_attn_" + n][None]

    def per_expert(w):
        return w.reshape(EXPERTS, -1, P, w.shape[-1]).transpose(0, 2, 1, 3)

    def expert_columns(b):
        return b.reshape(EXPERTS, -1, P).transpose(0, 2, 1)

    out["L0_ffn_router_W"] = chunked(a["L0_ffn_router_W"])
    out["L0_ffn_router_b"] = a["L0_ffn_router_b"][None]
    out["L0_ffn_b2"] = a["L0_ffn_b2"]
    out["L0_ffn_W1"], out["L0_ffn_W2"] = per_expert(a["L0_ffn_W1"]), per_expert(a["L0_ffn_W2"])
    for n in ("b1", "ln_g", "ln_b"):
        out["L0_ffn_" + n] = expert_columns(a["L0_ffn_" + n])
    for n in ("wg_w", "w1_w", "w2_w"):
        out["L1_ffn_" + n] = per_expert(a["L1_ffn_" + n].transpose(0, 2, 1))
    for n in ("wg_b", "w1_b"):
        out["L1_ffn_" + n] = expert_columns(a["L1_ffn_" + n])
    out["L1_ffn_w2_b"] = a["L1_ffn_w2_b"]
    out["L1_ffn_router_w"] = chunked(a["L1_ffn_router_w"].T)
    out["L2_ffn_W_gate"] = chunked(a["L2_ffn_W_gate"])
    out["L2_ffn_b2"] = a["L2_ffn_b2"]
    out["L2_ffn_W1"], out["L2_ffn_W2"] = per_expert(a["L2_ffn_W1"]), per_expert(a["L2_ffn_W2"])
    out["L2_ffn_b1"] = expert_columns(a["L2_ffn_b1"])

    p = "L1_xattn_"
    out[p + "Wq"] = chunked(pad_heads(a[p + "Wq"], 16, 32))
    out[p + "bq"] = column(pad_heads(a[p + "bq"][None], 16, 32)[0])
    out[p + "WkT"] = chunked(pad_heads(a[p + "Wk"], 16, 32).T)
    out[p + "Wv"] = halves_first(a[p + "Wv"].T, 16).T
    out[p + "bv"] = column(halves_first(a[p + "bv"][:, None], 16)[:, 0])
    out[p + "Wo"] = chunked(halves_first(a[p + "Wo"], 16))
    out[p + "bo"] = a[p + "bo"][None]
    p = "L3_xattn_"
    out[p + "Wq"] = chunked(pad_heads(a[p + "Wq"].T, 16, 32))
    out[p + "WkT"] = chunked(pad_heads(a[p + "Wkv"][:DIM].T, 16, 32).T)
    out[p + "Wv"] = halves_first(a[p + "Wkv"][DIM:], 16).T
    out[p + "bv"] = np.zeros((P, DC), np.float32)
    out[p + "Wo"] = chunked(halves_first(a[p + "Wo"].T, 16))
    p = "L2_xattn_"
    out[p + "Wq"], out[p + "bq"] = chunked(a[p + "Wq"]), column(a[p + "bq"])
    out[p + "WkT"] = chunked(a[p + "Wk"].T)
    out[p + "Wv"], out[p + "bv"] = a[p + "Wv"], a[p + "bv"][None]

    p = "L1_attn_"
    for n in ("norm_w", "norm_b", "b_dt"):
        out[p + n] = column(a[p + n])
    for n in ("W_in", "W_gate", "W_dt", "W_out", "A_log"):
        out[p + n] = chunked(a[p + n])
    out[p + "W_BC"] = chunked(np.concatenate([a[p + "W_B"], a[p + "W_C"]], axis=1))
    p = "L2_attn_"
    out[p + "key_w"], out[p + "key_b"] = chunked(a[p + "key_w"].T), column(a[p + "key_b"])
    out[p + "v_w"], out[p + "q_w"] = chunked(a[p + "vq_w"][:DIM].T), chunked(a[p + "vq_w"][DIM:].T)
    out[p + "out_w"], out[p + "out_b"] = chunked(a[p + "out_w"].T), a[p + "out_b"][None]
    p = "L3_attn_"
    out[p + "ln_gamma"], out[p + "ln_beta"] = column(a[p + "ln_gamma"]), column(a[p + "ln_beta"])
    out[p + "w_qkv"], out[p + "w_out"], out[p + "b_out"] = chunked(a[p + "w_qkv"]), chunked(a[p + "w_out"]), a[p + "b_out"][None]
    p = "L3_ffn_"
    for n in ("q_w", "k_w", "v_w", "o_w"):
        out[p + n] = chunked(a[p + n].T)
    for n in ("norm_w", "norm_b", "q_b", "k_b"):
        out[p + n] = column(a[p + n])
    for n in ("v_b", "o_b"):
        out[p + n] = a[p + n][None]
    return {k: np.ascontiguousarray(v) for k, v in out.items()}


def constants():
    import numpy as np

    f = np.float32
    out = {"ident": np.eye(P, dtype=f), "iota8": np.arange(EXPERTS, dtype=f)[None]}
    s = np.arange(SEQ)
    out["causal"] = np.tile((s[None, :] > s[:, None]).astype(f), (2, 1))
    r = np.arange(P)
    g = np.zeros((P, 16, P), f)
    for e in range(16):
        g[:, e, :] = (r[:, None] // 16 == r[None, :] // 16) & (r[None, :] % 16 == e)
    out["gather_rows"] = g
    inv = (1.0 / 10000.0 ** (np.arange(0, 64, 2, dtype=f) / f(64))).astype(f)
    ang = (np.arange(SEQ, dtype=f)[:, None] * inv[None, :]).astype(f)
    out["rope_cos"] = np.tile(np.cos(ang).T, (4, 1)).astype(f)
    out["rope_sin"] = np.tile(np.sin(ang).T, (4, 1)).astype(f)
    w = np.zeros((P, P), f)
    for h in (0, 64):
        for i in range(32):
            w[h + 32 + i, h + i] = -1
            w[h + i, h + 32 + i] = 1
    out["rope_swap"] = w
    width = DIM >> (s // 16)
    m = (np.arange(DIM)[:, None] < width[None, :]).astype(f)
    out["width_turned"] = m.reshape(DC, P, SEQ).transpose(1, 0, 2)
    out["width_rows"] = np.tile(m.T, (2, 1))
    return {k: np.ascontiguousarray(v) for k, v in out.items()}


def kernel(**inputs):
    import concourse.bacc as _bacc
    from concourse.bass_utils import run_bass_kernel_spmd as _run

    nc = _bacc.Bacc("TRN2", target_bir_lowering=False, num_devices=1)
    arrays, dram = {}, {}
    for name, a in {**layouts(inputs), **constants()}.items():
        arrays[f"in_{name}"] = a
        dram[name] = nc.dram_tensor(f"in_{name}", a.shape, F32, kind="ExternalInput").ap()
    for name, shape in (("context_norm", (BATCH, KEYS, CDIM)), ("context_q16", (BATCH, CDIM, 16 * SEQ)),
                        ("context_q1", (BATCH, CDIM, SEQ)), ("bc_turned", (32, TOKENS)), ("v_turned", (DIM, TOKENS))):
        dram[name] = nc.dram_tensor(name, shape, F32, kind="Internal").ap()
    dram["out"] = nc.dram_tensor("out_x", (TOKENS, DIM), F32, kind="ExternalOutput").ap()
    perceiver(nc, dram)
    r = _run(nc, [arrays], core_ids=[0])
    return r.results[0]["out_x"].reshape(BATCH, SEQ, DIM)
```

```python
from contextlib import ExitStack

import concourse.bass as bass
from concourse import mybir

LAYERS = (0, 1, 2, 3, 4, 5, 6, 7, 8, 9, 10, 11)

F32 = mybir.dt.float32
F32R = mybir.dt.float32r
U32 = mybir.dt.uint32
ALU = mybir.AluOpType
ACT = mybir.ActivationFunctionType
AX_X = mybir.AxisListType.X

P = 128
BATCH, SEQ, DIM = 16, 64, 256
TOKENS = BATCH * SEQ
TILES = TOKENS // P
HALVES = TOKENS // 512
DC = DIM // P
KEYS, CDIM = 1601, 128
KT = -(-KEYS // P)
KLAST = KEYS - (KT - 1) * P
EXPERTS = 8
EPS = 1e-5
BANKS = 8
LAM_INIT = 0.8 - 0.6 * 2.718281828459045 ** (-0.3 * 12)


class Count:

    def __init__(self, sem):
        self.sem = sem
        self.past = 0

    def at(self, n):
        return n + self.past

    def passed(self, n):
        self.past += n


class Core:

    def __init__(self, nc, dram, hold):
        self.nc, self.dram, self.hold = nc, dram, hold
        self.known = {}
        self.serial = 0
        self.PS = hold.enter_context(nc.psum_tensor("PS", [P, BANKS, 512], F32))
        self.X = self.sb(hold, "residual", [P, TILES, DIM])
        self.ident = self.sb(hold, "ident", [P, P])
        self.ones_row = self.sb(hold, "ones_row", [1, P])

    def sb(self, own, name, shape, dtype=F32):
        self.serial += 1
        return own.enter_context(self.nc.sbuf_tensor(f"{name}_{self.serial}", shape, dtype))

    def semaphores(self, name, n):
        return [self.semaphore(f"{name}_{u}") for u in range(n)]

    def semaphore(self, name):
        if name not in self.known:
            self.known[name] = Count(self.hold.enter_context(self.nc.semaphore(name)))
        return self.known[name]


def fetch(core, pairs):
    nc, landed = core.nc, core.semaphore("weights_landed")
    with nc.Block() as block:
        @block.sync
        def _(sp):
            for dst, src in pairs:
                sp.dma_start(dst, src).then_inc(landed.sem, 16)
    landed.passed(16 * len(pairs))


def weights(core, own, **shapes):
    room, pairs = {}, []
    for name, shape in shapes.items():
        t = core.sb(own, name, shape)
        src = core.dram[name]
        if src.shape[0] == 1 and shape[0] > 1:
            src = src[0].partition_broadcast(shape[0])
        room[name] = t
        pairs.append((t[:], src))
    fetch(core, pairs)
    return room


def wait_weights(core, eng):
    landed = core.semaphore("weights_landed")
    eng.wait_ge(landed.sem, landed.past)


def normalize(core, src, dst, gain=None, shift=None):
    nc = core.nc
    step, var_ready, dev_ready = core.semaphore("norm_step"), core.semaphore("variance_ready"), core.semaphore("deviation_ready")
    with ExitStack() as own:
        stats = core.sb(own, "stats", [P, TILES, 6])
        moments = core.sb(own, "moments", [P, TILES, 2])
        dev = core.sb(own, "deviation", [P, TILES])
        rstd = core.sb(own, "rstd", [P, TILES])
        with nc.Block() as block:
            @block.vector
            def _(dve):
                for t in range(TILES):
                    nc.vector.bn_stats(stats[:, t, :], src[:, t, :]).then_inc(step.sem, 1)
                dve.wait_ge(step.sem, step.at(TILES))
                for t in range(TILES):
                    nc.vector.bn_aggr(moments[:, t, :], stats[:, t, :]).then_inc(step.sem, 1)
                dve.wait_ge(step.sem, step.at(2 * TILES))
                nc.vector.tensor_scalar(dev[:], moments[:, :, 1], EPS, None, ALU.add).then_inc(var_ready.sem, 1)
                dve.wait_ge(dev_ready.sem, dev_ready.at(1))
                nc.vector.reciprocal(rstd[:], dev[:]).then_inc(step.sem, 1)
                dve.wait_ge(step.sem, step.at(2 * TILES + 1))
                for t in range(TILES):
                    nc.vector.tensor_scalar(dst[:, t, :], src[:, t, :], moments[:, t, 0:1], rstd[:, t:t + 1],
                                            ALU.subtract, ALU.mult).then_inc(step.sem, 1)
                if gain is not None:
                    wait_weights(core, dve)
                    dve.wait_ge(step.sem, step.at(3 * TILES + 1))
                    nc.vector.tensor_tensor(dst[:], dst[:], gain[:].unsqueeze(1).broadcast_to([P, TILES, DIM]),
                                            ALU.mult).then_inc(step.sem, 1)
                    dve.wait_ge(step.sem, step.at(3 * TILES + 2))
                    nc.vector.tensor_tensor(dst[:], dst[:], shift[:].unsqueeze(1).broadcast_to([P, TILES, DIM]),
                                            ALU.add).then_inc(step.sem, 1)

            @block.scalar
            def _(act):
                act.wait_ge(var_ready.sem, var_ready.at(1))
                nc.scalar.activation(dev[:], dev[:], ACT.Sqrt).then_inc(dev_ready.sem, 1)
    step.passed(3 * TILES + 1 + (2 if gain is not None else 0))
    var_ready.passed(1)
    dev_ready.passed(1)


def evacuate(core, block, fills, ready, by_act, by_dve, act_op, dve_op):
    @block.scalar
    def _(act):
        wait_weights(core, act)
        for f in range(0, fills, 2):
            act.wait_ge(ready.sem, ready.at(f + 1))
            act_op(f).then_inc(by_act.sem, 1)

    @block.vector
    def _(dve):
        wait_weights(core, dve)
        for f in range(1, fills, 2):
            dve.wait_ge(ready.sem, ready.at(f + 1))
            dve_op(f).then_inc(by_dve.sem, 1)


def wait_bank(pe, f, by_act, by_dve):
    if f >= BANKS:
        by = by_act if f % 2 == 0 else by_dve
        pe.wait_ge(by.sem, by.at((f - BANKS) // 2 + 1))


def turn(core, src, chunks, dst, gain=None, shift=None):
    nc, PS = core.nc, core.PS
    ready, by_act, by_dve = core.semaphore("fill_ready"), core.semaphore("fill_taken_act"), core.semaphore("fill_taken_dve")
    fills = chunks * HALVES

    def place(f):
        c, half = f // HALVES, f % HALVES
        return c, dst[:, c, half * 512:(half + 1) * 512], PS[:, f % BANKS, :]

    def act_op(f):
        c, out, bank = place(f)
        return nc.scalar.activation(out, bank, ACT.Identity,
                                    bias=0.0 if shift is None else shift[:, c:c + 1],
                                    scale=1.0 if gain is None else gain[:, c:c + 1])

    def dve_op(f):
        c, out, bank = place(f)
        if gain is None and shift is None:
            return nc.vector.tensor_copy(out, bank)
        return nc.vector.tensor_scalar(out, bank, 1.0 if gain is None else gain[:, c:c + 1],
                                       0.0 if shift is None else shift[:, c:c + 1], ALU.mult, ALU.add)

    with nc.Block() as block:
        @block.tensor
        def _(pe):
            for f in range(fills):
                c, half = f // HALVES, f % HALVES
                wait_bank(pe, f, by_act, by_dve)
                for j in range(4):
                    last = nc.tensor.transpose(PS[:, f % BANKS, j * P:(j + 1) * P],
                                               src[:, half * 4 + j, c * P:(c + 1) * P], core.ident[:])
                last.then_inc(ready.sem, 1)

        evacuate(core, block, fills, ready, by_act, by_dve, act_op, dve_op)
    ready.passed(fills)
    by_act.passed((fills + 1) // 2)
    by_dve.passed(fills // 2)


def linear_turned(core, src, w, dst, bias=None, func=ACT.Identity, rows=P):
    nc, PS = core.nc, core.PS
    ready, by_act, by_dve = core.semaphore("fill_ready"), core.semaphore("fill_taken_act"), core.semaphore("fill_taken_dve")
    kc = src.shape[1]
    fills = dst.shape[1] * HALVES
    plain = func == ACT.Identity

    def place(f):
        m, half = f // HALVES, f % HALVES
        return m, dst[0:rows, m, half * 512:(half + 1) * 512], PS[0:rows, f % BANKS, :]

    def act_op(f):
        m, out, bank = place(f)
        return nc.scalar.activation(out, bank, func, bias=0.0 if bias is None else bias[:, m:m + 1])

    def dve_op(f):
        m, out, bank = place(f)
        if bias is None:
            return nc.vector.tensor_copy(out, bank)
        return nc.vector.tensor_scalar(out, bank, bias[:, m:m + 1], None, ALU.add)

    with nc.Block() as block:
        @block.tensor
        def _(pe):
            wait_weights(core, pe)
            for f in range(fills):
                m, half = f // HALVES, f % HALVES
                if plain:
                    wait_bank(pe, f, by_act, by_dve)
                elif f >= BANKS:
                    pe.wait_ge(by_act.sem, by_act.at(f - BANKS + 1))
                for c in range(kc):
                    last = nc.tensor.matmul(PS[0:rows, f % BANKS, :], w[:, c, m * P:m * P + rows],
                                            src[:, c, half * 512:(half + 1) * 512],
                                            start=(c == 0), stop=(c == kc - 1))
                last.then_inc(ready.sem, 1)

        if plain:
            evacuate(core, block, fills, ready, by_act, by_dve, act_op, dve_op)
        else:
            @block.scalar
            def _(act):
                wait_weights(core, act)
                for f in range(fills):
                    act.wait_ge(ready.sem, ready.at(f + 1))
                    act_op(f).then_inc(by_act.sem, 1)
    ready.passed(fills)
    if plain:
        by_act.passed((fills + 1) // 2)
        by_dve.passed(fills // 2)
    else:
        by_act.passed(fills)


def linear_rows(core, src, w, dst, bias=None, base=None):
    nc, PS = core.nc, core.PS
    ready, taken = core.semaphore("rows_ready"), core.semaphore("rows_taken")
    kc, n_all = src.shape[1], dst.shape[2]
    cuts = [(n, min(512, n_all - n)) for n in range(0, n_all, 512)]
    fills = [(t, n, k) for t in range(TILES) for n, k in cuts]
    with nc.Block() as block:
        @block.tensor
        def _(pe):
            wait_weights(core, pe)
            for f, (t, n, k) in enumerate(fills):
                if f >= BANKS:
                    pe.wait_ge(taken.sem, taken.at(f - BANKS + 1))
                out = PS[:, f % BANKS, 0:k]
                if bias is not None:
                    nc.tensor.matmul(out, core.ones_row[0:1, :], bias[0:1, n:n + k], start=True, stop=False)
                for c in range(kc):
                    last = nc.tensor.matmul(out, src[:, c, t * P:(t + 1) * P], w[:, c, n:n + k],
                                            start=(c == 0 and bias is None), stop=(c == kc - 1))
                last.then_inc(ready.sem, 1)

        @block.vector
        def _(dve):
            for f, (t, n, k) in enumerate(fills):
                dve.wait_ge(ready.sem, ready.at(f + 1))
                if base is None:
                    ins = nc.vector.tensor_copy(dst[:, t, n:n + k], PS[:, f % BANKS, 0:k])
                else:
                    ins = nc.vector.tensor_tensor(dst[:, t, n:n + k], PS[:, f % BANKS, 0:k], base[:, t, n:n + k],
                                                  ALU.add)
                ins.then_inc(taken.sem, 1)
    ready.passed(len(fills))
    taken.passed(len(fills))


def vector_steps(core, steps):
    nc, step = core.nc, core.semaphore("vector_step")
    with nc.Block() as block:
        @block.vector
        def _(dve):
            wait_weights(core, dve)
            for n, run in enumerate(steps):
                if n:
                    dve.wait_ge(step.sem, step.at(n))
                run().then_inc(step.sem, 1)
    step.passed(len(steps))


def add(core, dst, a, b):
    vector_steps(core, [lambda: core.nc.vector.tensor_tensor(dst[:], a[:], b[:], ALU.add)])


def self_attention(core, qT, kT, V, O, heads, d, dv, scale, mask=None, minus_lam=None):
    nc, PS = core.nc, core.PS
    qc = qT.shape[1]
    groups = P // d
    per = heads // groups
    diff = minus_lam is not None
    og = groups // 2 if diff else groups
    squares = og * per
    tfills = squares // 4
    staged = core.semaphores("tile_staged", 2)
    s_ready, shifted = core.semaphore("scores_ready"), core.semaphore("scores_shifted")
    exps, probs = core.semaphore("exps_ready"), core.semaphore("squares_ready")
    turned, t_act = core.semaphore("squares_turned"), core.semaphore("squares_taken_act")
    o_ready, o_taken, step = core.semaphore("out_ready"), core.semaphore("out_taken"), core.semaphore("softmax_step")
    begun = core.semaphore("scores_begun")
    steps = 4 + (1 if diff else 0) + (1 if mask is not None else 0)

    def head_of(pos):
        g, k = pos // per, pos % per
        return k * og + g

    with ExitStack() as own:
        qs = core.sb(own, "q_tile", [P, 2, qc, P])
        ks = core.sb(own, "k_tile", [P, 2, qc, P])
        vs = core.sb(own, "v_tile", [P, 2, V.shape[2]])
        E = core.sb(own, "exps", [P, groups, per, SEQ])
        squares_sb = core.sb(own, "squares", [P, og, per, P])
        turned_sb = core.sb(own, "squares_turned", [P, squares, P])
        top = core.sb(own, "row_max", [P, groups, per])
        total = core.sb(own, "row_sum", [P, groups, per])
        warm = core.sb(own, "warm", [1, 1])
        S = PS[:, 0:groups, 0:per * SEQ].rearrange("p g (k t) -> p g k t", t=SEQ)
        flat = squares_sb[:].rearrange("p g k s -> p (g k) s")
        O_ps = PS[:, 6:8, :].rearrange("p b n -> p (b n)")
        wide = squares * dv
        with nc.Block() as block:
            @block.sync
            def _(sp):
                with sp.Fori(0, TILES // 2) as it:
                    for u in range(2):
                        i = it * 2 + u
                        sp.wait_ge(o_ready.sem, o_ready.at(i + 1))
                        sp.dma_start(qs[:, u], qT[:, :, bass.ds(i * P, P)]).then_inc(staged[u].sem, 16)
                        sp.dma_start(ks[:, u], kT[:, :, bass.ds(i * P, P)]).then_inc(staged[u].sem, 16)
                        sp.dma_start(vs[:, u], V[:, bass.ds(i, 1), :].rearrange("p a n -> p (a n)")).then_inc(staged[u].sem, 16)

            @block.tensor
            def _(pe):
                pe.sem_inc(o_ready.sem, 2)
                with pe.Fori(0, TILES // 2) as it:
                    for u in range(2):
                        i = it * 2 + u
                        pe.wait_ge(staged[u].sem, staged[u].at(it * 48 + 48))
                        pe.wait_ge(shifted.sem, shifted.at(i + 1))
                        if d == 64:
                            pe.sem_inc(begun.sem, 1)
                        for h in range(heads):
                            g, k = h % groups, h // groups
                            for b in range(2):
                                last = nc.tensor.matmul(PS[b * SEQ:(b + 1) * SEQ, g, k * SEQ:(k + 1) * SEQ],
                                                        qs[g * d:(g + 1) * d, u, k, b * SEQ:(b + 1) * SEQ],
                                                        ks[g * d:(g + 1) * d, u, k, b * SEQ:(b + 1) * SEQ],
                                                        start=True, stop=True)
                        last.then_inc(s_ready.sem, 1)
                        pe.wait_ge(probs.sem, probs.at(i * 2 + 2))
                        for j in range(tfills):
                            pe.wait_ge(t_act.sem, t_act.at(i * tfills + j + 1))
                            for m in range(4):
                                last = nc.tensor.transpose(PS[:, 4 + j % 2, m * P:(m + 1) * P], flat[:, 4 * j + m, :],
                                                           core.ident[:])
                            last.then_inc(turned.sem, 1)
                        pe.wait_ge(t_act.sem, t_act.at(i * tfills + tfills + 2))
                        pe.wait_ge(o_taken.sem, o_taken.at(i + 1))
                        for pos in range(squares):
                            h = head_of(pos)
                            last = nc.tensor.matmul(O_ps[:, h * dv:(h + 1) * dv], turned_sb[:, pos, :],
                                                    vs[:, u, h * dv:(h + 1) * dv], start=True, stop=True)
                        last.then_inc(o_ready.sem, 1)

            @block.vector
            def _(dve):
                nc.vector.memset(squares_sb[:], 0.0).then_inc(step.sem, 1)
                dve.wait_ge(step.sem, step.at(1))
                dve.sem_inc(shifted.sem, 1)
                dve.sem_inc(o_taken.sem, 1)
                with dve.Fori(0, TILES) as i:
                    done = [0]

                    def then(ins):
                        done[0] += 1
                        ins.then_inc(step.sem, 1)
                        dve.wait_ge(step.sem, step.at(i * steps + 1 + done[0]))

                    dve.wait_ge(s_ready.sem, s_ready.at(i + 1))
                    then(nc.vector.tensor_reduce(top[:], S, AX_X, ALU.max))
                    nc.vector.tensor_tensor(E[:], S, top[:].unsqueeze(3).broadcast_to([P, groups, per, SEQ]),
                                            ALU.subtract).then_inc(shifted.sem, 1)
                    dve.wait_ge(exps.sem, exps.at(i + 1))
                    then(nc.vector.tensor_reduce(total[:], E[:], AX_X, ALU.add))
                    then(nc.vector.reciprocal(total[:], total[:]))
                    if diff:
                        odd = total[:, 1::2, :]
                        then(nc.vector.tensor_scalar(odd, odd, minus_lam, None, ALU.mult))
                    then(nc.vector.tensor_tensor(E[:], E[:], total[:].unsqueeze(3).broadcast_to([P, groups, per, SEQ]),
                                                 ALU.mult))
                    if mask is not None:
                        Ef = E[:].rearrange("p g k t -> p (g k) t")
                        then(nc.vector.tensor_tensor(Ef, Ef, mask[:].unsqueeze(1).broadcast_to([P, heads, SEQ]), ALU.mult))
                    for b in range(2):
                        rows = slice(b * SEQ, (b + 1) * SEQ)
                        out = squares_sb[rows, :, :, b * SEQ:(b + 1) * SEQ]
                        if diff:
                            ins = nc.vector.tensor_tensor(out, E[rows, 0::2], E[rows, 1::2], ALU.add)
                        else:
                            ins = nc.vector.tensor_copy(out, E[rows])
                        ins.then_inc(probs.sem, 1)
                    dve.wait_ge(o_ready.sem, o_ready.at(i + 3))
                    nc.vector.tensor_copy(O[:, bass.ds(i, 1), :].rearrange("p a n -> p (a n)"),
                                          O_ps[:, 0:wide]).then_inc(o_taken.sem, 1)

            @block.scalar
            def _(act):
                nc.scalar.activation(warm[:], core.ident[0:1, 0:1], ACT.Exp)
                act.sem_inc(t_act.sem, 2)
                with act.Fori(0, TILES) as i:
                    act.wait_ge(shifted.sem, shifted.at(i + 2))
                    nc.scalar.activation(E[:], E[:], ACT.Exp, scale=scale).then_inc(exps.sem, 1)
                    for j in range(tfills):
                        act.wait_ge(turned.sem, turned.at(i * tfills + j + 1))
                        nc.scalar.copy(turned_sb[:, 4 * j:4 * j + 4, :].rearrange("p m s -> p (m s)"),
                                       PS[:, 4 + j % 2, :]).then_inc(t_act.sem, 1)
    for s in staged:
        s.passed(48 * TILES // 2)
    for s in (s_ready, exps):
        s.passed(TILES)
    o_ready.passed(TILES + 2)
    shifted.passed(TILES + 1)
    o_taken.passed(TILES + 1)
    probs.passed(2 * TILES)
    if d == 64:
        begun.passed(TILES)
    turned.passed(tfills * TILES)
    t_act.passed(tfills * TILES + 2)
    step.passed(steps * TILES + 1)


def store(core, pairs):
    nc, stored = core.nc, core.semaphore("stored")
    with nc.Block() as block:
        @block.sync
        def _(sp):
            for dst, src in pairs:
                sp.dma_start(dst, src).then_inc(stored.sem, 16)
            sp.wait_ge(stored.sem, stored.at(16 * len(pairs)))
    stored.passed(16 * len(pairs))


PRODUCTS = ((0, 0), (0, 1), (1, 0))


def context_attention(core, qT, queries, q_fills, q_cols, gain, context, wv_of, sums, pairs, heads_in, per_group, unroll,
                      y_bufs, scale, d_out):
    nc, PS = core.nc, core.PS
    y_landed, q_staged = core.semaphores("context_landed", y_bufs), core.semaphores("tile_staged", 2)
    s_ready, m_ready, e_done = core.semaphore("scores_ready"), core.semaphore("max_ready"), core.semaphore("exps_ready")
    turned, t_act, t_dve = core.semaphore("squares_turned"), core.semaphore("lead_taken"), core.semaphore("rest_taken")
    y_lead, y_split, y_begun = core.semaphore("context_lead"), core.semaphore("context_split"), core.semaphore("split_begun")
    o_ready, o_taken = core.semaphore("weighted_ready"), core.semaphore("weighted_taken")
    f_ready, f_taken, step = core.semaphore("out_ready"), core.semaphore("out_taken"), core.semaphore("softmax_step")
    sum_done, inv_done = core.semaphore("row_sum_ready"), core.semaphore("row_scale_ready")
    zeroed = core.semaphore("zero_ready")
    turns = BATCH // unroll
    steps_all = BATCH * pairs
    per_turn = unroll * pairs
    groups_all = steps_all // per_group
    groups_batch = pairs // per_group
    groups = unroll * groups_batch
    wide = per_group * P
    even = KEYS + KEYS % 2
    halves = (slice(0, 1024), slice(1024, KEYS))
    ahead = q_fills + 4
    per_step = ahead // pairs
    parts = [list(range(KT))[KT * n // per_group:KT * (n + 1) // per_group] for n in range(per_group)]
    S = PS[:, 0:4, :].rearrange("p b n -> p (b n)")
    O_ps = PS[:, 7, 0:wide]
    F_ps = PS[:, 3, P:P + per_group * heads_in * d_out].rearrange("p (g a d) -> p g a d", g=per_group, a=heads_in)
    q_wide = q_cols // q_fills
    blocks = max(1, q_wide // SEQ)

    def keys_in(k):
        return KLAST if k == KT - 1 else P

    with ExitStack() as own:
        y = core.sb(own, "context_rows", [P, y_bufs, KT, CDIM])
        yp = [core.sb(own, "context_part", [P, 2, KT, CDIM], F32R) for _ in range(2)]
        yT = [core.sb(own, "context_turned", [P, 2, even], F32R) for _ in range(2)]
        q_tile = core.sb(own, "q_tile", [P, 2, qT.shape[1], blocks * SEQ])
        qs = [core.sb(own, "queries", [P, 2, pairs * P], F32R) for _ in range(2)]
        probs = core.sb(own, "probs", [P, 2, KEYS])
        probsT = [core.sb(own, "probs_turned", [P, 2, KT, wide], F32R) for _ in range(2)]
        OT = core.sb(own, "weighted", [P, 2, wide])
        top = core.sb(own, "row_max", [P, 2, 2])
        bias = core.sb(own, "minus_max", [P, 2])
        total = core.sb(own, "row_sum", [P, per_turn, 2])
        warm = core.sb(own, "warm", [1, 1])
        inverse = core.sb(own, "row_scale", [P, 4, per_group])

        def brings(it, local):
            return not (isinstance(it, int) and it == turns - 1 and local >= per_turn - pairs)

        def fill_number(it, local, at):
            n = it * per_turn + local
            if isinstance(n, int) and n == 0:
                return ahead + at - 2
            missing = max(0, local - (per_turn - pairs)) if isinstance(it, int) and it == turns - 1 else 0
            return n * (4 + per_step) + (ahead - 4 - missing * per_step + at)

        def turn_number(it, local, j):
            return fill_number(it, local, j if j < 2 or not brings(it, local) else j + per_step)

        def bring_number(it, local, x):
            return fill_number(it, local, 2 + x)

        def parity(it, local, at):
            return fill_number(it if isinstance(it, int) else 2, local, at) % 2

        def turn_bank(it, local, j):
            if per_step == 1:
                return 4 + j % 2
            return 4 + parity(it, local, j if j < 2 or not brings(it, local) else j + per_step)

        def bring_bank(it, local, x):
            return 6 if per_step == 1 else 4 + parity(it, local, 2 + x)

        def wait_fill(pe, number, between=1):
            pe.wait_ge(t_dve.sem, t_dve.at(number + 2 - between))

        def pe_bring(pe, e, b, number, bank):
            between = 2 if bank == 6 else 1
            if e < q_fills:
                if e == 0:
                    pe.wait_ge(q_staged[b[1] % 2].sem, q_staged[b[1] % 2].at(16 * blocks * (b[0] * (unroll // 2) + b[1] // 2 + 1)))
                wait_fill(pe, number, between)
                for cols, w, moving, start, stop in queries(e, q_tile[:, b[1] % 2]):
                    last = nc.tensor.matmul(PS[:, bank, cols], w, moving, start=start, stop=stop)
            else:
                j = e - q_fills
                slot = landed_slot(b)
                if j == 0:
                    pe.wait_ge(y_landed[slot].sem, y_landed[slot].at(landed_count(b)))
                wait_fill(pe, number, between)
                for k in range(4 * j, min(4 * j + 4, KT)):
                    kk = keys_in(k)
                    last = nc.tensor.transpose(PS[:, bank, (k - 4 * j) * P:(k - 4 * j) * P + kk], y[0:kk, slot, k, :],
                                               core.ident[0:kk, 0:kk])
            last.then_inc(turned.sem, 1)

        def landed_slot(b):
            return b[1] % y_bufs

        def landed_count(b):
            it, u = b
            return 32 * (it * (unroll // y_bufs) + u // y_bufs + 1)

        def brought(e, b, bank):
            v = b[1] % 2
            if e < q_fills:
                at = slice(e * q_wide, (e + 1) * q_wide)
                return [q[:, v, at] for q in qs], PS[:, bank, 0:q_wide], gain
            j = e - q_fills
            cols = min(512, KEYS - 512 * j)
            return [t[:, v, 512 * j:512 * j + cols] for t in yT], PS[:, bank, 0:cols], None

        def act_bring(act, e, b, number, bank):
            (lead, _), fill, factor = brought(e, b, bank)
            act.wait_ge(turned.sem, turned.at(number + 1))
            if factor is None:
                nc.scalar.copy(lead, fill).then_inc(t_act.sem, 1)
            else:
                nc.scalar.activation(lead, fill, ACT.Identity, scale=factor[:, 0:1]).then_inc(t_act.sem, 1)

        def dve_bring(dve, e, b, number, bank):
            (lead, rest), fill, factor = brought(e, b, bank)
            dve.wait_ge(t_act.sem, t_act.at(number + 1))
            if factor is None:
                nc.vector.tensor_tensor(rest, fill, lead, ALU.subtract).then_inc(t_dve.sem, 1)
            else:
                nc.vector.scalar_tensor_tensor(rest, fill, factor[:, 0:1], lead, ALU.mult,
                                               ALU.subtract).then_inc(t_dve.sem, 1)

        def bring_step(one, eng, it, local):
            if brings(it, local):
                b = (it, local // pairs + 1)
                for x in range(per_step):
                    one(eng, (local % pairs) * per_step + x, b, bring_number(it, local, x), bring_bank(it, local, x))

        def bring_first(one, eng):
            for e in range(ahead):
                one(eng, e, (0, 0), e, 4 + e % 2)

        def out_due(local, first):
            return (local - 2) % per_group == 0 and alive(local, first, 2 * per_group + 2)

        def pe_scores(pe, it, local, first):
            n, p, v = it * per_turn + local, local % pairs, (local // pairs) % 2
            if p == 0:
                brought_all = ahead if first and local == 0 else bring_number(it, local - 1, per_step - 1) + 1
                pe.wait_ge(t_dve.sem, t_dve.at(brought_all + 2))
            for half in range(2):
                if not (first and local == 0):
                    pe.wait_ge(e_done.sem, e_done.at(n * 2 - 1 + half))
                for j in (2 * half, 2 * half + 1):
                    if j == 3 and out_due(local, first):
                        pe_out(pe, it, local)
                    cols = min(512, even - 512 * j)
                    for m, (a, b) in enumerate(PRODUCTS):
                        last = nc.tensor.matmul(S[:, 512 * j:512 * j + cols], qs[a][:, v, p * P:(p + 1) * P],
                                                yT[b][:, v, 512 * j:512 * j + cols], start=(m == 0), stop=(m == 2))
                last.then_inc(s_ready.sem, 1)

        def pe_turn(pe, it, local, half):
            pe.wait_ge(e_done.sem, e_done.at((it * per_turn + local) * 2 - 1 + half))
            for j in (2 * half, 2 * half + 1):
                wait_fill(pe, turn_number(it, local, j), 2 if per_step == 1 and half == 1 and brings(it, local) else 1)
                for k in range(4 * j, min(4 * j + 4, KT)):
                    kk = keys_in(k)
                    last = nc.tensor.transpose(PS[0:kk, turn_bank(it, local, j), (k - 4 * j) * P:(k - 4 * j + 1) * P],
                                               probs[:, (local - 1) % 2, k * P:k * P + kk], core.ident[:])
                last.then_inc(turned.sem, 1)

        def pe_weighted(pe, it, local):
            part = (local - 1) % per_group
            back = local - 1 - part - per_group
            u = (back // pairs) % 2
            par = (back // per_group) % 2
            if part == 0:
                pe.wait_ge(t_dve.sem, t_dve.at(turn_number(it, local - 1, 3) + 3))
                pe.wait_ge(y_split.sem, y_split.at(it * unroll + back // pairs + 1))
                pe.wait_ge(o_taken.sem, o_taken.at(it * groups + back // per_group + 1))
            for k in parts[part]:
                kk = keys_in(k)
                for m, (a, b) in enumerate(PRODUCTS):
                    last = nc.tensor.matmul(O_ps, yp[a][0:kk, u, k, :], probsT[b][0:kk, par, k, :],
                                            start=(k == 0 and m == 0), stop=(k == KT - 1 and m == 2))
            if part == per_group - 1:
                last.then_inc(o_ready.sem, 1)

        def pe_out(pe, it, local):
            back = local - 2 - 2 * per_group
            g = it * groups + back // per_group
            par = (back // per_group) % 2
            pe.wait_ge(o_taken.sem, o_taken.at(g + 2))
            pe.wait_ge(f_taken.sem, f_taken.at(g * heads_in + heads_in))
            for m in range(per_group):
                last = nc.tensor.matmul(F_ps[:, m], OT[:, par, m * P:(m + 1) * P], wv_of((back + m) % pairs),
                                        start=True, stop=True)
            last.then_inc(f_ready.sem, 1)

        def turned_part(part, it, local, j):
            k0, k1 = 4 * j, min(4 * j + 4, KT)
            kk = keys_in(k0)
            m = (local - 1) % per_group
            return (probsT[part][0:kk, ((local - 1) // per_group) % 2, k0:k1, m * P:(m + 1) * P],
                    PS[0:kk, turn_bank(it, local, j), 0:(k1 - k0) * P].rearrange("p (k r) -> p k r", r=P))

        def act_turn(act, it, local, half):
            for j in (2 * half, 2 * half + 1):
                out, bank = turned_part(0, it, local, j)
                act.wait_ge(turned.sem, turned.at(turn_number(it, local, j) + 1))
                nc.scalar.copy(out, bank).then_inc(t_act.sem, 1)

        def act_exp(act, it, local, half):
            if half == 0:
                act.wait_ge(m_ready.sem, m_ready.at(it * per_turn + local + 1))
            cols = halves[half]
            nc.scalar.activation(probs[:, local % 2, cols], S[:, cols], ACT.Exp, bias=bias[:, local % 2:local % 2 + 1],
                                 scale=scale, accum_out=total[:, local, half:half + 1]).then_inc(e_done.sem, 1)

        def dve_turn(dve, it, local, half):
            for j in (2 * half, 2 * half + 1):
                lead, _ = turned_part(0, it, local, j)
                rest, bank = turned_part(1, it, local, j)
                dve.wait_ge(t_act.sem, t_act.at(turn_number(it, local, j) + 1))
                nc.vector.tensor_tensor(rest, bank, lead, ALU.subtract).then_inc(t_dve.sem, 1)

        def dve_weighted(dve, it, local):
            back = local - 2 * per_group
            g = it * groups + back // per_group
            slot = back % per_turn
            inv = inverse[:, (back // per_group) % 4, :]
            nc.vector.tensor_reduce(inv, total[:, slot:slot + per_group, :], AX_X, ALU.add).then_inc(sum_done.sem, 1)
            dve.wait_ge(sum_done.sem, sum_done.at(g + 1))
            nc.vector.reciprocal(inv, inv).then_inc(inv_done.sem, 1)
            dve.wait_ge(o_ready.sem, o_ready.at(g + 1))
            nc.vector.tensor_copy(OT[:, (back // per_group) % 2, :], O_ps).then_inc(o_taken.sem, 1)

        def dve_max(dve, it, local, first):
            n, q = it * per_turn + local, local % 2
            for half, cols in enumerate(halves):
                dve.wait_ge(s_ready.sem, s_ready.at(n * 2 + half + 1))
                nc.vector.tensor_reduce(top[:, q, half:half + 1], S[:, cols], AX_X, ALU.max).then_inc(step.sem, 1)
            if out_due(local, first):
                dve_out(dve, it, local)
            dve.wait_ge(step.sem, step.at(n * 2 + 2))
            nc.vector.tensor_scalar(bias[:, q:q + 1], top[:, q, 0:1], top[:, q, 1:2], -scale, ALU.max,
                                    ALU.mult).then_inc(m_ready.sem, 1)

        def dve_out(dve, it, local):
            back = local - 2 - 2 * per_group
            g = it * groups + back // per_group
            pair0 = back % pairs
            b = it * unroll + back // pairs
            inv = inverse[:, (back // per_group) % 4, :]
            dve.wait_ge(inv_done.sem, inv_done.at(g + 1))
            dve.wait_ge(f_ready.sem, f_ready.at(g + 1))
            for a in range(heads_in):
                r = slice(a * SEQ, (a + 1) * SEQ)
                nc.vector.tensor_tensor(sums[r, bass.ds(b, 1), pair0:pair0 + per_group, :].rearrange("p x g d -> p (x g) d"),
                                        F_ps[r, :, a, :], inv[r, :].unsqueeze(2).broadcast_to([SEQ, per_group, d_out]),
                                        ALU.mult).then_inc(f_taken.sem, 1)

        def alive(local, first, back):
            return not first or local >= back

        def turns_pair(local, first, tail):
            return alive(local, first, 1) and not (tail and local > per_turn)

        def pe_step(pe, it, local, first, tail):
            if not tail:
                pe_scores(pe, it, local, first)
            if turns_pair(local, first, tail):
                pe_turn(pe, it, local, 0)
            if tail and out_due(local, first):
                pe.wait_ge(e_done.sem, e_done.at(2 * steps_all))
                pe_out(pe, it, local)
            if alive(local, first, per_group + 1) and not (tail and local > per_turn + per_group):
                pe_weighted(pe, it, local)
            if not tail:
                bring_step(pe_bring, pe, it, local)
            if turns_pair(local, first, tail):
                pe_turn(pe, it, local, 1)

        def act_step(act, it, local, first, tail):
            if turns_pair(local, first, tail):
                act_turn(act, it, local, 0)
            if not tail:
                act_exp(act, it, local, 0)
                if per_step > 1:
                    act_exp(act, it, local, 1)
                bring_step(act_bring, act, it, local)
                if per_step == 1:
                    act_exp(act, it, local, 1)
            if turns_pair(local, first, tail):
                act_turn(act, it, local, 1)

        def dve_step(dve, it, local, first, tail):
            if not tail:
                dve_max(dve, it, local, first)
            if tail and out_due(local, first):
                dve_out(dve, it, local)
            if turns_pair(local, first, tail):
                dve_turn(dve, it, local, 0)
            if not tail:
                bring_step(dve_bring, dve, it, local)
            if turns_pair(local, first, tail):
                dve_turn(dve, it, local, 1)
            if local % per_group == 0 and alive(local, first, 2 * per_group) and not (tail and local > per_turn + per_group):
                dve_weighted(dve, it, local)

        def run(eng, one, bring):
            bring_first(bring, eng)
            for local in range(per_turn):
                one(eng, 0, local, True, False)
            with eng.Fori(1, turns - 1) as it:
                for local in range(per_turn):
                    one(eng, it, local, False, False)
            for local in range(per_turn + per_group + 3):
                one(eng, turns - 1, local, False, local >= per_turn)

        def load(sp, b, slot):
            sp.dma_start(y[:, slot, 0:KT - 1, :], context[bass.ds(b, 1), 0:(KT - 1) * P, :].rearrange(
                "a (k p) c -> p (a k) c", p=P)).then_inc(y_landed[slot].sem, 16)
            sp.dma_start(y[0:KLAST, slot, KT - 1, :], context[bass.ds(b, 1), (KT - 1) * P:KEYS, :].rearrange(
                "a p c -> p (a c)")).then_inc(y_landed[slot].sem, 16)

        def stage(sp, b, slot):
            for i in range(blocks):
                r = slice(i * P // blocks, (i + 1) * P // blocks)
                sp.dma_start(q_tile[r, slot, :, i * SEQ:(i + 1) * SEQ],
                             qT[r, :, bass.ds(b * SEQ, SEQ)]).then_inc(q_staged[slot].sem, 16)

        def reload(sp, b, u):
            before, q_next = b - y_bufs, b + 2 - y_bufs
            first = isinstance(before, int) and before == 0
            sp.wait_ge(turned.sem, turned.at(ahead if first else before * (pairs * (4 + per_step)) + (ahead - 4)))
            if not (isinstance(b, int) and q_next == BATCH):
                stage(sp, q_next, (u + 2 - y_bufs) % 2)
            sp.wait_ge(y_split.sem, y_split.at(b - y_bufs + 1))
            load(sp, b, u % y_bufs)

        def split_rows(pool, it, u):
            b, slot, v = (it, u), landed_slot((it, u)), u % 2
            pool.wait_ge(y_landed[slot].sem, y_landed[slot].at(landed_count(b)))
            if not (isinstance(it, int) and it == 0 and u < 2):
                pool.wait_ge(o_ready.sem, o_ready.at((it * unroll + u - 1) * groups_batch))
            pool.sem_inc(y_begun.sem, 1)
            cuts = ((slice(0, P), slice(0, KT - 1)), (slice(0, KLAST), slice(KT - 1, KT)))
            for r, k in cuts:
                nc.gpsimd.tensor_copy(yp[0][r, v, k, :], y[r, slot, k, :]).then_inc(y_lead.sem, 1)
            pool.wait_ge(y_lead.sem, y_lead.at((it * unroll + u) * 2 + 2))
            for n, (r, k) in enumerate(cuts):
                ins = nc.gpsimd.tensor_tensor(yp[1][r, v, k, :], y[r, slot, k, :], yp[0][r, v, k, :], ALU.subtract)
            ins.then_inc(y_split.sem, 1)

        with nc.Block() as block:
            @block.sync
            def _(sp):
                for b in range(y_bufs):
                    load(sp, b, b)
                sp.wait_ge(zeroed.sem, zeroed.at(1))
                for b in range(2):
                    stage(sp, b, b)
                for b in range(y_bufs, 4):
                    reload(sp, b, b % 2)
                with sp.Fori(2, BATCH // 2 - 1) as r:
                    for u in range(2):
                        reload(sp, r * 2 + u, u)
                for b in range(BATCH - 2, BATCH):
                    reload(sp, b, b % 2)

            @block.gpsimd
            def _(pool):
                nc.gpsimd.memset(q_tile[:], 0.0).then_inc(zeroed.sem, 1)
                for u in range(unroll):
                    split_rows(pool, 0, u)
                with pool.Fori(1, turns) as it:
                    for u in range(unroll):
                        split_rows(pool, it, u)

            @block.tensor
            def _(pe):
                wait_weights(core, pe)
                run(pe, pe_step, pe_bring)

            @block.scalar
            def _(act):
                wait_weights(core, act)
                nc.scalar.activation(warm[:], core.ident[0:1, 0:1], ACT.Exp)
                run(act, act_step, act_bring)

            @block.vector
            def _(dve):
                wait_weights(core, dve)
                for t in yT:
                    nc.vector.memset(t[:, :, KEYS:even].bitcast(F32), 0.0)
                if q_cols < pairs * P:
                    for q in qs:
                        nc.vector.memset(q[:, :, q_cols:].bitcast(F32), 0.0)
                dve.sem_inc(t_dve.sem, 2)
                dve.sem_inc(o_taken.sem, 1)
                dve.sem_inc(f_taken.sem, heads_in)
                run(dve, dve_step, dve_bring)
    for s in y_landed:
        s.passed(32 * BATCH // y_bufs)
    for s in q_staged:
        s.passed(16 * blocks * BATCH // 2)
    zeroed.passed(1)
    m_ready.passed(steps_all)
    for n in (s_ready, e_done, step):
        n.passed(2 * steps_all)
    y_lead.passed(2 * BATCH)
    y_split.passed(BATCH)
    y_begun.passed(BATCH)
    fills = 4 * steps_all + ahead * BATCH
    turned.passed(fills)
    t_act.passed(fills)
    t_dve.passed(fills + 2)
    o_ready.passed(groups_all)
    o_taken.passed(groups_all + 1)
    f_ready.passed(groups_all)
    f_taken.passed(groups_all * heads_in + heads_in)
    sum_done.passed(groups_all)
    inv_done.passed(groups_all)


def head_queries(wkT):
    return lambda j, q: [(slice(0, 4 * SEQ), wkT[:, j, :], q[:, j, :], True, True)]


def turn_sums(core, sums, pairs, d, dst, shift):
    nc, PS = core.nc, core.PS
    ready, by_act, by_dve = core.semaphore("fill_ready"), core.semaphore("fill_taken_act"), core.semaphore("fill_taken_dve")
    chunks = pairs * d // P
    flat = sums[:].rearrange("p b h d -> p b (h d)")
    fills = chunks * (BATCH // 4)

    def place(f, half):
        c, b4 = f // (BATCH // 4), f % (BATCH // 4)
        k = half * chunks + c
        out = dst[:, k, b4 * 4 * SEQ:(b4 + 1) * 4 * SEQ].rearrange("p (b s) -> p b s", s=SEQ)
        bank = PS[:, f % BANKS, :].rearrange("p (b a s) -> p b a s", b=4, a=2)[:, :, half, :]
        return out, bank, shift[:, k:k + 1]

    with nc.Block() as block:
        @block.tensor
        def _(pe):
            for f in range(fills):
                c, b4 = f // (BATCH // 4), f % (BATCH // 4)
                if f >= BANKS:
                    by = by_act if f % 2 == 0 else by_dve
                    pe.wait_ge(by.sem, by.at(2 * ((f - BANKS) // 2 + 1)))
                for j in range(4):
                    last = nc.tensor.transpose(PS[:, f % BANKS, j * P:(j + 1) * P],
                                               flat[:, b4 * 4 + j, c * P:(c + 1) * P], core.ident[:])
                last.then_inc(ready.sem, 1)

        @block.scalar
        def _(act):
            wait_weights(core, act)
            for f in range(0, fills, 2):
                act.wait_ge(ready.sem, ready.at(f + 1))
                for half in range(2):
                    out, bank, bias = place(f, half)
                    nc.scalar.activation(out, bank, ACT.Identity, bias=bias).then_inc(by_act.sem, 1)

        @block.vector
        def _(dve):
            wait_weights(core, dve)
            for f in range(1, fills, 2):
                dve.wait_ge(ready.sem, ready.at(f + 1))
                for half in range(2):
                    out, bank, bias = place(f, half)
                    nc.vector.tensor_scalar(out, bank, bias, None, ALU.add).then_inc(by_dve.sem, 1)
    for s in (ready, by_act, by_dve):
        s.passed(fills)


def normalize_context(core):
    nc = core.nc
    src, dst = core.dram["ctx_512"], core.dram["context_norm"]
    landed, stored = core.semaphores("context_landed", 2), core.semaphores("context_stored", 2)
    m_step, p_step = core.semaphore("norm_step"), core.semaphore("pool_step")
    centred, squared, var_ready, dev_ready, scaled = (core.semaphore("centred"), core.semaphore("squared"), core.semaphore("variance_ready"),
                                                      core.semaphore("deviation_ready"), core.semaphore("context_scaled"))
    per = BATCH * KEYS // P
    left = BATCH * KEYS - per * P
    cut = 25
    cuts = per // cut
    flat_in = src.rearrange("b k c -> (b k) c")
    flat_out = dst.rearrange("b k c -> (b k) c")
    body_in = flat_in[0:per * P, :].rearrange("(p r) c -> p r c", p=P)
    body_out = flat_out[0:per * P, :].rearrange("(p r) c -> p r c", p=P)
    with ExitStack() as own:
        rows = core.sb(own, "rows", [P, 2, cut, CDIM])
        sq = core.sb(own, "squares", [P, 2, cut, CDIM])
        mean = core.sb(own, "mean", [P, 2, cut])
        var = core.sb(own, "variance", [P, 2, cut])

        def moves(n):
            if n < cuts:
                return body_in[:, n * cut:(n + 1) * cut, :], body_out[:, n * cut:(n + 1) * cut, :], P, cut
            return flat_in[per * P:, :].unsqueeze(1), flat_out[per * P:, :].unsqueeze(1), left, 1

        with nc.Block() as block:
            @block.sync
            def _(sp):
                for n in range(cuts + 1):
                    a, _, p, r = moves(n)
                    if n >= 2:
                        sp.wait_ge(stored[n % 2].sem, stored[n % 2].at(16 * (n // 2)))
                    sp.dma_start(rows[0:p, n % 2, 0:r, :], a).then_inc(landed[n % 2].sem, 16)
                    if n >= 1:
                        _, b, p, r = moves(n - 1)
                        sp.wait_ge(scaled.sem, scaled.at(n))
                        sp.dma_start(b, rows[0:p, (n - 1) % 2, 0:r, :]).then_inc(stored[(n - 1) % 2].sem, 16)
                _, b, p, r = moves(cuts)
                sp.wait_ge(scaled.sem, scaled.at(cuts + 1))
                sp.dma_start(b, rows[0:p, cuts % 2, 0:r, :]).then_inc(stored[cuts % 2].sem, 16)
                for q in range(2):
                    sp.wait_ge(stored[q].sem, stored[q].at(16 * ((cuts + 2 - q) // 2)))

            @block.vector
            def _(dve):
                for n in range(cuts + 1):
                    _, _, p, r = moves(n)
                    x, q = rows[0:p, n % 2, 0:r, :], n % 2
                    m, v = mean[0:p, q, 0:r], var[0:p, q, 0:r]
                    dve.wait_ge(landed[q].sem, landed[q].at(16 * (n // 2) + 16))
                    nc.vector.tensor_reduce(m, x, AX_X, ALU.add).then_inc(m_step.sem, 1)
                    dve.wait_ge(m_step.sem, m_step.at(3 * n + 1))
                    nc.vector.tensor_scalar(m, m, 1.0 / CDIM, None, ALU.mult).then_inc(m_step.sem, 1)
                    dve.wait_ge(m_step.sem, m_step.at(3 * n + 2))
                    nc.vector.tensor_tensor(x, x, m.unsqueeze(2).broadcast_to([p, r, CDIM]), ALU.subtract).then_inc(centred.sem, 1)
                    dve.wait_ge(squared.sem, squared.at(n + 1))
                    nc.vector.tensor_reduce(v, sq[0:p, q, 0:r, :], AX_X, ALU.add).then_inc(m_step.sem, 1)
                    dve.wait_ge(m_step.sem, m_step.at(3 * n + 3))
                    nc.vector.tensor_scalar(v, v, 1.0 / CDIM, EPS, ALU.mult, ALU.add).then_inc(var_ready.sem, 1)
                    dve.wait_ge(dev_ready.sem, dev_ready.at(n + 1))
                    nc.vector.reciprocal(v, v).then_inc(p_step.sem, 1)

            @block.scalar
            def _(act):
                for n in range(cuts + 1):
                    _, _, p, r = moves(n)
                    act.wait_ge(centred.sem, centred.at(n + 1))
                    nc.scalar.activation(sq[0:p, n % 2, 0:r, :], rows[0:p, n % 2, 0:r, :], ACT.Square).then_inc(squared.sem, 1)
                    act.wait_ge(var_ready.sem, var_ready.at(n + 1))
                    v = var[0:p, n % 2, 0:r]
                    nc.scalar.activation(v, v, ACT.Sqrt).then_inc(dev_ready.sem, 1)

            @block.gpsimd
            def _(pool):
                for n in range(cuts + 1):
                    _, _, p, r = moves(n)
                    x = rows[0:p, n % 2, 0:r, :]
                    pool.wait_ge(p_step.sem, p_step.at(n + 1))
                    nc.gpsimd.tensor_tensor(x, x, var[0:p, n % 2, 0:r].unsqueeze(2).broadcast_to([p, r, CDIM]),
                                            ALU.mult).then_inc(scaled.sem, 1)
    k = cuts + 1
    for q in range(2):
        landed[q].passed(16 * ((k + 1 - q) // 2))
        stored[q].passed(16 * ((k + 1 - q) // 2))
    m_step.passed(3 * k)
    for s in (p_step, centred, squared, var_ready, dev_ready, scaled):
        s.passed(k)


def mlp(core, pre, rows):
    with ExitStack() as own:
        shapes = {"ln3_g": [P, DC], "ln3_b": [P, DC], "li2_w": [P, DC, 4 * DIM], "li2_b": [P, 4 * DC],
                  "li3_w": [P, 4 * DC, DIM], "li3_b": [1, DIM]}
        w = {k[len(pre):]: t for k, t in weights(core, own, **{pre + k: s for k, s in shapes.items()}).items()}
        hat = core.sb(own, "hat", [P, TILES, DIM])
        hatT = core.sb(own, "hat_turned", [P, DC, TOKENS])
        inner = core.sb(own, "inner", [P, 4 * DC, TOKENS])
        normalize(core, rows, hat)
        turn(core, hat, DC, hatT, w["ln3_g"], w["ln3_b"])
        linear_turned(core, hatT, w["li2_w"], inner, w["li2_b"], ACT.Gelu)
        linear_rows(core, inner, w["li3_w"], rows, w["li3_b"], rows)


def l0_xattn(core):
    X, nc = core.X, core.nc
    normalize_context(core)
    with ExitStack() as layer:
        U = core.sb(layer, "u", [P, TILES, DIM])
        ln = weights(core, layer, L0_xattn_ln1_g=[P, DIM], L0_xattn_ln1_b=[P, DIM], L0_xattn_ln2_g=[P, DIM],
                     L0_xattn_ln2_b=[P, DIM], causal=[P, SEQ])
        normalize(core, X, U)
        normalize(core, U, U, ln["L0_xattn_ln1_g"], ln["L0_xattn_ln1_b"])
        for a, heads, d in (("a1", 16, 32), ("a2", 16, 32)):
            inner = heads * d
            pre = f"L0_xattn_{a}_"
            with ExitStack() as own:
                cy = DIM if a == "a1" else CDIM
                shapes = {"wv": [P, cy // P, inner],
                          "lnx_g": [P, DC], "lnx_b": [P, DC], "lny_g": [P, cy // P], "lny_b": [P, cy // P]}
                if a == "a1":
                    shapes.update({"wq": [P, DC, inner], "wk": [P, DC, inner], "li1_w": [P, inner // P, DIM], "li1_b": [1, DIM]})
                else:
                    shapes["wkT"] = [P, inner // P, CDIM]
                w = {k[len(pre):]: v for k, v in weights(core, own, **{pre + k: s for k, s in shapes.items()}).items()}
                if a == "a1":
                    R = core.sb(own, "r", [P, TILES, DIM])
                    with ExitStack() as work:
                        hat = core.sb(work, "hat", [P, TILES, DIM])
                        normT = core.sb(work, "norm_turned", [P, DC, TOKENS])
                        qT = core.sb(work, "qT", [P, inner // P, TOKENS])
                        kT = core.sb(work, "kT", [P, inner // P, TOKENS])
                        V = core.sb(work, "v", [P, TILES, inner])
                        O = core.sb(work, "o", [P, TILES, inner])
                        normalize(core, U, hat)
                        turn(core, hat, DC, normT, w["lnx_g"], w["lnx_b"])
                        linear_turned(core, normT, w["wq"], qT)
                        turn(core, hat, DC, normT, w["lny_g"], w["lny_b"])
                        linear_turned(core, normT, w["wk"], kT)
                        linear_rows(core, normT, w["wv"], V)
                        self_attention(core, qT, kT, V, O, heads, d, d, d ** -0.5, mask=ln["causal"])
                        turn(core, O, inner // P, qT)
                        linear_rows(core, qT, w["li1_w"], R, w["li1_b"], U)
                    mlp(core, pre, R)
                    add(core, U, U, R)
                    normalize(core, U, U, ln["L0_xattn_ln2_g"], ln["L0_xattn_ln2_b"])
                else:
                    with ExitStack() as work:
                        sums = core.sb(work, "sums", [P, BATCH, heads // 2, d])
                        vb = core.sb(work, "v_bias", [P, inner // P])
                        wv = core.sb(work, "wv_scaled", [P, inner])
                        qT = core.sb(work, "qT", [P, inner // P, TOKENS])
                        with ExitStack() as front:
                            wq = weights(core, front, **{pre + "wq": [P, DC, inner]})[pre + "wq"]
                            hat = core.sb(front, "hat", [P, TILES, DIM])
                            normT = core.sb(front, "norm_turned", [P, DC, TOKENS])
                            normalize(core, U, hat)
                            turn(core, hat, DC, normT, w["lnx_g"], w["lnx_b"])
                            linear_turned(core, normT, wq, qT)
                        value_affine(core, w["wv"], w["lny_g"], w["lny_b"], wv, vb)
                        wv5 = wv[:].rearrange("c (a p d) -> c p a d", a=2, d=d)
                        context_attention(core, qT, head_queries(w["wkT"]), 4, heads * SEQ, w["lny_g"],
                                          core.dram["context_norm"], lambda pair: wv5[:, pair],
                                          sums, heads // 2, 2, 2, 2, 1, d ** -0.5, d)
                        R = core.sb(work, "r", [P, TILES, DIM])
                        with ExitStack() as back:
                            oT = core.sb(back, "oT", [P, inner // P, TOKENS])
                            li1 = weights(core, back, **{pre + "li1_w": [P, inner // P, DIM], pre + "li1_b": [1, DIM]})
                            turn_sums(core, sums, heads // 2, d, oT, vb)
                            linear_rows(core, oT, li1[pre + "li1_w"], R, li1[pre + "li1_b"], U)
                        mlp(core, pre, R)
                        vector_steps(core, [lambda: nc.vector.tensor_tensor(R[:], R[:], U[:], ALU.add),
                                            lambda: nc.vector.tensor_tensor(X[:], X[:], R[:], ALU.add)])


def value_affine(core, wv, gain, shift, scaled, bias):
    nc, PS = core.nc, core.PS
    ready, step = core.semaphore("rows_ready"), core.semaphore("vector_step")
    chunks = bias.shape[1]
    with nc.Block() as block:
        @block.tensor
        def _(pe):
            wait_weights(core, pe)
            for k in range(chunks):
                last = nc.tensor.matmul(PS[:, k, 0:1], wv[:, 0, k * P:(k + 1) * P], shift[:, 0:1], start=True, stop=True)
            last.then_inc(ready.sem, 1)

        @block.vector
        def _(dve):
            wait_weights(core, dve)
            nc.vector.tensor_scalar(scaled[:], wv[:, 0, :], gain[:, 0:1], None, ALU.mult).then_inc(step.sem, 1)
            dve.wait_ge(ready.sem, ready.at(1))
            nc.vector.tensor_copy(bias[:], PS[:, 0:chunks, 0]).then_inc(step.sem, 1)
    ready.passed(1)
    step.passed(2)


def l0_attn(core):
    nc, X = core.nc, core.X
    heads, d, dv, pad = 8, 16, 32, 32
    with ExitStack() as own:
        w = weights(core, own, L0_attn_Wq=[P, DC, 2 * heads * pad], L0_attn_Wk=[P, DC, 2 * heads * pad],
                    L0_attn_Wv=[P, DC, DIM], L0_attn_Wo=[P, DC, DIM], L0_attn_lq1=[P, d], L0_attn_lk1=[P, d],
                    L0_attn_lq2=[P, d], L0_attn_lk2=[P, d], L0_attn_ln_g=[P, dv], L0_attn_ln_b=[P, dv])
        U = core.sb(own, "u", [P, TILES, DIM])
        uT = core.sb(own, "uT", [P, DC, TOKENS])
        qT = core.sb(own, "qT", [P, 4, TOKENS])
        kT = core.sb(own, "kT", [P, 4, TOKENS])
        V = core.sb(own, "v", [P, TILES, DIM])
        O = core.sb(own, "o", [P, TILES, DIM])
        lam = core.sb(own, "lam", [P, 4])
        normalize(core, X, U)
        turn(core, U, DC, uT)
        linear_turned(core, uT, w["L0_attn_Wq"], qT)
        linear_turned(core, uT, w["L0_attn_Wk"], kT)
        linear_rows(core, uT, w["L0_attn_Wv"], V)
        v = nc.vector
        vector_steps(core, [
            lambda: v.tensor_tensor(w["L0_attn_lq1"][:], w["L0_attn_lq1"][:], w["L0_attn_lk1"][:], ALU.mult),
            lambda: v.tensor_reduce(lam[:, 0:1], w["L0_attn_lq1"][:], AX_X, ALU.add),
            lambda: v.tensor_tensor(w["L0_attn_lq2"][:], w["L0_attn_lq2"][:], w["L0_attn_lk2"][:], ALU.mult),
            lambda: v.tensor_reduce(lam[:, 1:2], w["L0_attn_lq2"][:], AX_X, ALU.add)])
        scalar_step(core, lambda: nc.scalar.activation(lam[:, 0:2], lam[:, 0:2], ACT.Exp))
        vector_steps(core, [
            lambda: v.tensor_tensor(lam[:, 2:3], lam[:, 1:2], lam[:, 0:1], ALU.subtract),
            lambda: v.tensor_scalar(lam[:, 2:3], lam[:, 2:3], -LAM_INIT, None, ALU.add)])
        self_attention(core, qT, kT, V, O, 2 * heads, pad, dv, d ** -0.5, minus_lam=lam[:, 2:3])
        rows = TILES * heads
        O4 = O[:].rearrange("p t (h d) -> p (t h) d", d=dv)
        U4 = U[:].rearrange("p t (h d) -> p (t h) d", d=dv)
        mean = core.sb(own, "mean", [P, rows])
        var = core.sb(own, "variance", [P, rows])
        over = lambda a: a[:].unsqueeze(2).broadcast_to([P, rows, dv])
        along = lambda a: a[:].unsqueeze(1).broadcast_to([P, rows, dv])
        vector_steps(core, [
            lambda: v.tensor_reduce(mean[:], O4, AX_X, ALU.add),
            lambda: v.tensor_scalar(mean[:], mean[:], 1.0 / dv, None, ALU.mult),
            lambda: v.tensor_tensor(O4, O4, over(mean), ALU.subtract),
            lambda: v.tensor_tensor(U4, O4, O4, ALU.mult),
            lambda: v.tensor_reduce(var[:], U4, AX_X, ALU.add),
            lambda: v.tensor_scalar(var[:], var[:], 1.0 / dv, EPS, ALU.mult, ALU.add)])
        scalar_step(core, lambda: nc.scalar.activation(var[:], var[:], ACT.Sqrt))
        vector_steps(core, [
            lambda: v.reciprocal(var[:], var[:]),
            lambda: v.tensor_tensor(O4, O4, over(var), ALU.mult),
            lambda: v.tensor_tensor(O4, O4, along(w["L0_attn_ln_g"]), ALU.mult),
            lambda: v.tensor_tensor(O4, O4, along(w["L0_attn_ln_b"]), ALU.add)])
        turn(core, O, DC, uT)
        linear_rows(core, uT, w["L0_attn_Wo"], X, None, X)


def scalar_step(core, run):
    nc, step = core.nc, core.semaphore("scalar_step")
    with nc.Block() as block:
        @block.scalar
        def _(act):
            wait_weights(core, act)
            run().then_inc(step.sem, 1)
    step.passed(1)


def top_two(core, own, scores):
    nc, step = core.nc, core.semaphore("vector_step")
    best = core.sb(own, "best", [P, TILES, 8])
    place = core.sb(own, "place", [P, TILES, 8], U32)
    placef = core.sb(own, "place_f", [P, TILES, 8])
    first = core.sb(own, "first", [P, TILES, EXPERTS])
    second = core.sb(own, "second", [P, TILES, EXPERTS])
    iota = weights(core, own, iota8=[P, EXPERTS])["iota8"]
    with nc.Block() as block:
        @block.vector
        def _(dve):
            for t in range(TILES):
                nc.vector.max(best[:, t, :], scores[:, t, :]).then_inc(step.sem, 1)
            dve.wait_ge(step.sem, step.at(TILES))
            for t in range(TILES):
                nc.vector.max_index(place[:, t, :], best[:, t, :], scores[:, t, :]).then_inc(step.sem, 1)
            dve.wait_ge(step.sem, step.at(2 * TILES))
            nc.vector.tensor_copy(placef[:], place[:]).then_inc(step.sem, 1)
            dve.wait_ge(step.sem, step.at(2 * TILES + 1))
            wait_weights(core, dve)
            for n, out in enumerate((first, second)):
                nc.vector.tensor_tensor(out[:], iota[:].unsqueeze(1).broadcast_to([P, TILES, EXPERTS]),
                                        placef[:, :, n:n + 1].broadcast_to([P, TILES, EXPERTS]),
                                        ALU.is_equal).then_inc(step.sem, 1)
    step.passed(2 * TILES + 3)
    return best, first, second


def spread(a):
    return a.broadcast_to([P, TILES, EXPERTS])


def gate_bias(core, gates, b2, acc):
    nc, PS = core.nc, core.PS
    ready, taken, rows_ready, rows_taken = (core.semaphore("fill_ready"), core.semaphore("fill_taken_act"),
                                            core.semaphore("rows_ready"), core.semaphore("rows_taken"))
    with ExitStack() as own:
        gT = core.sb(own, "gates_turned", [EXPERTS, TILES, P])
        with nc.Block() as block:
            @block.tensor
            def _(pe):
                wait_weights(core, pe)
                for t in range(TILES):
                    last = nc.tensor.transpose(PS[0:EXPERTS, t // 4, (t % 4) * P:(t % 4 + 1) * P], gates[:, t, :], core.ident[:])
                last.then_inc(ready.sem, 1)
                pe.wait_ge(taken.sem, taken.at(1))
                for t in range(TILES):
                    last = nc.tensor.matmul(PS[:, 2 + t // 2, (t % 2) * DIM:(t % 2 + 1) * DIM], gT[:, t, :], b2[:], start=True, stop=True)
                last.then_inc(rows_ready.sem, 1)

            @block.scalar
            def _(act):
                act.wait_ge(ready.sem, ready.at(1))
                nc.scalar.copy(gT[:].rearrange("e t p -> e (t p)"),
                               PS[0:EXPERTS, 0:2, :].rearrange("e b n -> e (b n)")).then_inc(taken.sem, 1)

            @block.vector
            def _(dve):
                dve.wait_ge(rows_ready.sem, rows_ready.at(1))
                nc.vector.tensor_copy(acc[:].rearrange("p t d -> p (t d)"),
                                      PS[:, 2:6, :].rearrange("p b n -> p (b n)")).then_inc(rows_taken.sem, 1)
    for s in (ready, taken, rows_ready, rows_taken):
        s.passed(1)


class Experts:

    def __init__(self, core, own, w1, w2, wm=None):
        self.core, self.source = core, {"up": w1, "down": w2}
        if wm is not None:
            self.source["second"] = wm
        sizes = {"up": [P, DC, 4 * DIM], "second": [P, DC, 4 * DIM], "down": [P, 4 * DC, DIM]}
        self.raw = {k: core.sb(own, "raw_" + k, sizes[k]) for k in self.source}
        self.parts = {k: [core.sb(own, "part_" + k, sizes[k], F32R) for _ in range(2)] for k in self.source}
        self.landed = {k: core.semaphore("expert_landed_" + k) for k in self.source}
        with core.nc.Block() as block:
            @block.sync
            def _(sp):
                for k in self.source:
                    self.load(sp, k, 0)

    def load(self, sp, k, e):
        sp.dma_start(self.raw[k][:], self.source[k][bass.ds(e, 1)].squeeze(0)).then_inc(self.landed[k].sem, 16)


def experts(core, bank, xT, gates, acc, b1, func, gain=None, shift=None, bm=None):
    nc, PS = core.nc, core.PS
    FC = 4 * DC
    mult, affine = bm is not None, gain is not None
    up_names = ("up", "second") if mult else ("up",)
    begun, act_begun, w_lead = core.semaphore("split_begun"), core.semaphore("hidden_begun"), core.semaphore("weight_lead")
    split = {k: core.semaphore("weight_split_" + k) for k in bank.source}
    up_ready, up_act, up_dve = core.semaphore("up_ready"), core.semaphore("up_taken_act"), core.semaphore("up_taken_dve")
    a_lead, a_split = core.semaphore("hidden_lead"), core.semaphore("hidden_split")
    h_made, h_lead, h_split = core.semaphore("input_made"), core.semaphore("input_lead"), core.semaphore("input_split")
    down_ready, down_taken = core.semaphore("down_ready"), core.semaphore("down_taken")
    small = core.semaphore("expert_vectors_landed")
    ups = FC * HALVES
    ring = 2 if mult else 4
    depth, outs = 4, 4
    vectors = [b1] + ([bm] if mult else []) + ([gain, shift] if affine else [])
    makes = EXPERTS + 1 if affine else 1
    with ExitStack() as own:
        b1s = core.sb(own, "b1", [P, EXPERTS, FC])
        bms = core.sb(own, "bm", [P, EXPERTS, FC]) if mult else None
        if affine:
            gs, ss = core.sb(own, "gain", [P, EXPERTS + 1, DC]), core.sb(own, "shift", [P, EXPERTS + 1, DC])
            h32 = core.sb(own, "input", [P, DC, TOKENS])
        else:
            h32 = xT
        h = [core.sb(own, "input_part", [P, DC, TOKENS], F32R) for _ in range(2)]
        a32 = core.sb(own, "hidden", [P, depth, 512])
        aT = [core.sb(own, "hidden_part", [P, FC, TOKENS], F32R) for _ in range(2)]
        warm = core.sb(own, "warm", [1, 1])
        loads = [(b1s[:], b1)] + ([(bms[:], bm)] if mult else [])
        if affine:
            for s, v in ((gs, gain), (ss, shift)):
                loads += [(s[:, 0:EXPERTS], v), (s[:, EXPERTS:], v[0:1])]

        def hidden_part(part, k):
            half, f = k // FC, k % FC
            return aT[part][:, f, half * 512:(half + 1) * 512]

        with nc.Block() as block:
            @block.sync
            def _(sp):
                for dst, src in loads:
                    sp.dma_start(dst, src.rearrange("e p f -> p e f")).then_inc(small.sem, 16)
                with sp.Fori(1, EXPERTS) as e:
                    for k in bank.source:
                        sp.wait_ge(split[k].sem, split[k].at(e))
                        bank.load(sp, k, e)

            @block.gpsimd
            def _(pool):
                with pool.Fori(0, EXPERTS) as e:
                    for n, k in enumerate(up_names + ("down",)):
                        pool.wait_ge(bank.landed[k].sem, bank.landed[k].at(e * 16 + 16))
                        if k == "down":
                            pool.wait_ge(down_ready.sem, down_ready.at(e * TILES + 1))
                        else:
                            pool.wait_ge(up_ready.sem, up_ready.at(e * ups + 1))
                        pool.sem_inc(begun.sem, 1)
                        lead, rest = bank.parts[k]
                        nc.gpsimd.tensor_copy(lead[:], bank.raw[k][:]).then_inc(w_lead.sem, 1)
                        pool.wait_ge(w_lead.sem, w_lead.at(e * len(split) + n + 1))
                        nc.gpsimd.tensor_tensor(rest[:], bank.raw[k][:], lead[:], ALU.subtract).then_inc(split[k].sem, 1)

            @block.tensor
            def _(pe):
                pe.sem_inc(down_ready.sem, 1)
                pe.sem_inc(up_ready.sem, 1)
                with pe.Fori(0, EXPERTS) as e:
                    for k in up_names:
                        pe.wait_ge(split[k].sem, split[k].at(e + 1))
                    pe.wait_ge(h_split.sem, h_split.at((e + 1) * DC if affine else DC))
                    for k in range(ups):
                        half, f = k // FC, k % FC
                        by = up_dve if mult else up_act
                        pe.wait_ge(by.sem, by.at(e * ups + k + 1))
                        for x, name in enumerate(up_names):
                            for c in range(DC):
                                for m, (a, b) in enumerate(PRODUCTS):
                                    last = nc.tensor.matmul(PS[:, k % ring + 2 * x, :],
                                                            bank.parts[name][a][:, c, f * P:(f + 1) * P],
                                                            h[b][:, c, half * 512:(half + 1) * 512],
                                                            start=(c == 0 and m == 0), stop=(c == DC - 1 and m == 2))
                        last.then_inc(up_ready.sem, 1)
                    pe.wait_ge(split["down"].sem, split["down"].at(e + 1))
                    for t in range(TILES):
                        if t % 4 == 0:
                            pe.wait_ge(a_split.sem, a_split.at(e * ups + (t // 4 + 1) * FC + depth))
                        pe.wait_ge(down_taken.sem, down_taken.at(e * TILES + t + 1))
                        for f in range(FC):
                            for m, (a, b) in enumerate(PRODUCTS):
                                last = nc.tensor.matmul(PS[:, 4 + t % outs, 0:DIM], aT[a][:, f, t * P:(t + 1) * P],
                                                        bank.parts["down"][b][:, f, :],
                                                        start=(f == 0 and m == 0), stop=(f == FC - 1 and m == 2))
                        last.then_inc(down_ready.sem, 1)

            def lead_input(act, e):
                for c in range(DC):
                    if affine:
                        act.wait_ge(h_made.sem, h_made.at(e * DC + c + 1))
                    nc.scalar.copy(h[0][:, c, :], h32[:, c, :]).then_inc(h_lead.sem, 1)

            @block.scalar
            def _(act):
                nc.scalar.activation(warm[:], core.ident[0:1, 0:1], func)
                act.sem_inc(up_act.sem, ring)
                act.wait_ge(small.sem, small.at(16 * len(loads)))
                lead_input(act, 0)

                def lead_hidden(e, k):
                    by = up_dve if mult else up_act
                    act.wait_ge(by.sem, by.at(e * ups + k + 1 + ring))
                    nc.scalar.copy(hidden_part(0, k), a32[:, k % depth, :]).then_inc(a_lead.sem, 1)

                with act.Fori(0, EXPERTS) as e:
                    for k in range(ups):
                        act.wait_ge(up_ready.sem, up_ready.at(e * ups + k + 2))
                        act.wait_ge(a_split.sem, a_split.at(e * ups + k + 1))
                        act.sem_inc(act_begun.sem, 1)
                        nc.scalar.activation(a32[:, k % depth, :], PS[:, k % ring, :], func,
                                             bias=b1s[:, bass.ds(e, 1), k % FC:k % FC + 1].squeeze(1)).then_inc(up_act.sem, 1)
                        if k:
                            lead_hidden(e, k - 1)
                    lead_hidden(e, ups - 1)
                    if affine:
                        lead_input(act, e + 1)

            def make_input(dve, e):
                for c in range(DC):
                    nc.vector.tensor_scalar(h32[:, c, :], xT[:, c, :], gs[:, bass.ds(e, 1), c:c + 1].squeeze(1),
                                            ss[:, bass.ds(e, 1), c:c + 1].squeeze(1), ALU.mult, ALU.add).then_inc(h_made.sem, 1)

            def split_input(dve, e):
                for c in range(DC):
                    dve.wait_ge(h_lead.sem, h_lead.at(e * DC + c + 1))
                    nc.vector.tensor_tensor(h[1][:, c, :], h32[:, c, :], h[0][:, c, :], ALU.subtract).then_inc(h_split.sem, 1)

            @block.vector
            def _(dve):
                dve.sem_inc(down_taken.sem, outs)
                dve.sem_inc(a_split.sem, depth)
                if mult:
                    dve.sem_inc(up_dve.sem, ring)
                dve.wait_ge(small.sem, small.at(16 * len(loads)))
                if affine:
                    make_input(dve, 0)
                split_input(dve, 0)

                def split_hidden(e, k):
                    dve.wait_ge(a_lead.sem, a_lead.at(e * ups + k + 1))
                    nc.vector.tensor_tensor(hidden_part(1, k), a32[:, k % depth, :], hidden_part(0, k),
                                            ALU.subtract).then_inc(a_split.sem, 1)

                with dve.Fori(0, EXPERTS) as e:
                    for k in range(ups):
                        if mult:
                            dve.wait_ge(up_act.sem, up_act.at(e * ups + k + 1 + ring))
                            a = a32[:, k % depth, :]
                            nc.vector.scalar_tensor_tensor(a, PS[:, k % ring + 2, :],
                                                           bms[:, bass.ds(e, 1), k % FC:k % FC + 1].squeeze(1), a,
                                                           ALU.add, ALU.mult).then_inc(up_dve.sem, 1)
                        if k:
                            split_hidden(e, k - 1)
                    split_hidden(e, ups - 1)
                    if affine:
                        dve.wait_ge(up_ready.sem, up_ready.at(e * ups + ups + 1))
                        dve.wait_ge(h_split.sem, h_split.at(e * DC + DC))
                        make_input(dve, e + 1)
                        split_input(dve, e + 1)
                    for t in range(TILES):
                        dve.wait_ge(down_ready.sem, down_ready.at(e * TILES + t + 2))
                        nc.vector.scalar_tensor_tensor(
                            acc[:, t, :], PS[:, 4 + t % outs, 0:DIM], gates[:, t, bass.ds(e, 1)], acc[:, t, :],
                            ALU.mult, ALU.add).then_inc(down_taken.sem, 1)
    for k in bank.source:
        bank.landed[k].passed(16 * EXPERTS)
        split[k].passed(EXPERTS)
    begun.passed(EXPERTS * len(split))
    act_begun.passed(EXPERTS * ups)
    w_lead.passed(EXPERTS * len(split))
    small.passed(16 * len(loads))
    up_ready.passed(ups * EXPERTS + 1)
    up_act.passed(ups * EXPERTS + ring)
    if mult:
        up_dve.passed(ups * EXPERTS + ring)
    a_lead.passed(ups * EXPERTS)
    a_split.passed(ups * EXPERTS + depth)
    if affine:
        h_made.passed(DC * makes)
    h_lead.passed(DC * makes)
    h_split.passed(DC * makes)
    down_ready.passed(TILES * EXPERTS + 1)
    down_taken.passed(TILES * EXPERTS + outs)


def l0_ffn(core):
    nc, X = core.nc, core.X
    v = nc.vector
    with ExitStack() as own:
        w = weights(core, own, L0_ffn_router_W=[P, DC, EXPERTS], L0_ffn_router_b=[1, EXPERTS], L0_ffn_b2=[EXPERTS, DIM])
        d = core.dram
        bank = Experts(core, own, d["L0_ffn_W1"], d["L0_ffn_W2"])
        U = core.sb(own, "u", [P, TILES, DIM])
        hat = core.sb(own, "hat", [P, TILES, DIM])
        uT = core.sb(own, "uT", [P, DC, TOKENS])
        logits = core.sb(own, "logits", [P, TILES, EXPERTS])
        gates = core.sb(own, "gates", [P, TILES, EXPERTS])
        acc = core.sb(own, "acc", [P, TILES, DIM])
        share = core.sb(own, "share", [P, TILES, 2])
        whole = core.sb(own, "gate_sum", [P, TILES])
        normalize(core, X, U)
        turn(core, U, DC, uT)
        linear_rows(core, uT, w["L0_ffn_router_W"], logits, w["L0_ffn_router_b"])
        best, first, second = top_two(core, own, logits)
        vector_steps(core, [lambda: v.tensor_tensor(share[:], best[:, :, 0:2], best[:, :, 0:1].broadcast_to([P, TILES, 2]), ALU.subtract)])
        scalar_step(core, lambda: nc.scalar.activation(share[:], share[:], ACT.Exp))
        vector_steps(core, [
            lambda: v.tensor_reduce(whole[:], share[:], AX_X, ALU.add),
            lambda: v.reciprocal(whole[:], whole[:]),
            lambda: v.tensor_tensor(share[:], share[:], whole[:].unsqueeze(2).broadcast_to([P, TILES, 2]), ALU.mult),
            lambda: v.tensor_tensor(first[:], first[:], spread(share[:, :, 0:1]), ALU.mult),
            lambda: v.tensor_tensor(second[:], second[:], spread(share[:, :, 1:2]), ALU.mult),
            lambda: v.tensor_tensor(gates[:], first[:], second[:], ALU.add)])
        gate_bias(core, gates, w["L0_ffn_b2"], acc)
        vector_steps(core, [
            lambda: v.tensor_reduce(whole[:], gates[:], AX_X, ALU.add),
            lambda: v.tensor_tensor(hat[:], U[:], whole[:].unsqueeze(2).broadcast_to([P, TILES, DIM]), ALU.mult),
            lambda: v.tensor_tensor(acc[:], acc[:], hat[:], ALU.add)])
        normalize(core, U, hat)
        turn(core, hat, DC, uT)
        experts(core, bank, uT, gates, acc, d["L0_ffn_b1"], ACT.Gelu, gain=d["L0_ffn_ln_g"], shift=d["L0_ffn_ln_b"])
        add(core, X, X, acc)


def l1_ffn(core):
    nc, X = core.nc, core.X
    v = nc.vector
    with ExitStack() as own:
        w = weights(core, own, L1_ffn_router_w=[P, DC, EXPERTS], L1_ffn_w2_b=[EXPERTS, DIM])
        d = core.dram
        bank = Experts(core, own, d["L1_ffn_wg_w"], d["L1_ffn_w2_w"], d["L1_ffn_w1_w"])
        U = core.sb(own, "u", [P, TILES, DIM])
        uT = core.sb(own, "uT", [P, DC, TOKENS])
        probs = core.sb(own, "probs", [P, TILES, EXPERTS])
        gates = core.sb(own, "gates", [P, TILES, EXPERTS])
        acc = core.sb(own, "acc", [P, TILES, DIM])
        top = core.sb(own, "top", [P, TILES])
        normalize(core, X, U)
        turn(core, U, DC, uT)
        linear_rows(core, uT, w["L1_ffn_router_w"], probs)
        softmax_experts(core, probs, top, None)
        best, first, second = top_two(core, own, probs)
        vector_steps(core, [
            lambda: v.tensor_tensor(first[:], first[:], spread(best[:, :, 0:1]), ALU.mult),
            lambda: v.tensor_tensor(second[:], second[:], spread(best[:, :, 1:2]), ALU.mult),
            lambda: v.tensor_tensor(gates[:], first[:], second[:], ALU.add)])
        gate_bias(core, gates, w["L1_ffn_w2_b"], acc)
        experts(core, bank, uT, gates, acc, d["L1_ffn_wg_b"], ACT.Gelu, bm=d["L1_ffn_w1_b"])
        add(core, X, X, acc)


def softmax_experts(core, scores, top, keep):
    nc = core.nc
    v = nc.vector
    wide = lambda a: a[:].unsqueeze(2).broadcast_to([P, TILES, EXPERTS])
    vector_steps(core, [
        lambda: v.tensor_reduce(top[:], scores[:], AX_X, ALU.max),
        lambda: v.tensor_tensor(scores[:], scores[:], wide(top), ALU.subtract)])
    scalar_step(core, lambda: nc.scalar.activation(scores[:], scores[:], ACT.Exp))
    vector_steps(core, ([lambda: v.tensor_tensor(scores[:], scores[:], keep[:], ALU.mult)] if keep is not None else []) + [
        lambda: v.tensor_reduce(top[:], scores[:], AX_X, ALU.add),
        lambda: v.reciprocal(top[:], top[:]),
        lambda: v.tensor_tensor(scores[:], scores[:], wide(top), ALU.mult)])


def l2_ffn(core):
    nc, X = core.nc, core.X
    v = nc.vector
    with ExitStack() as own:
        w = weights(core, own, L2_ffn_W_gate=[P, DC, EXPERTS], L2_ffn_b2=[EXPERTS, DIM])
        d = core.dram
        bank = Experts(core, own, d["L2_ffn_W1"], d["L2_ffn_W2"])
        U = core.sb(own, "u", [P, TILES, DIM])
        uT = core.sb(own, "uT", [P, DC, TOKENS])
        gates = core.sb(own, "gates", [P, TILES, EXPERTS])
        keep = core.sb(own, "keep", [P, TILES, EXPERTS])
        best = core.sb(own, "best", [P, TILES, 8])
        acc = core.sb(own, "acc", [P, TILES, DIM])
        top = core.sb(own, "top", [P, TILES])
        normalize(core, X, U)
        turn(core, U, DC, uT)
        linear_rows(core, uT, w["L2_ffn_W_gate"], gates)
        vector_steps(core, [(lambda t: lambda: v.max(best[:, t, :], gates[:, t, :]))(t) for t in range(TILES)] + [
            lambda: v.tensor_tensor(keep[:], gates[:], spread(best[:, :, 1:2]), ALU.is_ge)])
        softmax_experts(core, gates, top, keep)
        vector_steps(core, [lambda: v.tensor_scalar(gates[:], gates[:], 1.0 / EXPERTS, None, ALU.mult)])
        gate_bias(core, gates, w["L2_ffn_b2"], acc)
        experts(core, bank, uT, gates, acc, d["L2_ffn_b1"], ACT.Relu)
        add(core, X, X, acc)


def l1_xattn(core):
    small_xattn(core, "L1_xattn_", True)


def l3_xattn(core):
    small_xattn(core, "L3_xattn_", False)


def small_xattn(core, pre, biased):
    heads, d, pad = 16, 16, 32
    X = core.X
    with ExitStack() as own:
        shapes = {"Wq": [P, DC, heads * pad], "WkT": [P, heads * pad // P, CDIM], "Wv": [P, DIM], "Wo": [P, DC, DIM],
                  "bv": [P, DC]}
        if biased:
            shapes.update({"bq": [P, heads * pad // P], "bo": [1, DIM]})
        w = {k[len(pre):]: t for k, t in weights(core, own, **{pre + k: s for k, s in shapes.items()}).items()}
        sums = core.sb(own, "sums", [P, BATCH, heads // 2, d])
        qT = core.sb(own, "qT", [P, heads * pad // P, TOKENS])
        with ExitStack() as front:
            U = core.sb(front, "u", [P, TILES, DIM])
            uT = core.sb(front, "uT", [P, DC, TOKENS])
            normalize(core, X, U)
            turn(core, U, DC, uT)
            linear_turned(core, uT, w["Wq"], qT, w["bq"] if biased else None)
        wv4 = w["Wv"][:].rearrange("c (a p d) -> c p a d", a=2, d=d)
        context_attention(core, qT, head_queries(w["WkT"]), 4, heads * SEQ, None, core.dram["ctx_512"],
                          lambda pair: wv4[:, pair], sums, heads // 2, 2, 2, 2, 1, d ** -0.5, d)
        oT = core.sb(own, "oT", [P, DC, TOKENS])
        turn_sums(core, sums, heads // 2, d, oT, w["bv"])
        linear_rows(core, oT, w["Wo"], X, w["bo"] if biased else None, X)


def l2_xattn(core):
    X, nc = core.X, core.nc
    with ExitStack() as own:
        w = weights(core, own, L2_xattn_Wq=[P, DC, DIM], L2_xattn_bq=[P, DC], L2_xattn_WkT=[P, DC, CDIM],
                    L2_xattn_Wv=[P, DIM], L2_xattn_bv=[P, DIM])
        sums = core.sb(own, "sums", [SEQ, BATCH, 1, DIM])
        qT = core.sb(own, "qT", [P, DC, TOKENS])
        with ExitStack() as front:
            U = core.sb(front, "u", [P, TILES, DIM])
            uT = core.sb(front, "uT", [P, DC, TOKENS])
            normalize(core, X, U)
            turn(core, U, DC, uT)
            linear_turned(core, uT, w["L2_xattn_Wq"], qT, w["L2_xattn_bq"])

        def queries(j, q):
            half = slice(j * SEQ // 2, (j + 1) * SEQ // 2)
            return [(slice(0, SEQ // 2), w["L2_xattn_WkT"][:, c, :], q[:, c, half], c == 0, c == DC - 1) for c in range(DC)]

        context_attention(core, qT, queries, 2, SEQ, None, core.dram["ctx_512"],
                          lambda pair: w["L2_xattn_Wv"][:].unsqueeze(1), sums, 1, 1, 1, 4, 2, 1.0, DIM)
        out = core.sb(own, "out", [P, TILES, DIM])
        s5 = sums[:].rearrange("s (t a) x d -> s t a (x d)", a=2)
        store(core, [(out[a * SEQ:(a + 1) * SEQ], s5[:, :, a, :]) for a in range(2)])
        v = nc.vector
        vector_steps(core, [
            lambda: v.tensor_tensor(out[:], out[:], w["L2_xattn_bv"][:].unsqueeze(1).broadcast_to([P, TILES, DIM]), ALU.add),
            lambda: v.tensor_tensor(X[:], X[:], out[:], ALU.add)])


def l1_attn(core):
    nc, X, PS = core.nc, core.X, core.PS
    v = nc.vector
    inner, states = 512, 16
    C = inner // P
    with ExitStack() as own:
        w = weights(core, own, L1_attn_norm_w=[P, DC], L1_attn_norm_b=[P, DC], L1_attn_W_in=[P, DC, inner],
                    L1_attn_W_gate=[P, DC, inner], L1_attn_W_dt=[P, C, inner], L1_attn_b_dt=[P, C],
                    L1_attn_W_BC=[P, C, 2 * states], L1_attn_A_log=[P, C, states], L1_attn_W_out=[P, C, DIM])
        zT = core.sb(own, "zT", [P, C, TOKENS])
        gateT = core.sb(own, "gateT", [P, C, TOKENS])
        dtT = core.sb(own, "dtT", [P, C, TOKENS])
        A = w["L1_attn_A_log"]
        with ExitStack() as front:
            U = core.sb(front, "u", [P, TILES, DIM])
            uT = core.sb(front, "uT", [P, DC, TOKENS])
            bcT = core.sb(front, "bcT", [2 * states, 1, TOKENS])
            e = core.sb(front, "e", [P, C, TOKENS])
            normalize(core, X, U)
            add(core, X, X, U)
            normalize(core, U, U)
            turn(core, U, DC, uT, w["L1_attn_norm_w"], w["L1_attn_norm_b"])
            linear_turned(core, uT, w["L1_attn_W_in"], zT)
            linear_turned(core, uT, w["L1_attn_W_gate"], gateT, None, ACT.Silu)
            linear_turned(core, zT, w["L1_attn_W_dt"], dtT, w["L1_attn_b_dt"])
            linear_turned(core, zT, w["L1_attn_W_BC"], bcT, rows=2 * states)
            store(core, [(core.dram["bc_turned"], bcT[:, 0, :])])
            scalar_step(core, lambda: nc.scalar.activation(e[:], dtT[:], ACT.Abs))
            scalar_step(core, lambda: nc.scalar.activation(e[:], e[:], ACT.Exp, scale=-1.0))
            scalar_step(core, lambda: nc.scalar.activation(A[:], A[:], ACT.Exp))
            scalar_step(core, lambda: nc.scalar.activation(e[:], e[:], ACT.Ln, bias=1.0))
            vector_steps(core, [
                lambda: v.scalar_tensor_tensor(dtT[:], dtT[:], 0.0, e[:], ALU.max, ALU.add),
                lambda: v.tensor_scalar(dtT[:], dtT[:], 0.001, 1.0, ALU.max, ALU.min),
                lambda: v.tensor_tensor(zT[:], zT[:], dtT[:], ALU.mult),
                lambda: v.tensor_scalar(A[:], A[:], 1e-6, 1.0, ALU.max, ALU.min),
                lambda: v.tensor_scalar(A[:], A[:], -1.0, None, ALU.mult),
                lambda: v.memset(dtT[:].rearrange("p c (b s) -> p c b s", s=SEQ)[:, :, :, 0:1], 1e30)])
        selective_scan(core, zT, dtT, A, C, states)
        y = dtT
        vector_steps(core, [lambda: v.tensor_tensor(y[:].rearrange("p c n -> p (c n)"), PS[:].rearrange("p b n -> p (b n)"),
                                                    gateT[:].rearrange("p c n -> p (c n)"), ALU.mult)])
        linear_rows(core, y, w["L1_attn_W_out"], X, None, X)


def selective_scan(core, dtz, dt, A, C, states):
    nc, PS = core.nc, core.PS
    landed = core.semaphores("rows_landed", 2)
    decay_ready, in_ready, h_ready, w_ready, summed = (core.semaphore("decay_ready"), core.semaphore("scan_in_ready"),
                                                       core.semaphore("state_ready"), core.semaphore("product_ready"),
                                                       core.semaphore("product_summed"))
    zero_ready = core.semaphore("zero_ready")
    bc = core.dram["bc_turned"]
    with ExitStack() as own:
        Bb = core.sb(own, "b_all", [P, 2, TOKENS])
        Cb = core.sb(own, "c_all", [P, 2, TOKENS])
        decay = core.sb(own, "decay", [P, 2, TOKENS])
        fresh = core.sb(own, "fresh", [P, 2, TOKENS])
        state = core.sb(own, "state", [P, 2, TOKENS])
        prod = core.sb(own, "prod", [P, 2, TOKENS])
        zeros = core.sb(own, "zeros", [P, 512])
        warm = core.sb(own, "warm", [1, 1])
        with nc.Block() as block:
            @block.sync
            def _(sp):
                with sp.Fori(0, states // 2) as it:
                    for u in range(2):
                        s = it * 2 + u
                        sp.wait_ge(w_ready.sem, w_ready.at(s * C + C))
                        sp.dma_start(Bb[:, u, :], bc[bass.ds(s, 1), :].broadcast_to([P, TOKENS])).then_inc(landed[u].sem, 16)
                        sp.dma_start(Cb[:, u, :], bc[bass.ds(s + states, 1), :].broadcast_to([P, TOKENS])).then_inc(landed[u].sem, 16)

            @block.scalar
            def _(act):
                nc.scalar.activation(warm[:], core.ident[0:1, 0:1], ACT.Exp)
                with act.Fori(0, states // 2) as it:
                    for u in range(2):
                        for c in range(C):
                            n = (it * 2 + u) * C + c
                            act.wait_ge(h_ready.sem, h_ready.at(n + 1))
                            nc.scalar.activation(decay[:, c % 2, :], dt[:, c, :], ACT.Exp,
                                                 scale=A[:, c, bass.ds(it * 2 + u, 1)]).then_inc(decay_ready.sem, 1)

            @block.gpsimd
            def _(pool):
                with pool.Fori(0, states // 2) as it:
                    for u in range(2):
                        pool.wait_ge(landed[u].sem, landed[u].at(it * 32 + 32))
                        for c in range(C):
                            n = (it * 2 + u) * C + c
                            pool.wait_ge(h_ready.sem, h_ready.at(n + 1))
                            nc.gpsimd.tensor_tensor(fresh[:, c % 2, :], dtz[:, c, :], Bb[:, u, :], ALU.mult).then_inc(in_ready.sem, 1)

            @block.vector
            def _(dve):
                nc.vector.memset(zeros[:], 0.0).then_inc(zero_ready.sem, 1)
                dve.sem_inc(h_ready.sem, 2)
                dve.sem_inc(w_ready.sem, 2 * C)
                with dve.Fori(0, states // 2) as it:
                    for u in range(2):
                        dve.wait_ge(landed[u].sem, landed[u].at(it * 32 + 32))
                        for c in range(C):
                            n = (it * 2 + u) * C + c
                            dve.wait_ge(decay_ready.sem, decay_ready.at(n + 1))
                            dve.wait_ge(in_ready.sem, in_ready.at(n + 1))
                            nc.vector.tensor_tensor_scan(state[:, c % 2, :], decay[:, c % 2, :], fresh[:, c % 2, :], 0.0,
                                                         ALU.mult, ALU.add).then_inc(h_ready.sem, 1)
                            dve.wait_ge(h_ready.sem, h_ready.at(n + 3))
                            dve.wait_ge(summed.sem, summed.at(n + 1))
                            nc.vector.tensor_tensor(prod[:, c % 2, :], state[:, c % 2, :], Cb[:, u, :], ALU.mult).then_inc(w_ready.sem, 1)

            @block.tensor
            def _(pe):
                pe.sem_inc(summed.sem, 2)
                pe.wait_ge(zero_ready.sem, zero_ready.at(1))
                for k in range(BANKS):
                    nc.tensor.matmul(PS[:, k, :], core.ident[:], zeros[:], start=True, stop=False, skip_group_check=True)
                with pe.Fori(0, states // 2) as it:
                    for u in range(2):
                        for c in range(C):
                            n = (it * 2 + u) * C + c
                            pe.wait_ge(w_ready.sem, w_ready.at(n + 1 + 2 * C))
                            for half in range(HALVES):
                                last = nc.tensor.matmul(PS[:, c * HALVES + half, :], core.ident[:],
                                                        prod[:, c % 2, half * 512:(half + 1) * 512], start=False, stop=False,
                                                        skip_group_check=True)
                            last.then_inc(summed.sem, 1)
                for k in range(BANKS):
                    last = nc.tensor.matmul(PS[:, k, :], core.ident[:], zeros[:], start=False, stop=True, skip_group_check=True)
                last.then_inc(summed.sem, 1)
                pe.wait_ge(summed.sem, summed.at(states * C + 3))
    n = states * C
    for s in landed:
        s.passed(32 * states // 2)
    decay_ready.passed(n)
    in_ready.passed(n)
    h_ready.passed(n + 2)
    w_ready.passed(n + 2 * C)
    summed.passed(n + 3)
    zero_ready.passed(1)


def l2_attn(core):
    nc, X = core.nc, core.X
    v = nc.vector
    heads, d = 16, 16
    with ExitStack() as own:
        w = weights(core, own, L2_attn_key_w=[P, DC, DIM], L2_attn_key_b=[P, DC], L2_attn_v_w=[P, DC, DIM],
                    L2_attn_q_w=[P, DC, DIM], L2_attn_out_w=[P, DC, DIM], L2_attn_out_b=[1, DIM], gather_rows=[P, d, P])
        kT = core.sb(own, "kT", [P, DC, TOKENS])
        freshT = core.sb(own, "freshT", [P, DC, TOKENS])
        qT = core.sb(own, "qT", [P, DC, TOKENS])
        vT = core.sb(own, "vT", [P, DC, TOKENS])
        U = core.sb(own, "u", [P, TILES, DIM])
        uT = core.sb(own, "uT", [P, DC, TOKENS])
        normalize(core, X, U)
        turn(core, U, DC, uT)
        linear_turned(core, uT, w["L2_attn_v_w"], vT)
        store(core, [(core.dram["v_turned"].rearrange("(c p) n -> p c n", p=P), vT[:])])
        linear_turned(core, uT, w["L2_attn_q_w"], qT)
        linear_turned(core, uT, w["L2_attn_key_w"], kT, w["L2_attn_key_b"], ACT.Sigmoid)
        vector_steps(core, [
            lambda: v.tensor_scalar(freshT[:], kT[:], -1.0, 1.0, ALU.mult, ALU.add),
            lambda: v.memset(kT[:].rearrange("p c (b s) -> p c b s", s=SEQ)[:, :, :, 0:1], 0.0)])
        memory_scan(core, kT, freshT, qT, w["gather_rows"], uT, d)
        linear_rows(core, uT, w["L2_attn_out_w"], X, w["L2_attn_out_b"], X)


def memory_scan(core, kT, freshT, qT, gather, dst, d):
    nc, PS = core.nc, core.PS
    landed, used = core.semaphores("rows_landed", DC), core.semaphore("rows_used")
    in_ready, h_ready, w_ready, summed = (core.semaphore("scan_in_ready"), core.semaphore("state_ready"),
                                          core.semaphore("product_ready"), core.semaphore("product_summed"))
    taken = core.semaphore("rows_taken")
    per = P // d
    vrows = core.dram["v_turned"].rearrange("(c h e) n -> c h e n", c=DC, e=d)
    with ExitStack() as own:
        Vb = core.sb(own, "v_all", [P, DC, TOKENS])
        fresh = core.sb(own, "fresh", [P, DC, TOKENS])
        state = core.sb(own, "state", [P, DC, TOKENS])
        prod = core.sb(own, "prod", [P, DC, TOKENS])
        with nc.Block() as block:
            @block.sync
            def _(sp):
                with sp.Fori(0, d) as e:
                    for c in range(DC):
                        sp.wait_ge(used.sem, used.at(e * DC + c + 1))
                        for h in range(per):
                            sp.dma_start(Vb[h * d:(h + 1) * d, c, :],
                                         vrows[c, h, bass.ds(e, 1), :].broadcast_to([d, TOKENS])).then_inc(landed[c].sem, 16)

            @block.gpsimd
            def _(pool):
                pool.sem_inc(used.sem, DC)
                with pool.Fori(0, d) as e:
                    for c in range(DC):
                        n = e * DC + c
                        pool.wait_ge(landed[c].sem, landed[c].at(e * 16 * per + 16 * per))
                        pool.wait_ge(h_ready.sem, h_ready.at(n + 1))
                        nc.gpsimd.tensor_tensor(fresh[:, c, :], freshT[:, c, :], Vb[:, c, :], ALU.mult).then_inc(in_ready.sem, 1)
                        pool.wait_ge(in_ready.sem, in_ready.at(n + 1))
                        pool.sem_inc(used.sem, 1)

            @block.vector
            def _(dve):
                dve.sem_inc(h_ready.sem, DC)
                with dve.Fori(0, d) as e:
                    for c in range(DC):
                        n = e * DC + c
                        dve.wait_ge(in_ready.sem, in_ready.at(n + 1))
                        nc.vector.tensor_tensor_scan(state[:, c, :], kT[:, c, :], fresh[:, c, :], 0.0,
                                                     ALU.mult, ALU.add).then_inc(h_ready.sem, 1)
                        dve.wait_ge(h_ready.sem, h_ready.at(n + DC + 1))
                        dve.wait_ge(summed.sem, summed.at(n + 1))
                        nc.vector.tensor_tensor(prod[:, c, :], state[:, c, :], qT[:, c, :], ALU.mult).then_inc(w_ready.sem, 1)
                dve.wait_ge(summed.sem, summed.at(d * DC + DC))
                nc.vector.tensor_copy(dst[:].rearrange("p c n -> p (c n)"),
                                      PS[:, 0:DC * HALVES, :].rearrange("p b n -> p (b n)")).then_inc(taken.sem, 1)

            @block.tensor
            def _(pe):
                wait_weights(core, pe)
                pe.sem_inc(summed.sem, DC)
                for e in range(d):
                    for c in range(DC):
                        pe.wait_ge(w_ready.sem, w_ready.at(e * DC + c + 1))
                        for half in range(HALVES):
                            last = nc.tensor.matmul(PS[:, c * HALVES + half, :], gather[:, e, :],
                                                    prod[:, c, half * 512:(half + 1) * 512], start=(e == 0), stop=(e == d - 1),
                                                    skip_group_check=True)
                        last.then_inc(summed.sem, 1)
    n = d * DC
    for s in landed:
        s.passed(16 * per * d)
    used.passed(n + DC)
    in_ready.passed(n)
    h_ready.passed(n + DC)
    w_ready.passed(n)
    summed.passed(n + DC)
    taken.passed(1)


def rotate(core, xT, swap, cos, sin):
    nc, PS = core.nc, core.PS
    ready, taken, step = core.semaphore("fill_ready"), core.semaphore("fill_taken_dve"), core.semaphore("norm_step")
    cos_done = core.semaphore("cos_done")
    fills = xT.shape[1] * HALVES
    nb = 512 // SEQ
    wide = lambda a: a[:].unsqueeze(1).broadcast_to([P, nb, SEQ])
    with ExitStack() as own:
        part = core.sb(own, "part", [P, 2, 512])
        with nc.Block() as block:
            @block.tensor
            def _(pe):
                wait_weights(core, pe)
                for f in range(fills):
                    c, half = f // HALVES, f % HALVES
                    if f >= BANKS:
                        pe.wait_ge(step.sem, step.at(f - BANKS + 1))
                    nc.tensor.matmul(PS[:, f % BANKS, :], swap[:], xT[:, c, half * 512:(half + 1) * 512],
                                     start=True, stop=True).then_inc(ready.sem, 1)

            @block.gpsimd
            def _(pool):
                wait_weights(core, pool)
                for f in range(fills):
                    c, half = f // HALVES, f % HALVES
                    x = xT[:, c, half * 512:(half + 1) * 512].rearrange("p (b s) -> p b s", s=SEQ)
                    pool.wait_ge(ready.sem, ready.at(f + 1))
                    nc.gpsimd.tensor_tensor(x, x, wide(cos), ALU.mult).then_inc(cos_done.sem, 1)

            @block.vector
            def _(dve):
                wait_weights(core, dve)
                for f in range(fills):
                    c, half = f // HALVES, f % HALVES
                    x = xT[:, c, half * 512:(half + 1) * 512]
                    dve.wait_ge(ready.sem, ready.at(f + 1))
                    nc.vector.tensor_tensor(part[:, f % 2, :].rearrange("p (b s) -> p b s", s=SEQ),
                                            PS[:, f % BANKS, :].rearrange("p (b s) -> p b s", s=SEQ), wide(sin),
                                            ALU.mult).then_inc(step.sem, 1)
                    dve.wait_ge(step.sem, step.at(f + 1))
                    dve.wait_ge(cos_done.sem, cos_done.at(f + 1))
                    nc.vector.tensor_tensor(x, x, part[:, f % 2, :], ALU.add).then_inc(taken.sem, 1)
    for s in (ready, taken, step, cos_done):
        s.passed(fills)


def l3_attn(core):
    heads, hd = 16, 64
    inner = heads * hd
    C = inner // P
    X = core.X
    with ExitStack() as own:
        w = weights(core, own, L3_attn_ln_gamma=[P, DC], L3_attn_ln_beta=[P, DC], L3_attn_w_out=[P, C, DIM],
                    L3_attn_b_out=[1, DIM], rope_cos=[P, SEQ], rope_sin=[P, SEQ], rope_swap=[P, P])
        qT = core.sb(own, "qT", [P, C, TOKENS])
        V = core.sb(own, "v", [P, TILES, inner])
        with ExitStack() as keys:
            kT = core.sb(keys, "kT", [P, C, TOKENS])
            with ExitStack() as front:
                wqkv = weights(core, front, L3_attn_w_qkv=[P, DC, 3 * inner])["L3_attn_w_qkv"]
                U = core.sb(front, "u", [P, TILES, DIM])
                uT = core.sb(front, "uT", [P, DC, TOKENS])
                normalize(core, X, U)
                normalize(core, U, U)
                turn(core, U, DC, uT, w["L3_attn_ln_gamma"], w["L3_attn_ln_beta"])
                linear_turned(core, uT, wqkv[:, :, 0:inner], qT)
                linear_turned(core, uT, wqkv[:, :, inner:2 * inner], kT)
                linear_rows(core, uT, wqkv[:, :, 2 * inner:3 * inner], V)
            rotate(core, qT, w["rope_swap"], w["rope_cos"], w["rope_sin"])
            rotate(core, kT, w["rope_swap"], w["rope_cos"], w["rope_sin"])
            self_attention(core, qT, kT, V, V, heads, hd, hd, hd ** -0.5)
        turn(core, V, C, qT)
        linear_rows(core, qT, w["L3_attn_w_out"], X, w["L3_attn_b_out"], X)


def l3_ffn(core):
    heads, d = 8, 32
    nc, X = core.nc, core.X
    v = nc.vector
    pre = "L3_ffn_"
    with ExitStack() as own:
        shapes = {"norm_w": [P, DC], "norm_b": [P, DC], "q_w": [P, DC, DIM], "k_w": [P, DC, DIM], "v_w": [P, DC, DIM],
                  "o_w": [P, DC, DIM], "q_b": [P, DC], "k_b": [P, DC], "v_b": [1, DIM], "o_b": [1, DIM]}
        w = {k[len(pre):]: t for k, t in weights(core, own, **{pre + k: s for k, s in shapes.items()}).items()}
        masks = weights(core, own, width_turned=[P, DC, SEQ], width_rows=[P, DIM])
        U = core.sb(own, "u", [P, TILES, DIM])
        hat = core.sb(own, "hat", [P, TILES, DIM])
        uT = core.sb(own, "uT", [P, DC, TOKENS])
        qT = core.sb(own, "qT", [P, DC, TOKENS])
        kT = core.sb(own, "kT", [P, DC, TOKENS])
        V = core.sb(own, "v", [P, TILES, DIM])
        O = core.sb(own, "o", [P, TILES, DIM])
        normalize(core, X, U)
        normalize(core, U, hat)
        turn(core, hat, DC, uT, w["norm_w"], w["norm_b"])

        def cut(c):
            x = uT[:, c, :].rearrange("p (b s) -> p b s", s=SEQ)
            return v.tensor_tensor(x, x, masks["width_turned"][:, c, :].unsqueeze(1).broadcast_to([P, BATCH, SEQ]), ALU.mult)

        vector_steps(core, [(lambda c: lambda: cut(c))(c) for c in range(DC)])
        linear_turned(core, uT, w["q_w"], qT, w["q_b"])
        linear_turned(core, uT, w["k_w"], kT, w["k_b"])
        linear_rows(core, uT, w["v_w"], V, w["v_b"])
        self_attention(core, qT, kT, V, O, heads, d, d, DIM ** -0.5)
        rows_mask = masks["width_rows"][:].unsqueeze(1).broadcast_to([P, TILES, DIM])
        vector_steps(core, [lambda: v.tensor_tensor(O[:], O[:], rows_mask, ALU.mult)])
        turn(core, O, DC, uT)
        linear_rows(core, uT, w["o_w"], O, w["o_b"])
        vector_steps(core, [lambda: v.tensor_tensor(O[:], O[:], rows_mask, ALU.mult),
                            lambda: v.tensor_tensor(O[:], O[:], U[:], ALU.add),
                            lambda: v.tensor_tensor(X[:], X[:], O[:], ALU.add)])


def perceiver(nc, dram):
    sublayers = (l0_xattn, l0_attn, l0_ffn, l1_xattn, l1_attn, l1_ffn, l2_xattn, l2_attn, l2_ffn, l3_xattn, l3_attn, l3_ffn)
    with ExitStack() as hold:
        core = Core(nc, dram, hold)
        first = core.semaphore("vector_step")
        with nc.Block() as block:
            @block.vector
            def _(dve):
                nc.vector.memset(core.ones_row[:], 1.0).then_inc(first.sem, 1)
        first.passed(1)
        fetch(core, [(core.X[:], dram["x"].rearrange("(t p) d -> p t d", p=P)), (core.ident[:], dram["ident"])])
        with nc.Block() as block:
            @block.vector
            def _(dve):
                wait_weights(core, dve)

            @block.tensor
            def _(pe):
                wait_weights(core, pe)

            @block.scalar
            def _(act):
                wait_weights(core, act)
        for n in LAYERS:
            sublayers[n](core)
        store(core, [(dram["out"].rearrange("(t p) d -> p t d", p=P), core.X[:])])




def layouts(inputs):
    import numpy as np

    a = {k: np.asarray(v) for k, v in inputs.items()}
    out = {}

    def chunked(w):
        return w.reshape(-1, P, w.shape[-1]).transpose(1, 0, 2)

    def column(b):
        return b.reshape(-1, P).T

    def pad_heads(w, d, to):
        k = w.shape[0]
        r = np.zeros((k, w.shape[1] // d, to), w.dtype)
        r[:, :, :d] = w.reshape(k, -1, d)
        return r.reshape(k, -1)

    def halves_first(w, d):
        return w.reshape(-1, 2, d, w.shape[-1]).transpose(1, 0, 2, 3).reshape(w.shape)

    out["x"] = a["x"].reshape(TOKENS, DIM)
    out["ctx_512"] = a["ctx_512"]
    for n in ("ln1_g", "ln1_b", "ln2_g", "ln2_b"):
        out[f"L0_xattn_{n}"] = a[f"L0_xattn_{n}"][None]
    for p in ("L0_xattn_a1_", "L0_xattn_a2_"):
        cols = lambda w: w.transpose(1, 0, 2).reshape(w.shape[1], -1)
        out[p + "wq"] = chunked(cols(a[p + "wq"]))
        if "a1" in p:
            out[p + "wk"] = chunked(cols(a[p + "wk"]))
            out[p + "wv"] = chunked(cols(a[p + "wv"]))
            out[p + "li1_w"] = chunked(a[p + "li1_w"])
        else:
            out[p + "wkT"] = chunked(cols(a[p + "wk"]).T)
            out[p + "wv"] = chunked(halves_first(cols(a[p + "wv"]).T, 32).T)
            out[p + "li1_w"] = chunked(halves_first(a[p + "li1_w"], 32))
        for n in ("li2_w", "li3_w"):
            out[p + n] = chunked(a[p + n])
        for n in ("lnx_g", "lnx_b", "lny_g", "lny_b", "ln3_g", "ln3_b", "li2_b"):
            out[p + n] = column(a[p + n])
        for n in ("li1_b", "li3_b"):
            out[p + n] = a[p + n][None]
    for n in ("Wq", "Wk"):
        out["L0_attn_" + n] = chunked(pad_heads(a["L0_attn_" + n], 16, 32))
    for n in ("Wv", "Wo"):
        out["L0_attn_" + n] = chunked(a["L0_attn_" + n])
    for n in ("lq1", "lk1", "lq2", "lk2", "ln_g", "ln_b"):
        out["L0_attn_" + n] = a["L0_attn_" + n][None]

    def per_expert(w):
        return w.reshape(EXPERTS, -1, P, w.shape[-1]).transpose(0, 2, 1, 3)

    def expert_columns(b):
        return b.reshape(EXPERTS, -1, P).transpose(0, 2, 1)

    out["L0_ffn_router_W"] = chunked(a["L0_ffn_router_W"])
    out["L0_ffn_router_b"] = a["L0_ffn_router_b"][None]
    out["L0_ffn_b2"] = a["L0_ffn_b2"]
    out["L0_ffn_W1"], out["L0_ffn_W2"] = per_expert(a["L0_ffn_W1"]), per_expert(a["L0_ffn_W2"])
    for n in ("b1", "ln_g", "ln_b"):
        out["L0_ffn_" + n] = expert_columns(a["L0_ffn_" + n])
    for n in ("wg_w", "w1_w", "w2_w"):
        out["L1_ffn_" + n] = per_expert(a["L1_ffn_" + n].transpose(0, 2, 1))
    for n in ("wg_b", "w1_b"):
        out["L1_ffn_" + n] = expert_columns(a["L1_ffn_" + n])
    out["L1_ffn_w2_b"] = a["L1_ffn_w2_b"]
    out["L1_ffn_router_w"] = chunked(a["L1_ffn_router_w"].T)
    out["L2_ffn_W_gate"] = chunked(a["L2_ffn_W_gate"])
    out["L2_ffn_b2"] = a["L2_ffn_b2"]
    out["L2_ffn_W1"], out["L2_ffn_W2"] = per_expert(a["L2_ffn_W1"]), per_expert(a["L2_ffn_W2"])
    out["L2_ffn_b1"] = expert_columns(a["L2_ffn_b1"])

    p = "L1_xattn_"
    out[p + "Wq"] = chunked(pad_heads(a[p + "Wq"], 16, 32))
    out[p + "bq"] = column(pad_heads(a[p + "bq"][None], 16, 32)[0])
    out[p + "WkT"] = chunked(pad_heads(a[p + "Wk"], 16, 32).T)
    out[p + "Wv"] = halves_first(a[p + "Wv"].T, 16).T
    out[p + "bv"] = column(halves_first(a[p + "bv"][:, None], 16)[:, 0])
    out[p + "Wo"] = chunked(halves_first(a[p + "Wo"], 16))
    out[p + "bo"] = a[p + "bo"][None]
    p = "L3_xattn_"
    out[p + "Wq"] = chunked(pad_heads(a[p + "Wq"].T, 16, 32))
    out[p + "WkT"] = chunked(pad_heads(a[p + "Wkv"][:DIM].T, 16, 32).T)
    out[p + "Wv"] = halves_first(a[p + "Wkv"][DIM:], 16).T
    out[p + "bv"] = np.zeros((P, DC), np.float32)
    out[p + "Wo"] = chunked(halves_first(a[p + "Wo"].T, 16))
    p = "L2_xattn_"
    out[p + "Wq"], out[p + "bq"] = chunked(a[p + "Wq"]), column(a[p + "bq"])
    out[p + "WkT"] = chunked(a[p + "Wk"].T)
    out[p + "Wv"], out[p + "bv"] = a[p + "Wv"], a[p + "bv"][None]

    p = "L1_attn_"
    for n in ("norm_w", "norm_b", "b_dt"):
        out[p + n] = column(a[p + n])
    for n in ("W_in", "W_gate", "W_dt", "W_out", "A_log"):
        out[p + n] = chunked(a[p + n])
    out[p + "W_BC"] = chunked(np.concatenate([a[p + "W_B"], a[p + "W_C"]], axis=1))
    p = "L2_attn_"
    out[p + "key_w"], out[p + "key_b"] = chunked(a[p + "key_w"].T), column(a[p + "key_b"])
    out[p + "v_w"], out[p + "q_w"] = chunked(a[p + "vq_w"][:DIM].T), chunked(a[p + "vq_w"][DIM:].T)
    out[p + "out_w"], out[p + "out_b"] = chunked(a[p + "out_w"].T), a[p + "out_b"][None]
    p = "L3_attn_"
    out[p + "ln_gamma"], out[p + "ln_beta"] = column(a[p + "ln_gamma"]), column(a[p + "ln_beta"])
    out[p + "w_qkv"], out[p + "w_out"], out[p + "b_out"] = chunked(a[p + "w_qkv"]), chunked(a[p + "w_out"]), a[p + "b_out"][None]
    p = "L3_ffn_"
    for n in ("q_w", "k_w", "v_w", "o_w"):
        out[p + n] = chunked(a[p + n].T)
    for n in ("norm_w", "norm_b", "q_b", "k_b"):
        out[p + n] = column(a[p + n])
    for n in ("v_b", "o_b"):
        out[p + n] = a[p + n][None]
    return {k: np.ascontiguousarray(v) for k, v in out.items()}


def constants():
    import numpy as np

    f = np.float32
    out = {"ident": np.eye(P, dtype=f), "iota8": np.arange(EXPERTS, dtype=f)[None]}
    s = np.arange(SEQ)
    out["causal"] = np.tile((s[None, :] > s[:, None]).astype(f), (2, 1))
    r = np.arange(P)
    g = np.zeros((P, 16, P), f)
    for e in range(16):
        g[:, e, :] = (r[:, None] // 16 == r[None, :] // 16) & (r[None, :] % 16 == e)
    out["gather_rows"] = g
    inv = (1.0 / 10000.0 ** (np.arange(0, 64, 2, dtype=f) / f(64))).astype(f)
    ang = (np.arange(SEQ, dtype=f)[:, None] * inv[None, :]).astype(f)
    out["rope_cos"] = np.tile(np.cos(ang).T, (4, 1)).astype(f)
    out["rope_sin"] = np.tile(np.sin(ang).T, (4, 1)).astype(f)
    w = np.zeros((P, P), f)
    for h in (0, 64):
        for i in range(32):
            w[h + 32 + i, h + i] = -1
            w[h + i, h + 32 + i] = 1
    out["rope_swap"] = w
    width = DIM >> (s // 16)
    m = (np.arange(DIM)[:, None] < width[None, :]).astype(f)
    out["width_turned"] = m.reshape(DC, P, SEQ).transpose(1, 0, 2)
    out["width_rows"] = np.tile(m.T, (2, 1))
    return {k: np.ascontiguousarray(v) for k, v in out.items()}


def kernel(**inputs):
    import concourse.bacc as _bacc
    from concourse.bass_utils import run_bass_kernel_spmd as _run

    nc = _bacc.Bacc("TRN2", target_bir_lowering=False, num_devices=1)
    arrays, dram = {}, {}
    for name, a in {**layouts(inputs), **constants()}.items():
        arrays[f"in_{name}"] = a
        dram[name] = nc.dram_tensor(f"in_{name}", a.shape, F32, kind="ExternalInput").ap()
    for name, shape, dtype in (("context_norm", (BATCH, KEYS, CDIM), F32),
                               ("bc_turned", (32, TOKENS), F32), ("v_turned", (DIM, TOKENS), F32)):
        dram[name] = nc.dram_tensor(name, shape, dtype, kind="Internal").ap()
    dram["out"] = nc.dram_tensor("out_x", (TOKENS, DIM), F32, kind="ExternalOutput").ap()
    perceiver(nc, dram)
    r = _run(nc, [arrays], core_ids=[0])
    return r.results[0]["out_x"].reshape(BATCH, SEQ, DIM)
```

```python
from contextlib import ExitStack

import concourse.bass as bass
from concourse import mybir

LAYERS = (0, 1, 2, 3, 4, 5, 6, 7, 8, 9, 10, 11)

F32 = mybir.dt.float32
F32R = mybir.dt.float32r
U32 = mybir.dt.uint32
ALU = mybir.AluOpType
ACT = mybir.ActivationFunctionType
AX_X = mybir.AxisListType.X

P = 128
BATCH, SEQ, DIM = 16, 64, 256
TOKENS = BATCH * SEQ
TILES = TOKENS // P
HALVES = TOKENS // 512
DC = DIM // P
KEYS, CDIM = 1601, 128
KT = -(-KEYS // P)
KLAST = KEYS - (KT - 1) * P
EXPERTS = 8
EPS = 1e-5
BANKS = 8
LAM_INIT = 0.8 - 0.6 * 2.718281828459045 ** (-0.3 * 12)


class Count:

    def __init__(self, sem):
        self.sem = sem
        self.past = 0

    def at(self, n):
        return n + self.past

    def passed(self, n):
        self.past += n


class Core:

    def __init__(self, nc, dram, hold):
        self.nc, self.dram, self.hold = nc, dram, hold
        self.known = {}
        self.serial = 0
        self.PS = hold.enter_context(nc.psum_tensor("PS", [P, BANKS, 512], F32))
        self.X = self.sb(hold, "residual", [P, TILES, DIM])
        self.ident = self.sb(hold, "ident", [P, P])
        self.ones_row = self.sb(hold, "ones_row", [1, P])

    def sb(self, own, name, shape, dtype=F32):
        self.serial += 1
        return own.enter_context(self.nc.sbuf_tensor(f"{name}_{self.serial}", shape, dtype))

    def semaphores(self, name, n):
        return [self.semaphore(f"{name}_{u}") for u in range(n)]

    def semaphore(self, name):
        if name not in self.known:
            self.known[name] = Count(self.hold.enter_context(self.nc.semaphore(name)))
        return self.known[name]


class Weights(dict):
    loads = ()


def weights(core, own, pre="", **shapes):
    landed = core.semaphore("weights_landed")
    room = Weights()
    loads = []
    for name, shape in shapes.items():
        t = core.sb(own, pre + name, shape)
        src = core.dram[pre + name]
        if src.shape[0] == 1 and shape[0] > 1:
            src = src[0].partition_broadcast(shape[0])
        room[name] = t
        loads.append((t[:], src, landed))
    room.loads = loads
    landed.passed(16 * len(loads))
    return room


def start_loads(block, loads):
    if loads:
        @block.sync
        def _(sp):
            for dst, src, landed in loads:
                sp.dma_start(dst, src).then_inc(landed.sem, 16)


def wait_weights(core, eng):
    landed = core.semaphore("weights_landed")
    eng.wait_ge(landed.sem, landed.past)


def normalize(core, src, dst, gain=None, shift=None, loads=(), clear=None):
    nc = core.nc
    step, var_ready, dev_ready = core.semaphore("norm_step"), core.semaphore("variance_ready"), core.semaphore("deviation_ready")
    cleared = core.semaphore("zero_ready")
    with ExitStack() as own:
        stats = core.sb(own, "stats", [P, TILES, 6])
        moments = core.sb(own, "moments", [P, TILES, 2])
        dev = core.sb(own, "deviation", [P, TILES])
        rstd = core.sb(own, "rstd", [P, TILES])
        with nc.Block() as block:
            start_loads(block, loads)

            if clear is not None:
                @block.gpsimd
                def _(pool):
                    nc.gpsimd.memset(clear[:], 0.0).then_inc(cleared.sem, 1)
                    pool.wait_ge(cleared.sem, cleared.at(1))

            @block.vector
            def _(dve):
                for t in range(TILES):
                    nc.vector.bn_stats(stats[:, t, :], src[:, t, :]).then_inc(step.sem, 1)
                dve.wait_ge(step.sem, step.at(TILES))
                for t in range(TILES):
                    nc.vector.bn_aggr(moments[:, t, :], stats[:, t, :]).then_inc(step.sem, 1)
                dve.wait_ge(step.sem, step.at(2 * TILES))
                nc.vector.tensor_scalar(dev[:], moments[:, :, 1], EPS, None, ALU.add).then_inc(var_ready.sem, 1)
                dve.wait_ge(dev_ready.sem, dev_ready.at(1))
                nc.vector.reciprocal(rstd[:], dev[:]).then_inc(step.sem, 1)
                dve.wait_ge(step.sem, step.at(2 * TILES + 1))
                for t in range(TILES):
                    nc.vector.tensor_scalar(dst[:, t, :], src[:, t, :], moments[:, t, 0:1], rstd[:, t:t + 1],
                                            ALU.subtract, ALU.mult).then_inc(step.sem, 1)
                if gain is not None:
                    wait_weights(core, dve)
                    dve.wait_ge(step.sem, step.at(3 * TILES + 1))
                    nc.vector.tensor_tensor(dst[:], dst[:], gain[:].unsqueeze(1).broadcast_to([P, TILES, DIM]),
                                            ALU.mult).then_inc(step.sem, 1)
                    dve.wait_ge(step.sem, step.at(3 * TILES + 2))
                    nc.vector.tensor_tensor(dst[:], dst[:], shift[:].unsqueeze(1).broadcast_to([P, TILES, DIM]),
                                            ALU.add).then_inc(step.sem, 1)

            @block.scalar
            def _(act):
                act.wait_ge(var_ready.sem, var_ready.at(1))
                nc.scalar.activation(dev[:], dev[:], ACT.Sqrt).then_inc(dev_ready.sem, 1)
    step.passed(3 * TILES + 1 + (2 if gain is not None else 0))
    var_ready.passed(1)
    dev_ready.passed(1)
    if clear is not None:
        cleared.passed(1)


def evacuate(core, block, fills, ready, by_act, by_dve, act_op, dve_op):
    @block.scalar
    def _(act):
        wait_weights(core, act)
        for f in range(0, fills, 2):
            act.wait_ge(ready.sem, ready.at(f + 1))
            act_op(f).then_inc(by_act.sem, 1)

    @block.vector
    def _(dve):
        wait_weights(core, dve)
        for f in range(1, fills, 2):
            dve.wait_ge(ready.sem, ready.at(f + 1))
            dve_op(f).then_inc(by_dve.sem, 1)


def wait_bank(pe, f, by_act, by_dve):
    if f >= BANKS:
        by = by_act if f % 2 == 0 else by_dve
        pe.wait_ge(by.sem, by.at((f - BANKS) // 2 + 1))


def turn(core, src, chunks, dst, gain=None, shift=None):
    nc, PS = core.nc, core.PS
    ready, by_act, by_dve = core.semaphore("fill_ready"), core.semaphore("fill_taken_act"), core.semaphore("fill_taken_dve")
    fills = chunks * HALVES

    def place(f):
        c, half = f // HALVES, f % HALVES
        return c, dst[:, c, half * 512:(half + 1) * 512], PS[:, f % BANKS, :]

    def act_op(f):
        c, out, bank = place(f)
        return nc.scalar.activation(out, bank, ACT.Identity,
                                    bias=0.0 if shift is None else shift[:, c:c + 1],
                                    scale=1.0 if gain is None else gain[:, c:c + 1])

    def dve_op(f):
        c, out, bank = place(f)
        if gain is None and shift is None:
            return nc.vector.tensor_copy(out, bank)
        return nc.vector.tensor_scalar(out, bank, 1.0 if gain is None else gain[:, c:c + 1],
                                       0.0 if shift is None else shift[:, c:c + 1], ALU.mult, ALU.add)

    with nc.Block() as block:
        @block.tensor
        def _(pe):
            for f in range(fills):
                c, half = f // HALVES, f % HALVES
                wait_bank(pe, f, by_act, by_dve)
                for j in range(4):
                    last = nc.tensor.transpose(PS[:, f % BANKS, j * P:(j + 1) * P],
                                               src[:, half * 4 + j, c * P:(c + 1) * P], core.ident[:])
                last.then_inc(ready.sem, 1)

        evacuate(core, block, fills, ready, by_act, by_dve, act_op, dve_op)
    ready.passed(fills)
    by_act.passed((fills + 1) // 2)
    by_dve.passed(fills // 2)


def linear_turned(core, src, w, dst, bias=None, func=ACT.Identity, rows=P):
    nc, PS = core.nc, core.PS
    ready, by_act, by_dve = core.semaphore("fill_ready"), core.semaphore("fill_taken_act"), core.semaphore("fill_taken_dve")
    kc = src.shape[1]
    fills = dst.shape[1] * HALVES
    plain = func == ACT.Identity

    def place(f):
        m, half = f // HALVES, f % HALVES
        return m, dst[0:rows, m, half * 512:(half + 1) * 512], PS[0:rows, f % BANKS, :]

    def act_op(f):
        m, out, bank = place(f)
        return nc.scalar.activation(out, bank, func, bias=0.0 if bias is None else bias[:, m:m + 1])

    def dve_op(f):
        m, out, bank = place(f)
        if bias is None:
            return nc.vector.tensor_copy(out, bank)
        return nc.vector.tensor_scalar(out, bank, bias[:, m:m + 1], None, ALU.add)

    with nc.Block() as block:
        @block.tensor
        def _(pe):
            wait_weights(core, pe)
            for f in range(fills):
                m, half = f // HALVES, f % HALVES
                if plain:
                    wait_bank(pe, f, by_act, by_dve)
                elif f >= BANKS:
                    pe.wait_ge(by_act.sem, by_act.at(f - BANKS + 1))
                for c in range(kc):
                    last = nc.tensor.matmul(PS[0:rows, f % BANKS, :], w[:, c, m * P:m * P + rows],
                                            src[:, c, half * 512:(half + 1) * 512],
                                            start=(c == 0), stop=(c == kc - 1))
                last.then_inc(ready.sem, 1)

        if plain:
            evacuate(core, block, fills, ready, by_act, by_dve, act_op, dve_op)
        else:
            @block.scalar
            def _(act):
                wait_weights(core, act)
                for f in range(fills):
                    act.wait_ge(ready.sem, ready.at(f + 1))
                    act_op(f).then_inc(by_act.sem, 1)
    ready.passed(fills)
    if plain:
        by_act.passed((fills + 1) // 2)
        by_dve.passed(fills // 2)
    else:
        by_act.passed(fills)


def linear_rows(core, src, w, dst, bias=None, base=None):
    nc, PS = core.nc, core.PS
    ready, taken = core.semaphore("rows_ready"), core.semaphore("rows_taken")
    kc, n_all = src.shape[1], dst.shape[2]
    cuts = [(n, min(512, n_all - n)) for n in range(0, n_all, 512)]
    fills = [(t, n, k) for t in range(TILES) for n, k in cuts]
    with nc.Block() as block:
        @block.tensor
        def _(pe):
            wait_weights(core, pe)
            for f, (t, n, k) in enumerate(fills):
                if f >= BANKS:
                    pe.wait_ge(taken.sem, taken.at(f - BANKS + 1))
                out = PS[:, f % BANKS, 0:k]
                if bias is not None:
                    nc.tensor.matmul(out, core.ones_row[0:1, :], bias[0:1, n:n + k], start=True, stop=False)
                for c in range(kc):
                    last = nc.tensor.matmul(out, src[:, c, t * P:(t + 1) * P], w[:, c, n:n + k],
                                            start=(c == 0 and bias is None), stop=(c == kc - 1))
                last.then_inc(ready.sem, 1)

        @block.vector
        def _(dve):
            for f, (t, n, k) in enumerate(fills):
                dve.wait_ge(ready.sem, ready.at(f + 1))
                if base is None:
                    ins = nc.vector.tensor_copy(dst[:, t, n:n + k], PS[:, f % BANKS, 0:k])
                else:
                    ins = nc.vector.tensor_tensor(dst[:, t, n:n + k], PS[:, f % BANKS, 0:k], base[:, t, n:n + k],
                                                  ALU.add)
                ins.then_inc(taken.sem, 1)
    ready.passed(len(fills))
    taken.passed(len(fills))


def vector_steps(core, steps):
    nc, step = core.nc, core.semaphore("vector_step")
    with nc.Block() as block:
        @block.vector
        def _(dve):
            wait_weights(core, dve)
            for n, run in enumerate(steps):
                if n:
                    dve.wait_ge(step.sem, step.at(n))
                run().then_inc(step.sem, 1)
    step.passed(len(steps))


def add(core, dst, a, b):
    vector_steps(core, [lambda: core.nc.vector.tensor_tensor(dst[:], a[:], b[:], ALU.add)])


def self_attention(core, qT, kT, V, O, heads, d, dv, scale, mask=None, minus_lam=None):
    nc, PS = core.nc, core.PS
    qc = qT.shape[1]
    groups = P // d
    per = heads // groups
    diff = minus_lam is not None
    og = groups // 2 if diff else groups
    squares = og * per
    tfills = squares // 4
    qk_staged, v_staged = core.semaphores("qk_staged", 2), core.semaphores("v_staged", 2)
    s_ready, shifted = core.semaphore("scores_ready"), core.semaphore("scores_shifted")
    exps, probs = core.semaphore("exps_ready"), core.semaphore("squares_ready")
    turned, t_act = core.semaphore("squares_turned"), core.semaphore("squares_taken_act")
    o_ready, o_taken, step = core.semaphore("out_ready"), core.semaphore("out_taken"), core.semaphore("softmax_step")
    begun = core.semaphore("scores_begun")
    steps = 4 + (1 if diff else 0) + (1 if mask is not None else 0)

    def head_of(pos):
        g, k = pos // per, pos % per
        return k * og + g

    with ExitStack() as own:
        qs = core.sb(own, "q_tile", [P, 2, qc, P])
        ks = core.sb(own, "k_tile", [P, 2, qc, P])
        vs = core.sb(own, "v_tile", [P, 2, V.shape[2]])
        E = core.sb(own, "exps", [P, groups, per, SEQ])
        squares_sb = core.sb(own, "squares", [P, og, per, P])
        turned_sb = core.sb(own, "squares_turned", [P, squares, P])
        top = core.sb(own, "row_max", [P, groups, per])
        total = core.sb(own, "row_sum", [P, groups, per])
        warm = core.sb(own, "warm", [1, 1])
        S = PS[:, 0:groups, 0:per * SEQ].rearrange("p g (k t) -> p g k t", t=SEQ)
        flat = squares_sb[:].rearrange("p g k s -> p (g k) s")
        O_ps = PS[:, 6:8, :].rearrange("p b n -> p (b n)")
        wide = squares * dv
        with nc.Block() as block:
            @block.sync
            def _(sp):
                def load_qk(i, u):
                    sp.dma_start(qs[:, u], qT[:, :, bass.ds(i * P, P)]).then_inc(qk_staged[u].sem, 16)
                    sp.dma_start(ks[:, u], kT[:, :, bass.ds(i * P, P)]).then_inc(qk_staged[u].sem, 16)

                def load_v(i, u):
                    sp.dma_start(vs[:, u], V[:, bass.ds(i, 1), :].rearrange("p a n -> p (a n)")).then_inc(v_staged[u].sem, 16)

                for u in range(2):
                    load_qk(u, u)
                    load_v(u, u)
                with sp.Fori(1, TILES // 2) as it:
                    for u in range(2):
                        i = it * 2 + u
                        sp.wait_ge(s_ready.sem, s_ready.at(i - 1))
                        load_qk(i, u)
                        sp.wait_ge(o_ready.sem, o_ready.at(i - 1))
                        load_v(i, u)

            @block.tensor
            def _(pe):
                def scores(i, pair, u):
                    pe.wait_ge(qk_staged[u].sem, qk_staged[u].at(pair * 32 + 32))
                    if not (isinstance(i, int) and i == 0):
                        pe.wait_ge(shifted.sem, shifted.at(i))
                    if d == 64:
                        pe.sem_inc(begun.sem, 1)
                    for h in range(heads):
                        g, k = h % groups, h // groups
                        for b in range(2):
                            last = nc.tensor.matmul(PS[b * SEQ:(b + 1) * SEQ, g, k * SEQ:(k + 1) * SEQ],
                                                    qs[g * d:(g + 1) * d, u, k, b * SEQ:(b + 1) * SEQ],
                                                    ks[g * d:(g + 1) * d, u, k, b * SEQ:(b + 1) * SEQ],
                                                    start=True, stop=True)
                    last.then_inc(s_ready.sem, 1)

                def output(i, pair, u):
                    pe.wait_ge(probs.sem, probs.at(i * 2 + 2))
                    for j in range(tfills):
                        pe.wait_ge(t_act.sem, t_act.at(i * tfills + j + 1))
                        for m in range(4):
                            last = nc.tensor.transpose(PS[:, 4 + j % 2, m * P:(m + 1) * P], flat[:, 4 * j + m, :],
                                                       core.ident[:])
                        last.then_inc(turned.sem, 1)
                    pe.wait_ge(v_staged[u].sem, v_staged[u].at(pair * 16 + 16))
                    pe.wait_ge(t_act.sem, t_act.at(i * tfills + tfills + 2))
                    pe.wait_ge(o_taken.sem, o_taken.at(i + 1))
                    for pos in range(squares):
                        h = head_of(pos)
                        last = nc.tensor.matmul(O_ps[:, h * dv:(h + 1) * dv], turned_sb[:, pos, :],
                                                vs[:, u, h * dv:(h + 1) * dv], start=True, stop=True)
                    last.then_inc(o_ready.sem, 1)

                scores(0, 0, 0)
                with pe.Fori(0, TILES // 2 - 1) as it:
                    scores(it * 2 + 1, it, 1)
                    output(it * 2, it, 0)
                    scores(it * 2 + 2, it + 1, 0)
                    output(it * 2 + 1, it, 1)
                scores(TILES - 1, TILES // 2 - 1, 1)
                output(TILES - 2, TILES // 2 - 1, 0)
                output(TILES - 1, TILES // 2 - 1, 1)

            @block.vector
            def _(dve):
                def softmax(i):
                    later = not (isinstance(i, int) and i == 0)
                    done = [0]

                    def then(ins):
                        done[0] += 1
                        ins.then_inc(step.sem, 1)
                        dve.wait_ge(step.sem, step.at(i * steps + 1 + done[0]))

                    dve.wait_ge(s_ready.sem, s_ready.at(i + 1))
                    then(nc.vector.tensor_reduce(top[:], S, AX_X, ALU.max))
                    if later:
                        dve.wait_ge(probs.sem, probs.at(i * 2))
                    nc.vector.tensor_tensor(E[:], S, top[:].unsqueeze(3).broadcast_to([P, groups, per, SEQ]),
                                            ALU.subtract).then_inc(shifted.sem, 1)
                    dve.wait_ge(exps.sem, exps.at(i + 1))
                    then(nc.vector.tensor_reduce(total[:], E[:], AX_X, ALU.add))
                    then(nc.vector.reciprocal(total[:], total[:]))
                    if diff:
                        odd = total[:, 1::2, :]
                        then(nc.vector.tensor_scalar(odd, odd, minus_lam, None, ALU.mult))
                    then(nc.vector.tensor_tensor(E[:], E[:], total[:].unsqueeze(3).broadcast_to([P, groups, per, SEQ]),
                                                 ALU.mult))
                    if mask is not None:
                        Ef = E[:].rearrange("p g k t -> p (g k) t")
                        then(nc.vector.tensor_tensor(Ef, Ef, mask[:].unsqueeze(1).broadcast_to([P, heads, SEQ]), ALU.mult))
                    if later:
                        dve.wait_ge(turned.sem, turned.at(i * tfills))
                    for b in range(2):
                        rows = slice(b * SEQ, (b + 1) * SEQ)
                        out = squares_sb[rows, :, :, b * SEQ:(b + 1) * SEQ]
                        if diff:
                            ins = nc.vector.tensor_tensor(out, E[rows, 0::2], E[rows, 1::2], ALU.add)
                        else:
                            ins = nc.vector.tensor_copy(out, E[rows])
                        ins.then_inc(probs.sem, 1)

                def take(i):
                    dve.wait_ge(o_ready.sem, o_ready.at(i + 1))
                    nc.vector.tensor_copy(O[:, bass.ds(i, 1), :].rearrange("p a n -> p (a n)"),
                                          O_ps[:, 0:wide]).then_inc(o_taken.sem, 1)

                nc.vector.memset(squares_sb[:], 0.0).then_inc(step.sem, 1)
                dve.wait_ge(step.sem, step.at(1))
                dve.sem_inc(o_taken.sem, 1)
                softmax(0)
                with dve.Fori(1, TILES) as i:
                    softmax(i)
                    take(i - 1)
                take(TILES - 1)

            @block.scalar
            def _(act):
                nc.scalar.activation(warm[:], core.ident[0:1, 0:1], ACT.Exp)
                act.sem_inc(t_act.sem, 2)
                with act.Fori(0, TILES) as i:
                    act.wait_ge(shifted.sem, shifted.at(i + 1))
                    nc.scalar.activation(E[:], E[:], ACT.Exp, scale=scale).then_inc(exps.sem, 1)
                    for j in range(tfills):
                        act.wait_ge(turned.sem, turned.at(i * tfills + j + 1))
                        nc.scalar.copy(turned_sb[:, 4 * j:4 * j + 4, :].rearrange("p m s -> p (m s)"),
                                       PS[:, 4 + j % 2, :]).then_inc(t_act.sem, 1)
    for u in range(2):
        qk_staged[u].passed(32 * TILES // 2)
        v_staged[u].passed(16 * TILES // 2)
    for s in (s_ready, shifted, exps, o_ready):
        s.passed(TILES)
    o_taken.passed(TILES + 1)
    probs.passed(2 * TILES)
    if d == 64:
        begun.passed(TILES)
    turned.passed(tfills * TILES)
    t_act.passed(tfills * TILES + 2)
    step.passed(steps * TILES + 1)


def store(core, pairs):
    nc, stored = core.nc, core.semaphore("stored")
    with nc.Block() as block:
        @block.sync
        def _(sp):
            for dst, src in pairs:
                sp.dma_start(dst, src).then_inc(stored.sem, 16)
            sp.wait_ge(stored.sem, stored.at(16 * len(pairs)))
    stored.passed(16 * len(pairs))


PRODUCTS = ((0, 0), (0, 1), (1, 0))


class ContextRoom:

    def __init__(self, core, own, y_bufs, chunks, blocks, spare=()):
        self.y = [core.sb(own, "context_rows", [P, KT, CDIM]) for _ in range(y_bufs - len(spare))] + list(spare)
        self.landed = core.semaphores("context_landed", y_bufs)
        self.blocks = blocks
        self.q_tile = core.sb(own, "q_tile", [P, 2, chunks, blocks * SEQ])
        self.loads = [load for slot in range(y_bufs) for load in self.rows(core, slot, slot)]

    def rows(self, core, b, slot):
        context, t = core.dram["ctx_512"], self.y[slot]
        return [(t[:, 0:KT - 1, :], context[bass.ds(b, 1), 0:(KT - 1) * P, :].rearrange("a (k p) c -> p (a k) c", p=P),
                 self.landed[slot]),
                (t[0:KLAST, KT - 1, :], context[bass.ds(b, 1), (KT - 1) * P:KEYS, :].rearrange("a p c -> p (a c)"),
                 self.landed[slot])]


def context_attention(core, room, qT, queries, q_fills, q_cols, norm, gain, wv_of, sums, pairs, heads_in, per_group, unroll,
                      scale, d_out):
    nc, PS = core.nc, core.PS
    y, y_bufs, y_landed, q_tile, blocks = room.y, len(room.y), room.landed, room.q_tile, room.blocks
    centred = core.semaphore("centred")
    stats_step, stats_begun, y_normal = (core.semaphore("stats_step"), core.semaphore("stats_begun"),
                                                      core.semaphore("context_normal"))
    var_ready, dev_ready = core.semaphore("variance_ready"), core.semaphore("deviation_ready")
    q_staged = core.semaphores("tile_staged", 2)
    s_ready, m_ready, e_done = core.semaphore("scores_ready"), core.semaphore("max_ready"), core.semaphore("exps_ready")
    turned, t_act, t_dve = core.semaphore("squares_turned"), core.semaphore("lead_taken"), core.semaphore("rest_taken")
    y_lead, y_split, y_begun = core.semaphore("context_lead"), core.semaphore("context_split"), core.semaphore("split_begun")
    o_ready, o_taken = core.semaphore("weighted_ready"), core.semaphore("weighted_taken")
    f_ready, f_taken, step = core.semaphore("out_ready"), core.semaphore("out_taken"), core.semaphore("softmax_step")
    sum_done, inv_done = core.semaphore("row_sum_ready"), core.semaphore("row_scale_ready")
    turns = BATCH // unroll
    steps_all = BATCH * pairs
    per_turn = unroll * pairs
    groups_all = steps_all // per_group
    groups_batch = pairs // per_group
    groups = unroll * groups_batch
    wide = per_group * P
    even = KEYS + KEYS % 2
    halves = (slice(0, 1024), slice(1024, KEYS))
    ahead = q_fills + 4
    per_step = ahead // pairs
    parts = [list(range(KT))[KT * n // per_group:KT * (n + 1) // per_group] for n in range(per_group)]
    S = PS[:, 0:4, :].rearrange("p b n -> p (b n)")
    O_ps = PS[:, 7, 0:wide]
    F_ps = PS[:, 3, P:P + per_group * heads_in * d_out].rearrange("p (g a d) -> p g a d", g=per_group, a=heads_in)
    q_wide = q_cols // q_fills

    def keys_in(k):
        return KLAST if k == KT - 1 else P

    with ExitStack() as own:
        yp = [core.sb(own, "context_part", [P, 2, KT, CDIM], F32R) for _ in range(2)]
        yT = [core.sb(own, "context_turned", [P, 2, even], F32R) for _ in range(2)]
        qs = [core.sb(own, "queries", [P, 2, pairs * P], F32R) for _ in range(2)]
        probs = core.sb(own, "probs", [P, 2, KEYS])
        probsT = [core.sb(own, "probs_turned", [P, 2, KT, wide], F32R) for _ in range(2)]
        OT = core.sb(own, "weighted", [P, 2, wide])
        if norm:
            stats = core.sb(own, "stats", [P, KT, 6])
            moments = core.sb(own, "moments", [P, KT, 2])
            rstd = core.sb(own, "rstd", [P, KT])
            minus_half = core.sb(own, "minus_half", [P, KT])
        top = core.sb(own, "row_max", [P, 2, 2])
        bias = core.sb(own, "minus_max", [P, 2])
        total = core.sb(own, "row_sum", [P, per_turn, 2])
        warm = core.sb(own, "warm", [1, 1])
        inverse = core.sb(own, "row_scale", [P, 4, per_group])

        def brings(it, local):
            return not (isinstance(it, int) and it == turns - 1 and local >= per_turn - pairs)

        def fill_number(it, local, at):
            n = it * per_turn + local
            if isinstance(n, int) and n == 0:
                return ahead + at - 2
            missing = max(0, local - (per_turn - pairs)) if isinstance(it, int) and it == turns - 1 else 0
            return n * (4 + per_step) + (ahead - 4 - missing * per_step + at)

        def turn_number(it, local, j):
            return fill_number(it, local, j if j < 2 or not brings(it, local) else j + per_step)

        def bring_number(it, local, x):
            return fill_number(it, local, 2 + x)

        def parity(it, local, at):
            return fill_number(it if isinstance(it, int) else 2, local, at) % 2

        def turn_bank(it, local, j):
            if per_step == 1:
                return 4 + j % 2
            return 4 + parity(it, local, j if j < 2 or not brings(it, local) else j + per_step)

        def bring_bank(it, local, x):
            return 6 if per_step == 1 else 4 + parity(it, local, 2 + x)

        def wait_fill(pe, number, between=1):
            pe.wait_ge(t_dve.sem, t_dve.at(number + 2 - between))

        def pe_bring(pe, e, b, number, bank):
            between = 2 if bank == 6 else 1
            if e < q_fills:
                if e == 0:
                    pe.wait_ge(q_staged[b[1] % 2].sem, q_staged[b[1] % 2].at(16 * blocks * (b[0] * (unroll // 2) + b[1] // 2 + 1)))
                wait_fill(pe, number, between)
                for cols, w, moving, start, stop in queries(e, q_tile[:, b[1] % 2]):
                    last = nc.tensor.matmul(PS[:, bank, cols], w, moving, start=start, stop=stop)
            else:
                j = e - q_fills
                slot = landed_slot(b)
                if j == 0 and norm:
                    pe.wait_ge(y_normal.sem, y_normal.at((b[0] * unroll + b[1]) * 2 + 2))
                elif j == 0:
                    pe.wait_ge(y_landed[slot].sem, y_landed[slot].at(landed_count(b)))
                wait_fill(pe, number, between)
                for k in range(4 * j, min(4 * j + 4, KT)):
                    kk = keys_in(k)
                    last = nc.tensor.transpose(PS[:, bank, (k - 4 * j) * P:(k - 4 * j) * P + kk], y[slot][0:kk, k, :],
                                               core.ident[0:kk, 0:kk])
            last.then_inc(turned.sem, 1)

        def landed_slot(b):
            return b[1] % y_bufs

        def landed_count(b):
            it, u = b
            return 32 * (it * (unroll // y_bufs) + u // y_bufs + 1)

        def brought(e, b, bank):
            v = b[1] % 2
            if e < q_fills:
                at = slice(e * q_wide, (e + 1) * q_wide)
                return [q[:, v, at] for q in qs], PS[:, bank, 0:q_wide], gain
            j = e - q_fills
            cols = min(512, KEYS - 512 * j)
            return [t[:, v, 512 * j:512 * j + cols] for t in yT], PS[:, bank, 0:cols], None

        def act_bring(act, e, b, number, bank):
            (lead, _), fill, factor = brought(e, b, bank)
            act.wait_ge(turned.sem, turned.at(number + 1))
            if factor is None:
                nc.scalar.copy(lead, fill).then_inc(t_act.sem, 1)
            else:
                nc.scalar.activation(lead, fill, ACT.Identity, scale=factor[:, 0:1]).then_inc(t_act.sem, 1)

        def dve_bring(dve, e, b, number, bank):
            (lead, rest), fill, factor = brought(e, b, bank)
            dve.wait_ge(t_act.sem, t_act.at(number + 1))
            if factor is None:
                nc.vector.tensor_tensor(rest, fill, lead, ALU.subtract).then_inc(t_dve.sem, 1)
            else:
                nc.vector.scalar_tensor_tensor(rest, fill, factor[:, 0:1], lead, ALU.mult,
                                               ALU.subtract).then_inc(t_dve.sem, 1)

        def bring_step(one, eng, it, local):
            if brings(it, local):
                b = (it, local // pairs + 1)
                for x in range(per_step):
                    one(eng, (local % pairs) * per_step + x, b, bring_number(it, local, x), bring_bank(it, local, x))

        def bring_first(one, eng):
            for e in range(ahead):
                one(eng, e, (0, 0), e, 4 + e % 2)

        def out_due(local, first):
            return (local - 2) % per_group == 0 and alive(local, first, 2 * per_group + 2)

        def pe_scores(pe, it, local, first):
            n, p, v = it * per_turn + local, local % pairs, (local // pairs) % 2
            if p == 0:
                brought_all = ahead if first and local == 0 else bring_number(it, local - 1, per_step - 1) + 1
                pe.wait_ge(t_dve.sem, t_dve.at(brought_all + 2))
            for half in range(2):
                if not (first and local == 0):
                    pe.wait_ge(e_done.sem, e_done.at(n * 2 - 1 + half))
                for j in (2 * half, 2 * half + 1):
                    if j == 3 and out_due(local, first):
                        pe_out(pe, it, local)
                    cols = min(512, even - 512 * j)
                    for m, (a, b) in enumerate(PRODUCTS):
                        last = nc.tensor.matmul(S[:, 512 * j:512 * j + cols], qs[a][:, v, p * P:(p + 1) * P],
                                                yT[b][:, v, 512 * j:512 * j + cols], start=(m == 0), stop=(m == 2))
                last.then_inc(s_ready.sem, 1)

        def pe_turn(pe, it, local, half):
            pe.wait_ge(e_done.sem, e_done.at((it * per_turn + local) * 2 - 1 + half))
            for j in (2 * half, 2 * half + 1):
                wait_fill(pe, turn_number(it, local, j), 2 if per_step == 1 and half == 1 and brings(it, local) else 1)
                for k in range(4 * j, min(4 * j + 4, KT)):
                    kk = keys_in(k)
                    last = nc.tensor.transpose(PS[0:kk, turn_bank(it, local, j), (k - 4 * j) * P:(k - 4 * j + 1) * P],
                                               probs[:, (local - 1) % 2, k * P:k * P + kk], core.ident[:])
                last.then_inc(turned.sem, 1)

        def pe_weighted(pe, it, local):
            part = (local - 1) % per_group
            back = local - 1 - part - per_group
            u = (back // pairs) % 2
            par = (back // per_group) % 2
            if part == 0:
                pe.wait_ge(t_dve.sem, t_dve.at(turn_number(it, local - 1, 3) + 3))
                pe.wait_ge(y_split.sem, y_split.at(it * unroll + back // pairs + 1))
                pe.wait_ge(o_taken.sem, o_taken.at(it * groups + back // per_group + 1))
            for k in parts[part]:
                kk = keys_in(k)
                for m, (a, b) in enumerate(PRODUCTS):
                    last = nc.tensor.matmul(O_ps, yp[a][0:kk, u, k, :], probsT[b][0:kk, par, k, :],
                                            start=(k == 0 and m == 0), stop=(k == KT - 1 and m == 2))
            if part == per_group - 1:
                last.then_inc(o_ready.sem, 1)

        def pe_out(pe, it, local):
            back = local - 2 - 2 * per_group
            g = it * groups + back // per_group
            par = (back // per_group) % 2
            pe.wait_ge(o_taken.sem, o_taken.at(g + 2))
            pe.wait_ge(f_taken.sem, f_taken.at(g * heads_in + heads_in))
            for m in range(per_group):
                last = nc.tensor.matmul(F_ps[:, m], OT[:, par, m * P:(m + 1) * P], wv_of((back + m) % pairs),
                                        start=True, stop=True)
            last.then_inc(f_ready.sem, 1)

        def turned_part(part, it, local, j):
            k0, k1 = 4 * j, min(4 * j + 4, KT)
            kk = keys_in(k0)
            m = (local - 1) % per_group
            return (probsT[part][0:kk, ((local - 1) // per_group) % 2, k0:k1, m * P:(m + 1) * P],
                    PS[0:kk, turn_bank(it, local, j), 0:(k1 - k0) * P].rearrange("p (k r) -> p k r", r=P))

        def act_turn(act, it, local, half):
            for j in (2 * half, 2 * half + 1):
                out, bank = turned_part(0, it, local, j)
                act.wait_ge(turned.sem, turned.at(turn_number(it, local, j) + 1))
                nc.scalar.copy(out, bank).then_inc(t_act.sem, 1)

        def act_exp(act, it, local, half):
            if half == 0:
                act.wait_ge(m_ready.sem, m_ready.at(it * per_turn + local + 1))
            cols = halves[half]
            nc.scalar.activation(probs[:, local % 2, cols], S[:, cols], ACT.Exp, bias=bias[:, local % 2:local % 2 + 1],
                                 scale=scale, accum_out=total[:, local, half:half + 1]).then_inc(e_done.sem, 1)

        def dve_turn(dve, it, local, half):
            for j in (2 * half, 2 * half + 1):
                lead, _ = turned_part(0, it, local, j)
                rest, bank = turned_part(1, it, local, j)
                dve.wait_ge(t_act.sem, t_act.at(turn_number(it, local, j) + 1))
                nc.vector.tensor_tensor(rest, bank, lead, ALU.subtract).then_inc(t_dve.sem, 1)

        stats_parts = (range(0, 4), range(4, KT - 3), range(KT - 3, KT))

        def dve_stats(dve, b, part):
            slot, n = landed_slot(b), b[0] * unroll + b[1]
            ks = stats_parts[part]
            if part == 0:
                dve.wait_ge(y_landed[slot].sem, y_landed[slot].at(landed_count(b)))
            for k in ks:
                kk = keys_in(k)
                nc.vector.bn_stats(stats[0:kk, k, :], y[slot][0:kk, k, :]).then_inc(stats_step.sem, 1)
            dve.wait_ge(stats_step.sem, stats_step.at(n * 2 * KT + ks[0] * 2 + len(ks)))
            dve.sem_inc(stats_begun.sem, 1)
            for k in ks:
                kk = keys_in(k)
                nc.vector.bn_aggr(moments[0:kk, k, :], stats[0:kk, k, :]).then_inc(stats_step.sem, 1)
            if part == 2:
                dve.wait_ge(stats_step.sem, stats_step.at(n * 2 * KT + 2 * KT))
                nc.vector.tensor_scalar(rstd[:], moments[:, :, 1], EPS, None, ALU.add).then_inc(var_ready.sem, 1)

        def dve_weighted(dve, it, local):
            back = local - 2 * per_group
            g = it * groups + back // per_group
            slot = back % per_turn
            inv = inverse[:, (back // per_group) % 4, :]
            nc.vector.tensor_reduce(inv, total[:, slot:slot + per_group, :], AX_X, ALU.add).then_inc(sum_done.sem, 1)
            dve.wait_ge(sum_done.sem, sum_done.at(g + 1))
            nc.vector.reciprocal(inv, inv).then_inc(inv_done.sem, 1)
            dve.wait_ge(o_ready.sem, o_ready.at(g + 1))
            nc.vector.tensor_copy(OT[:, (back // per_group) % 2, :], O_ps).then_inc(o_taken.sem, 1)

        def dve_max(dve, it, local, first):
            n, q = it * per_turn + local, local % 2
            for half, cols in enumerate(halves):
                dve.wait_ge(s_ready.sem, s_ready.at(n * 2 + half + 1))
                nc.vector.tensor_reduce(top[:, q, half:half + 1], S[:, cols], AX_X, ALU.max).then_inc(step.sem, 1)
            if out_due(local, first):
                dve_out(dve, it, local)
            dve.wait_ge(step.sem, step.at(n * 2 + 2))
            nc.vector.tensor_scalar(bias[:, q:q + 1], top[:, q, 0:1], top[:, q, 1:2], -scale, ALU.max,
                                    ALU.mult).then_inc(m_ready.sem, 1)

        def dve_out(dve, it, local):
            back = local - 2 - 2 * per_group
            g = it * groups + back // per_group
            pair0 = back % pairs
            b = it * unroll + back // pairs
            inv = inverse[:, (back // per_group) % 4, :]
            dve.wait_ge(inv_done.sem, inv_done.at(g + 1))
            dve.wait_ge(f_ready.sem, f_ready.at(g + 1))
            for a in range(heads_in):
                r = slice(a * SEQ, (a + 1) * SEQ)
                nc.vector.tensor_tensor(sums[r, bass.ds(b, 1), pair0:pair0 + per_group, :].rearrange("p x g d -> p (x g) d"),
                                        F_ps[r, :, a, :], inv[r, :].unsqueeze(2).broadcast_to([SEQ, per_group, d_out]),
                                        ALU.mult).then_inc(f_taken.sem, 1)

        def alive(local, first, back):
            return not first or local >= back

        def stats_due(it, local, tail):
            return norm and not tail and brings(it, local) and local % pairs < len(stats_parts)

        def turns_pair(local, first, tail):
            return alive(local, first, 1) and not (tail and local > per_turn)

        def pe_step(pe, it, local, first, tail):
            if not tail:
                pe_scores(pe, it, local, first)
            if turns_pair(local, first, tail):
                pe_turn(pe, it, local, 0)
            if tail and out_due(local, first):
                pe.wait_ge(e_done.sem, e_done.at(2 * steps_all))
                pe_out(pe, it, local)
            if alive(local, first, per_group + 1) and not (tail and local > per_turn + per_group):
                pe_weighted(pe, it, local)
            if not tail:
                bring_step(pe_bring, pe, it, local)
            if turns_pair(local, first, tail):
                pe_turn(pe, it, local, 1)

        def act_step(act, it, local, first, tail):
            if turns_pair(local, first, tail):
                act_turn(act, it, local, 0)
            if not tail:
                act_exp(act, it, local, 0)
                if per_step > 1:
                    act_exp(act, it, local, 1)
                bring_step(act_bring, act, it, local)
                if per_step == 1:
                    act_exp(act, it, local, 1)
            if turns_pair(local, first, tail):
                act_turn(act, it, local, 1)

        def dve_step(dve, it, local, first, tail):
            if not tail:
                dve_max(dve, it, local, first)
            if tail and out_due(local, first):
                dve_out(dve, it, local)
            if turns_pair(local, first, tail):
                dve_turn(dve, it, local, 0)
            if not tail:
                bring_step(dve_bring, dve, it, local)
            if stats_due(it, local, tail):
                dve_stats(dve, (it, local // pairs + 1), local % pairs)
            if turns_pair(local, first, tail):
                dve_turn(dve, it, local, 1)
            if local % per_group == 0 and alive(local, first, 2 * per_group) and not (tail and local > per_turn + per_group):
                dve_weighted(dve, it, local)

        def run(eng, one, bring):
            bring_first(bring, eng)
            for local in range(per_turn):
                one(eng, 0, local, True, False)
            with eng.Fori(1, turns - 1) as it:
                for local in range(per_turn):
                    one(eng, it, local, False, False)
            for local in range(per_turn + per_group + 3):
                one(eng, turns - 1, local, False, local >= per_turn)

        def load(sp, b, slot):
            for dst, src, landed in room.rows(core, b, slot):
                sp.dma_start(dst, src).then_inc(landed.sem, 16)

        def stage(sp, b, slot):
            for i in range(blocks):
                r = slice(i * P // blocks, (i + 1) * P // blocks)
                sp.dma_start(q_tile[r, slot, :, i * SEQ:(i + 1) * SEQ],
                             qT[r, :, bass.ds(b * SEQ, SEQ)]).then_inc(q_staged[slot].sem, 16)

        def reload(sp, b, u):
            before, q_next = b - y_bufs, b + 2 - y_bufs
            first = isinstance(before, int) and before == 0
            sp.wait_ge(turned.sem, turned.at(ahead if first else before * (pairs * (4 + per_step)) + (ahead - 4)))
            if not (isinstance(b, int) and q_next == BATCH):
                stage(sp, q_next, (u + 2 - y_bufs) % 2)
            sp.wait_ge(y_split.sem, y_split.at(b - y_bufs + 1))
            load(sp, b, u % y_bufs)

        def split_rows(pool, it, u):
            b, slot, v = (it, u), landed_slot((it, u)), u % 2
            cuts = ((slice(0, P), slice(0, KT - 1)), (slice(0, KLAST), slice(KT - 1, KT)))
            if norm:
                n = it * unroll + u
                pool.wait_ge(var_ready.sem, var_ready.at(n + 1))
                nc.gpsimd.tensor_tensor(rstd[:], rstd[:], minus_half[:], ALU.pow).then_inc(dev_ready.sem, 1)
                pool.wait_ge(dev_ready.sem, dev_ready.at(n + 1))
                wide = [(y[slot][r, k, :], moments[r, k, 0:1], rstd[r, k].unsqueeze(2), [r.stop, k.stop - k.start, CDIM])
                        for r, k in cuts]
                for rows, mean, _, to in wide:
                    nc.gpsimd.tensor_tensor(rows, rows, mean.broadcast_to(to), ALU.subtract).then_inc(centred.sem, 1)
                pool.wait_ge(centred.sem, centred.at(n * 2 + 2))
                for rows, _, scale_by, to in wide:
                    nc.gpsimd.tensor_tensor(rows, rows, scale_by.broadcast_to(to), ALU.mult).then_inc(y_normal.sem, 1)
                pool.wait_ge(y_normal.sem, y_normal.at(n * 2 + 2))
            else:
                pool.wait_ge(y_landed[slot].sem, y_landed[slot].at(landed_count(b)))
            if not (isinstance(it, int) and it == 0 and u < 2):
                pool.wait_ge(o_ready.sem, o_ready.at((it * unroll + u - 1) * groups_batch))
            pool.sem_inc(y_begun.sem, 1)
            for r, k in cuts:
                nc.gpsimd.tensor_copy(yp[0][r, v, k, :], y[slot][r, k, :]).then_inc(y_lead.sem, 1)
            pool.wait_ge(y_lead.sem, y_lead.at((it * unroll + u) * 2 + 2))
            for n, (r, k) in enumerate(cuts):
                ins = nc.gpsimd.tensor_tensor(yp[1][r, v, k, :], y[slot][r, k, :], yp[0][r, v, k, :], ALU.subtract)
            ins.then_inc(y_split.sem, 1)

        with nc.Block() as block:
            @block.sync
            def _(sp):
                for b in range(2):
                    stage(sp, b, b)
                for b in range(y_bufs, 4):
                    reload(sp, b, b % 2)
                with sp.Fori(2, BATCH // 2 - 1) as r:
                    for u in range(2):
                        reload(sp, r * 2 + u, u)
                for b in range(BATCH - 2, BATCH):
                    reload(sp, b, b % 2)

            @block.gpsimd
            def _(pool):
                for u in range(unroll):
                    split_rows(pool, 0, u)
                with pool.Fori(1, turns) as it:
                    for u in range(unroll):
                        split_rows(pool, it, u)

            @block.tensor
            def _(pe):
                wait_weights(core, pe)
                run(pe, pe_step, pe_bring)

            @block.scalar
            def _(act):
                wait_weights(core, act)
                nc.scalar.activation(warm[:], core.ident[0:1, 0:1], ACT.Exp)
                run(act, act_step, act_bring)

            @block.vector
            def _(dve):
                wait_weights(core, dve)
                for t in yT:
                    nc.vector.memset(t[:, :, KEYS:even].bitcast(F32), 0.0)
                if q_cols < pairs * P:
                    for q in qs:
                        nc.vector.memset(q[:, :, q_cols:].bitcast(F32), 0.0)
                dve.sem_inc(t_dve.sem, 2)
                dve.sem_inc(o_taken.sem, 1)
                dve.sem_inc(f_taken.sem, heads_in)
                if norm:
                    nc.vector.memset(minus_half[:], -0.5)
                    nc.vector.memset(moments[:], 0.0)
                    for part in range(len(stats_parts)):
                        dve_stats(dve, (0, 0), part)
                run(dve, dve_step, dve_bring)
    for s in y_landed:
        s.passed(32 * BATCH // y_bufs)
    for s in q_staged:
        s.passed(16 * blocks * BATCH // 2)
    if norm:
        stats_step.passed(2 * KT * BATCH)
        for n in (var_ready, dev_ready):
            n.passed(BATCH)
        stats_begun.passed(len(stats_parts) * BATCH)
        y_normal.passed(2 * BATCH)
        centred.passed(2 * BATCH)
    m_ready.passed(steps_all)
    for n in (s_ready, e_done, step):
        n.passed(2 * steps_all)
    y_lead.passed(2 * BATCH)
    y_split.passed(BATCH)
    y_begun.passed(BATCH)
    fills = 4 * steps_all + ahead * BATCH
    turned.passed(fills)
    t_act.passed(fills)
    t_dve.passed(fills + 2)
    o_ready.passed(groups_all)
    o_taken.passed(groups_all + 1)
    f_ready.passed(groups_all)
    f_taken.passed(groups_all * heads_in + heads_in)
    sum_done.passed(groups_all)
    inv_done.passed(groups_all)


def head_queries(wkT):
    return lambda j, q: [(slice(0, 4 * SEQ), wkT[:, j, :], q[:, j, :], True, True)]


def turn_sums(core, sums, pairs, d, dst, shift, loads=()):
    nc, PS = core.nc, core.PS
    ready, by_act, by_dve = core.semaphore("fill_ready"), core.semaphore("fill_taken_act"), core.semaphore("fill_taken_dve")
    chunks = pairs * d // P
    flat = sums[:].rearrange("p b h d -> p b (h d)")
    fills = chunks * (BATCH // 4)

    def place(f, half):
        c, b4 = f // (BATCH // 4), f % (BATCH // 4)
        k = half * chunks + c
        out = dst[:, k, b4 * 4 * SEQ:(b4 + 1) * 4 * SEQ].rearrange("p (b s) -> p b s", s=SEQ)
        bank = PS[:, f % BANKS, :].rearrange("p (b a s) -> p b a s", b=4, a=2)[:, :, half, :]
        return out, bank, shift[:, k:k + 1]

    with nc.Block() as block:
        start_loads(block, loads)

        @block.tensor
        def _(pe):
            for f in range(fills):
                c, b4 = f // (BATCH // 4), f % (BATCH // 4)
                if f >= BANKS:
                    by = by_act if f % 2 == 0 else by_dve
                    pe.wait_ge(by.sem, by.at(2 * ((f - BANKS) // 2 + 1)))
                for j in range(4):
                    last = nc.tensor.transpose(PS[:, f % BANKS, j * P:(j + 1) * P],
                                               flat[:, b4 * 4 + j, c * P:(c + 1) * P], core.ident[:])
                last.then_inc(ready.sem, 1)

        @block.scalar
        def _(act):
            wait_weights(core, act)
            for f in range(0, fills, 2):
                act.wait_ge(ready.sem, ready.at(f + 1))
                for half in range(2):
                    out, bank, bias = place(f, half)
                    nc.scalar.activation(out, bank, ACT.Identity, bias=bias).then_inc(by_act.sem, 1)

        @block.vector
        def _(dve):
            wait_weights(core, dve)
            for f in range(1, fills, 2):
                dve.wait_ge(ready.sem, ready.at(f + 1))
                for half in range(2):
                    out, bank, bias = place(f, half)
                    nc.vector.tensor_scalar(out, bank, bias, None, ALU.add).then_inc(by_dve.sem, 1)
    for s in (ready, by_act, by_dve):
        s.passed(fills)


def mlp(core, pre, rows, extra=[]):
    with ExitStack() as own:
        shapes = {"ln3_g": [P, DC], "ln3_b": [P, DC], "li2_w": [P, DC, 4 * DIM], "li2_b": [P, 4 * DC],
                  "li3_w": [P, 4 * DC, DIM], "li3_b": [1, DIM]}
        w = weights(core, own, pre, **shapes)
        hat = core.sb(own, "hat", [P, TILES, DIM])
        hatT = core.sb(own, "hat_turned", [P, DC, TOKENS])
        inner = core.sb(own, "inner", [P, 4 * DC, TOKENS])
        normalize(core, rows, hat, loads=w.loads + extra)
        turn(core, hat, DC, hatT, w["ln3_g"], w["ln3_b"])
        linear_turned(core, hatT, w["li2_w"], inner, w["li2_b"], ACT.Gelu)
        linear_rows(core, inner, w["li3_w"], rows, w["li3_b"], rows)


def l0_xattn(core):
    X, nc = core.X, core.nc
    with ExitStack() as layer:
        U = core.sb(layer, "u", [P, TILES, DIM])
        with ExitStack() as own:
            ln = weights(core, own, L0_xattn_ln1_g=[P, DIM], L0_xattn_ln1_b=[P, DIM])
            normalize(core, X, U, loads=ln.loads)
            normalize(core, U, U, ln["L0_xattn_ln1_g"], ln["L0_xattn_ln1_b"])
        for a, heads, d in (("a1", 16, 32), ("a2", 16, 32)):
            inner = heads * d
            pre = f"L0_xattn_{a}_"
            with ExitStack() as own:
                cy = DIM if a == "a1" else CDIM
                shapes = {"wv": [P, cy // P, inner],
                          "lnx_g": [P, DC], "lnx_b": [P, DC], "lny_g": [P, cy // P], "lny_b": [P, cy // P]}
                if a == "a1":
                    ln = weights(core, own, L0_xattn_ln2_g=[P, DIM], L0_xattn_ln2_b=[P, DIM], causal=[P, SEQ])
                    shapes.update({"wq": [P, DC, inner], "wk": [P, DC, inner], "li1_w": [P, inner // P, DIM], "li1_b": [1, DIM]})
                else:
                    shapes["wkT"] = [P, inner // P, CDIM]
                w = weights(core, own, pre, **shapes)
                if a == "a1":
                    R = core.sb(own, "r", [P, TILES, DIM])
                    with ExitStack() as work:
                        hat = core.sb(work, "hat", [P, TILES, DIM])
                        normT = core.sb(work, "norm_turned", [P, DC, TOKENS])
                        qT = core.sb(work, "qT", [P, inner // P, TOKENS])
                        kT = core.sb(work, "kT", [P, inner // P, TOKENS])
                        V = core.sb(work, "v", [P, TILES, inner])
                        O = core.sb(work, "o", [P, TILES, inner])
                        normalize(core, U, hat, loads=w.loads + ln.loads)
                        turn(core, hat, DC, normT, w["lnx_g"], w["lnx_b"])
                        linear_turned(core, normT, w["wq"], qT)
                        turn(core, hat, DC, normT, w["lny_g"], w["lny_b"])
                        linear_turned(core, normT, w["wk"], kT)
                        linear_rows(core, normT, w["wv"], V)
                        self_attention(core, qT, kT, V, O, heads, d, d, d ** -0.5, mask=ln["causal"])
                        turn(core, O, inner // P, qT)
                        linear_rows(core, qT, w["li1_w"], R, w["li1_b"], U)
                    mlp(core, pre, R)
                    add(core, U, U, R)
                    normalize(core, U, U, ln["L0_xattn_ln2_g"], ln["L0_xattn_ln2_b"])
                else:
                    with ExitStack() as work:
                        sums = core.sb(work, "sums", [P, BATCH, heads // 2, d])
                        vb = core.sb(work, "v_bias", [P, inner // P])
                        wv = core.sb(work, "wv_scaled", [P, inner])
                        qT = core.sb(work, "qT", [P, inner // P, TOKENS])
                        rows = X[:].rearrange("p t d -> p (t d)")[:, 0:KT * CDIM].rearrange("p (k c) -> p k c", c=CDIM)
                        room = ContextRoom(core, work, 2, inner // P, P // d, [rows])
                        with ExitStack() as front:
                            wq = weights(core, front, pre, wq=[P, DC, inner])
                            hat = core.sb(front, "hat", [P, TILES, DIM])
                            normT = core.sb(front, "norm_turned", [P, DC, TOKENS])
                            normalize(core, U, hat, loads=w.loads + wq.loads + room.loads, clear=room.q_tile)
                            turn(core, hat, DC, normT, w["lnx_g"], w["lnx_b"])
                            linear_turned(core, normT, wq["wq"], qT)
                        value_affine(core, w["wv"], w["lny_g"], w["lny_b"], wv, vb)
                        wv5 = wv[:].rearrange("c (a p d) -> c p a d", a=2, d=d)
                        context_attention(core, room, qT, head_queries(w["wkT"]), 4, heads * SEQ, True, w["lny_g"], lambda pair: wv5[:, pair],
                                          sums, heads // 2, 2, 2, 2, d ** -0.5, d)
                        R = core.sb(work, "r", [P, TILES, DIM])
                        with ExitStack() as back:
                            oT = core.sb(back, "oT", [P, inner // P, TOKENS])
                            li1 = weights(core, back, pre, li1_w=[P, inner // P, DIM], li1_b=[1, DIM])
                            turn_sums(core, sums, heads // 2, d, oT, vb, li1.loads)
                            linear_rows(core, oT, li1["li1_w"], R, li1["li1_b"], U)
                        landed = core.semaphore("weights_landed")
                        residual = (X[:], core.dram["x"].rearrange("(t p) d -> p t d", p=P), landed)
                        landed.passed(16)
                        mlp(core, pre, R, [residual])
                        vector_steps(core, [lambda: nc.vector.tensor_tensor(R[:], R[:], U[:], ALU.add),
                                            lambda: nc.vector.tensor_tensor(X[:], X[:], R[:], ALU.add)])


def value_affine(core, wv, gain, shift, scaled, bias):
    nc, PS = core.nc, core.PS
    ready, step = core.semaphore("rows_ready"), core.semaphore("vector_step")
    chunks = bias.shape[1]
    with nc.Block() as block:
        @block.tensor
        def _(pe):
            wait_weights(core, pe)
            for k in range(chunks):
                last = nc.tensor.matmul(PS[:, k, 0:1], wv[:, 0, k * P:(k + 1) * P], shift[:, 0:1], start=True, stop=True)
            last.then_inc(ready.sem, 1)

        @block.vector
        def _(dve):
            wait_weights(core, dve)
            nc.vector.tensor_scalar(scaled[:], wv[:, 0, :], gain[:, 0:1], None, ALU.mult).then_inc(step.sem, 1)
            dve.wait_ge(ready.sem, ready.at(1))
            nc.vector.tensor_copy(bias[:], PS[:, 0:chunks, 0]).then_inc(step.sem, 1)
    ready.passed(1)
    step.passed(2)


def l0_attn(core):
    nc, X = core.nc, core.X
    heads, d, dv, pad = 8, 16, 32, 32
    with ExitStack() as own:
        w = weights(core, own, L0_attn_Wq=[P, DC, 2 * heads * pad], L0_attn_Wk=[P, DC, 2 * heads * pad],
                    L0_attn_Wv=[P, DC, DIM], L0_attn_Wo=[P, DC, DIM], L0_attn_lq1=[P, d], L0_attn_lk1=[P, d],
                    L0_attn_lq2=[P, d], L0_attn_lk2=[P, d], L0_attn_ln_g=[P, dv], L0_attn_ln_b=[P, dv])
        U = core.sb(own, "u", [P, TILES, DIM])
        uT = core.sb(own, "uT", [P, DC, TOKENS])
        qT = core.sb(own, "qT", [P, 4, TOKENS])
        kT = core.sb(own, "kT", [P, 4, TOKENS])
        V = core.sb(own, "v", [P, TILES, DIM])
        O = core.sb(own, "o", [P, TILES, DIM])
        lam = core.sb(own, "lam", [P, 4])
        normalize(core, X, U, loads=w.loads)
        turn(core, U, DC, uT)
        linear_turned(core, uT, w["L0_attn_Wq"], qT)
        linear_turned(core, uT, w["L0_attn_Wk"], kT)
        linear_rows(core, uT, w["L0_attn_Wv"], V)
        v = nc.vector
        vector_steps(core, [
            lambda: v.tensor_tensor(w["L0_attn_lq1"][:], w["L0_attn_lq1"][:], w["L0_attn_lk1"][:], ALU.mult),
            lambda: v.tensor_reduce(lam[:, 0:1], w["L0_attn_lq1"][:], AX_X, ALU.add),
            lambda: v.tensor_tensor(w["L0_attn_lq2"][:], w["L0_attn_lq2"][:], w["L0_attn_lk2"][:], ALU.mult),
            lambda: v.tensor_reduce(lam[:, 1:2], w["L0_attn_lq2"][:], AX_X, ALU.add)])
        scalar_step(core, lambda: nc.scalar.activation(lam[:, 0:2], lam[:, 0:2], ACT.Exp))
        vector_steps(core, [
            lambda: v.tensor_tensor(lam[:, 2:3], lam[:, 1:2], lam[:, 0:1], ALU.subtract),
            lambda: v.tensor_scalar(lam[:, 2:3], lam[:, 2:3], -LAM_INIT, None, ALU.add)])
        self_attention(core, qT, kT, V, O, 2 * heads, pad, dv, d ** -0.5, minus_lam=lam[:, 2:3])
        rows = TILES * heads
        O4 = O[:].rearrange("p t (h d) -> p (t h) d", d=dv)
        U4 = U[:].rearrange("p t (h d) -> p (t h) d", d=dv)
        mean = core.sb(own, "mean", [P, rows])
        var = core.sb(own, "variance", [P, rows])
        over = lambda a: a[:].unsqueeze(2).broadcast_to([P, rows, dv])
        along = lambda a: a[:].unsqueeze(1).broadcast_to([P, rows, dv])
        vector_steps(core, [
            lambda: v.tensor_reduce(mean[:], O4, AX_X, ALU.add),
            lambda: v.tensor_scalar(mean[:], mean[:], 1.0 / dv, None, ALU.mult),
            lambda: v.tensor_tensor(O4, O4, over(mean), ALU.subtract),
            lambda: v.tensor_tensor(U4, O4, O4, ALU.mult),
            lambda: v.tensor_reduce(var[:], U4, AX_X, ALU.add),
            lambda: v.tensor_scalar(var[:], var[:], 1.0 / dv, EPS, ALU.mult, ALU.add)])
        scalar_step(core, lambda: nc.scalar.activation(var[:], var[:], ACT.Sqrt))
        vector_steps(core, [
            lambda: v.reciprocal(var[:], var[:]),
            lambda: v.tensor_tensor(O4, O4, over(var), ALU.mult),
            lambda: v.tensor_tensor(O4, O4, along(w["L0_attn_ln_g"]), ALU.mult),
            lambda: v.tensor_tensor(O4, O4, along(w["L0_attn_ln_b"]), ALU.add)])
        turn(core, O, DC, uT)
        linear_rows(core, uT, w["L0_attn_Wo"], X, None, X)


def scalar_step(core, run):
    nc, step = core.nc, core.semaphore("scalar_step")
    with nc.Block() as block:
        @block.scalar
        def _(act):
            wait_weights(core, act)
            run().then_inc(step.sem, 1)
    step.passed(1)


def top_two(core, own, scores, iota):
    nc, step = core.nc, core.semaphore("vector_step")
    best = core.sb(own, "best", [P, TILES, 8])
    place = core.sb(own, "place", [P, TILES, 8], U32)
    placef = core.sb(own, "place_f", [P, TILES, 8])
    first = core.sb(own, "first", [P, TILES, EXPERTS])
    second = core.sb(own, "second", [P, TILES, EXPERTS])
    with nc.Block() as block:
        @block.vector
        def _(dve):
            for t in range(TILES):
                nc.vector.max(best[:, t, :], scores[:, t, :]).then_inc(step.sem, 1)
            dve.wait_ge(step.sem, step.at(TILES))
            for t in range(TILES):
                nc.vector.max_index(place[:, t, :], best[:, t, :], scores[:, t, :]).then_inc(step.sem, 1)
            dve.wait_ge(step.sem, step.at(2 * TILES))
            nc.vector.tensor_copy(placef[:], place[:]).then_inc(step.sem, 1)
            dve.wait_ge(step.sem, step.at(2 * TILES + 1))
            wait_weights(core, dve)
            for n, out in enumerate((first, second)):
                nc.vector.tensor_tensor(out[:], iota[:].unsqueeze(1).broadcast_to([P, TILES, EXPERTS]),
                                        placef[:, :, n:n + 1].broadcast_to([P, TILES, EXPERTS]),
                                        ALU.is_equal).then_inc(step.sem, 1)
    step.passed(2 * TILES + 3)
    return best, first, second


def spread(a):
    return a.broadcast_to([P, TILES, EXPERTS])


def gate_bias(core, gates, b2, acc):
    nc, PS = core.nc, core.PS
    ready, taken, rows_ready, rows_taken = (core.semaphore("fill_ready"), core.semaphore("fill_taken_act"),
                                            core.semaphore("rows_ready"), core.semaphore("rows_taken"))
    with ExitStack() as own:
        gT = core.sb(own, "gates_turned", [EXPERTS, TILES, P])
        with nc.Block() as block:
            @block.tensor
            def _(pe):
                wait_weights(core, pe)
                for t in range(TILES):
                    last = nc.tensor.transpose(PS[0:EXPERTS, t // 4, (t % 4) * P:(t % 4 + 1) * P], gates[:, t, :], core.ident[:])
                last.then_inc(ready.sem, 1)
                pe.wait_ge(taken.sem, taken.at(1))
                for t in range(TILES):
                    last = nc.tensor.matmul(PS[:, 2 + t // 2, (t % 2) * DIM:(t % 2 + 1) * DIM], gT[:, t, :], b2[:], start=True, stop=True)
                last.then_inc(rows_ready.sem, 1)

            @block.scalar
            def _(act):
                act.wait_ge(ready.sem, ready.at(1))
                nc.scalar.copy(gT[:].rearrange("e t p -> e (t p)"),
                               PS[0:EXPERTS, 0:2, :].rearrange("e b n -> e (b n)")).then_inc(taken.sem, 1)

            @block.vector
            def _(dve):
                dve.wait_ge(rows_ready.sem, rows_ready.at(1))
                nc.vector.tensor_copy(acc[:].rearrange("p t d -> p (t d)"),
                                      PS[:, 2:6, :].rearrange("p b n -> p (b n)")).then_inc(rows_taken.sem, 1)
    for s in (ready, taken, rows_ready, rows_taken):
        s.passed(1)


class Experts:

    def __init__(self, core, own, w1, w2, b1, wm=None, bm=None, gain=None, shift=None):
        self.core, self.source = core, {"up": w1, "down": w2}
        if wm is not None:
            self.source["second"] = wm
        sizes = {"up": [P, DC, 4 * DIM], "second": [P, DC, 4 * DIM], "down": [P, 4 * DC, DIM]}
        self.raw = {k: core.sb(own, "raw_" + k, sizes[k]) for k in self.source}
        self.parts = {k: [core.sb(own, "part_" + k, sizes[k], F32R) for _ in range(2)] for k in self.source}
        self.landed = {k: core.semaphore("expert_landed_" + k) for k in self.source}
        self.loads = [(self.raw[k][:], self.source[k][0], self.landed[k]) for k in self.source]
        landed = core.semaphore("weights_landed")

        def vectors(name, v, more=0):
            if v is None:
                return None
            t = core.sb(own, name, [P, EXPERTS + more, v.shape[2]])
            cuts = [(t[:, 0:EXPERTS], v)] + ([(t[:, EXPERTS:], v[0:more])] if more else [])
            self.loads += [(dst, src.rearrange("e p f -> p e f"), landed) for dst, src in cuts]
            landed.passed(16 * len(cuts))
            return t

        self.b1, self.bm = vectors("b1", b1), vectors("bm", bm)
        self.gain, self.shift = vectors("gain", gain, 1), vectors("shift", shift, 1)

    def load(self, sp, k, e):
        sp.dma_start(self.raw[k][:], self.source[k][bass.ds(e, 1)].squeeze(0)).then_inc(self.landed[k].sem, 16)


def experts(core, bank, xT, gates, acc, func):
    nc, PS = core.nc, core.PS
    FC = 4 * DC
    mult, affine = bank.bm is not None, bank.gain is not None
    b1s, bms, gs, ss = bank.b1, bank.bm, bank.gain, bank.shift
    up_names = ("up", "second") if mult else ("up",)
    begun, act_begun, w_lead = core.semaphore("split_begun"), core.semaphore("hidden_begun"), core.semaphore("weight_lead")
    up_lead = core.semaphore("up_weight_lead")
    split = {k: core.semaphore("weight_split_" + k) for k in bank.source}
    up_ready, up_act, up_dve = core.semaphore("up_ready"), core.semaphore("up_taken_act"), core.semaphore("up_taken_dve")
    a_lead, a_split = core.semaphore("hidden_lead"), core.semaphore("hidden_split")
    h_made, h_lead, h_split = core.semaphore("input_made"), core.semaphore("input_lead"), core.semaphore("input_split")
    down_ready, down_taken = core.semaphore("down_ready"), core.semaphore("down_taken")
    ups = FC * HALVES
    ring = 2 if mult else 4
    depth, outs = 4, 4
    makes = EXPERTS + 1 if affine else 1
    with ExitStack() as own:
        h32 = core.sb(own, "input", [P, DC, TOKENS]) if affine else xT
        h = [core.sb(own, "input_part", [P, DC, TOKENS], F32R) for _ in range(2)]
        a32 = core.sb(own, "hidden", [P, depth, 512])
        aT = [core.sb(own, "hidden_part", [P, FC, TOKENS], F32R) for _ in range(2)]
        warm = core.sb(own, "warm", [1, 1])
        def hidden_part(part, k):
            half, f = k // FC, k % FC
            return aT[part][:, f, half * 512:(half + 1) * 512]

        with nc.Block() as block:
            @block.sync
            def _(sp):
                with sp.Fori(1, EXPERTS) as e:
                    for k in bank.source:
                        sp.wait_ge(split[k].sem, split[k].at(e))
                        bank.load(sp, k, e)

            @block.gpsimd
            def _(pool):
                with pool.Fori(0, EXPERTS) as e:
                    for n, k in enumerate(up_names + ("down",)):
                        if k == "down":
                            pool.wait_ge(bank.landed[k].sem, bank.landed[k].at(e * 16 + 16))
                            pool.wait_ge(down_ready.sem, down_ready.at(e * TILES + 1))
                        else:
                            pool.wait_ge(up_lead.sem, up_lead.at(e * len(up_names) + n + 1))
                        pool.sem_inc(begun.sem, 1)
                        lead, rest = bank.parts[k]
                        if k == "down":
                            nc.gpsimd.tensor_copy(lead[:], bank.raw[k][:]).then_inc(w_lead.sem, 1)
                            pool.wait_ge(w_lead.sem, w_lead.at(e + 1))
                        nc.gpsimd.tensor_tensor(rest[:], bank.raw[k][:], lead[:], ALU.subtract).then_inc(split[k].sem, 1)

            @block.tensor
            def _(pe):
                pe.sem_inc(down_ready.sem, 1)
                pe.sem_inc(up_ready.sem, 1)
                with pe.Fori(0, EXPERTS) as e:
                    for k in up_names:
                        pe.wait_ge(split[k].sem, split[k].at(e + 1))
                    pe.wait_ge(h_split.sem, h_split.at((e + 1) * DC if affine else DC))
                    for k in range(ups):
                        half, f = k // FC, k % FC
                        by = up_dve if mult else up_act
                        pe.wait_ge(by.sem, by.at(e * ups + k + 1))
                        for x, name in enumerate(up_names):
                            for c in range(DC):
                                for m, (a, b) in enumerate(PRODUCTS):
                                    last = nc.tensor.matmul(PS[:, k % ring + 2 * x, :],
                                                            bank.parts[name][a][:, c, f * P:(f + 1) * P],
                                                            h[b][:, c, half * 512:(half + 1) * 512],
                                                            start=(c == 0 and m == 0), stop=(c == DC - 1 and m == 2))
                        last.then_inc(up_ready.sem, 1)
                    pe.wait_ge(split["down"].sem, split["down"].at(e + 1))
                    for t in range(TILES):
                        if t % 4 == 0:
                            pe.wait_ge(a_split.sem, a_split.at(e * ups + (t // 4 + 1) * FC + depth))
                        pe.wait_ge(down_taken.sem, down_taken.at(e * TILES + t + 1))
                        for f in range(FC):
                            for m, (a, b) in enumerate(PRODUCTS):
                                last = nc.tensor.matmul(PS[:, 4 + t % outs, 0:DIM], aT[a][:, f, t * P:(t + 1) * P],
                                                        bank.parts["down"][b][:, f, :],
                                                        start=(f == 0 and m == 0), stop=(f == FC - 1 and m == 2))
                        last.then_inc(down_ready.sem, 1)

            def lead_input(act, e):
                for c in range(DC):
                    if affine:
                        act.wait_ge(h_made.sem, h_made.at(e * DC + c + 1))
                    nc.scalar.copy(h[0][:, c, :], h32[:, c, :]).then_inc(h_lead.sem, 1)

            @block.scalar
            def _(act):
                nc.scalar.activation(warm[:], core.ident[0:1, 0:1], func)
                act.sem_inc(up_act.sem, ring)
                wait_weights(core, act)
                lead_input(act, 0)

                def lead_hidden(e, k):
                    by = up_dve if mult else up_act
                    act.wait_ge(by.sem, by.at(e * ups + k + 1 + ring))
                    nc.scalar.copy(hidden_part(0, k), a32[:, k % depth, :]).then_inc(a_lead.sem, 1)

                with act.Fori(0, EXPERTS) as e:
                    act.wait_ge(up_ready.sem, up_ready.at(e * ups + 1))
                    for k in up_names:
                        act.wait_ge(bank.landed[k].sem, bank.landed[k].at(e * 16 + 16))
                        nc.scalar.copy(bank.parts[k][0][:], bank.raw[k][:]).then_inc(up_lead.sem, 1)
                    for k in range(ups):
                        act.wait_ge(up_ready.sem, up_ready.at(e * ups + k + 2))
                        act.wait_ge(a_split.sem, a_split.at(e * ups + k + 1))
                        act.sem_inc(act_begun.sem, 1)
                        nc.scalar.activation(a32[:, k % depth, :], PS[:, k % ring, :], func,
                                             bias=b1s[:, bass.ds(e, 1), k % FC:k % FC + 1].squeeze(1)).then_inc(up_act.sem, 1)
                        if k:
                            lead_hidden(e, k - 1)
                    lead_hidden(e, ups - 1)
                    if affine:
                        lead_input(act, e + 1)

            def make_input(dve, e):
                for c in range(DC):
                    nc.vector.tensor_scalar(h32[:, c, :], xT[:, c, :], gs[:, bass.ds(e, 1), c:c + 1].squeeze(1),
                                            ss[:, bass.ds(e, 1), c:c + 1].squeeze(1), ALU.mult, ALU.add).then_inc(h_made.sem, 1)

            def split_input(dve, e):
                for c in range(DC):
                    dve.wait_ge(h_lead.sem, h_lead.at(e * DC + c + 1))
                    nc.vector.tensor_tensor(h[1][:, c, :], h32[:, c, :], h[0][:, c, :], ALU.subtract).then_inc(h_split.sem, 1)

            @block.vector
            def _(dve):
                dve.sem_inc(down_taken.sem, outs)
                dve.sem_inc(a_split.sem, depth)
                if mult:
                    dve.sem_inc(up_dve.sem, ring)
                wait_weights(core, dve)
                if affine:
                    make_input(dve, 0)
                split_input(dve, 0)

                def split_hidden(e, k):
                    dve.wait_ge(a_lead.sem, a_lead.at(e * ups + k + 1))
                    nc.vector.tensor_tensor(hidden_part(1, k), a32[:, k % depth, :], hidden_part(0, k),
                                            ALU.subtract).then_inc(a_split.sem, 1)

                with dve.Fori(0, EXPERTS) as e:
                    for k in range(ups):
                        if mult:
                            dve.wait_ge(up_act.sem, up_act.at(e * ups + k + 1 + ring))
                            a = a32[:, k % depth, :]
                            nc.vector.scalar_tensor_tensor(a, PS[:, k % ring + 2, :],
                                                           bms[:, bass.ds(e, 1), k % FC:k % FC + 1].squeeze(1), a,
                                                           ALU.add, ALU.mult).then_inc(up_dve.sem, 1)
                        if k:
                            split_hidden(e, k - 1)
                    split_hidden(e, ups - 1)
                    if affine:
                        dve.wait_ge(up_ready.sem, up_ready.at(e * ups + ups + 1))
                        dve.wait_ge(h_split.sem, h_split.at(e * DC + DC))
                        make_input(dve, e + 1)
                        split_input(dve, e + 1)
                    for t in range(TILES):
                        dve.wait_ge(down_ready.sem, down_ready.at(e * TILES + t + 2))
                        nc.vector.scalar_tensor_tensor(
                            acc[:, t, :], PS[:, 4 + t % outs, 0:DIM], gates[:, t, bass.ds(e, 1)], acc[:, t, :],
                            ALU.mult, ALU.add).then_inc(down_taken.sem, 1)
    for k in bank.source:
        bank.landed[k].passed(16 * EXPERTS)
        split[k].passed(EXPERTS)
    begun.passed(EXPERTS * len(split))
    act_begun.passed(EXPERTS * ups)
    w_lead.passed(EXPERTS)
    up_lead.passed(EXPERTS * len(up_names))
    up_ready.passed(ups * EXPERTS + 1)
    up_act.passed(ups * EXPERTS + ring)
    if mult:
        up_dve.passed(ups * EXPERTS + ring)
    a_lead.passed(ups * EXPERTS)
    a_split.passed(ups * EXPERTS + depth)
    if affine:
        h_made.passed(DC * makes)
    h_lead.passed(DC * makes)
    h_split.passed(DC * makes)
    down_ready.passed(TILES * EXPERTS + 1)
    down_taken.passed(TILES * EXPERTS + outs)


def l0_ffn(core):
    nc, X = core.nc, core.X
    v = nc.vector
    with ExitStack() as own:
        w = weights(core, own, L0_ffn_router_W=[P, DC, EXPERTS], L0_ffn_router_b=[1, EXPERTS], L0_ffn_b2=[EXPERTS, DIM],
                    iota8=[P, EXPERTS])
        d = core.dram
        bank = Experts(core, own, d["L0_ffn_W1"], d["L0_ffn_W2"], d["L0_ffn_b1"],
                       gain=d["L0_ffn_ln_g"], shift=d["L0_ffn_ln_b"])
        U = core.sb(own, "u", [P, TILES, DIM])
        hat = core.sb(own, "hat", [P, TILES, DIM])
        uT = core.sb(own, "uT", [P, DC, TOKENS])
        logits = core.sb(own, "logits", [P, TILES, EXPERTS])
        gates = core.sb(own, "gates", [P, TILES, EXPERTS])
        acc = core.sb(own, "acc", [P, TILES, DIM])
        share = core.sb(own, "share", [P, TILES, 2])
        whole = core.sb(own, "gate_sum", [P, TILES])
        normalize(core, X, U, loads=w.loads + bank.loads)
        turn(core, U, DC, uT)
        linear_rows(core, uT, w["L0_ffn_router_W"], logits, w["L0_ffn_router_b"])
        best, first, second = top_two(core, own, logits, w["iota8"])
        vector_steps(core, [lambda: v.tensor_tensor(share[:], best[:, :, 0:2], best[:, :, 0:1].broadcast_to([P, TILES, 2]), ALU.subtract)])
        scalar_step(core, lambda: nc.scalar.activation(share[:], share[:], ACT.Exp))
        vector_steps(core, [
            lambda: v.tensor_reduce(whole[:], share[:], AX_X, ALU.add),
            lambda: v.reciprocal(whole[:], whole[:]),
            lambda: v.tensor_tensor(share[:], share[:], whole[:].unsqueeze(2).broadcast_to([P, TILES, 2]), ALU.mult),
            lambda: v.tensor_tensor(first[:], first[:], spread(share[:, :, 0:1]), ALU.mult),
            lambda: v.tensor_tensor(second[:], second[:], spread(share[:, :, 1:2]), ALU.mult),
            lambda: v.tensor_tensor(gates[:], first[:], second[:], ALU.add)])
        gate_bias(core, gates, w["L0_ffn_b2"], acc)
        vector_steps(core, [
            lambda: v.tensor_reduce(whole[:], gates[:], AX_X, ALU.add),
            lambda: v.tensor_tensor(hat[:], U[:], whole[:].unsqueeze(2).broadcast_to([P, TILES, DIM]), ALU.mult),
            lambda: v.tensor_tensor(acc[:], acc[:], hat[:], ALU.add)])
        normalize(core, U, hat)
        turn(core, hat, DC, uT)
        experts(core, bank, uT, gates, acc, ACT.Gelu)
        add(core, X, X, acc)


def l1_ffn(core):
    nc, X = core.nc, core.X
    v = nc.vector
    with ExitStack() as own:
        w = weights(core, own, L1_ffn_router_w=[P, DC, EXPERTS], L1_ffn_w2_b=[EXPERTS, DIM], iota8=[P, EXPERTS])
        d = core.dram
        bank = Experts(core, own, d["L1_ffn_wg_w"], d["L1_ffn_w2_w"], d["L1_ffn_wg_b"],
                       d["L1_ffn_w1_w"], d["L1_ffn_w1_b"])
        U = core.sb(own, "u", [P, TILES, DIM])
        uT = core.sb(own, "uT", [P, DC, TOKENS])
        probs = core.sb(own, "probs", [P, TILES, EXPERTS])
        gates = core.sb(own, "gates", [P, TILES, EXPERTS])
        acc = core.sb(own, "acc", [P, TILES, DIM])
        top = core.sb(own, "top", [P, TILES])
        normalize(core, X, U, loads=w.loads + bank.loads)
        turn(core, U, DC, uT)
        linear_rows(core, uT, w["L1_ffn_router_w"], probs)
        softmax_experts(core, probs, top, None)
        best, first, second = top_two(core, own, probs, w["iota8"])
        vector_steps(core, [
            lambda: v.tensor_tensor(first[:], first[:], spread(best[:, :, 0:1]), ALU.mult),
            lambda: v.tensor_tensor(second[:], second[:], spread(best[:, :, 1:2]), ALU.mult),
            lambda: v.tensor_tensor(gates[:], first[:], second[:], ALU.add)])
        gate_bias(core, gates, w["L1_ffn_w2_b"], acc)
        experts(core, bank, uT, gates, acc, ACT.Gelu)
        add(core, X, X, acc)


def softmax_experts(core, scores, top, keep):
    nc = core.nc
    v = nc.vector
    wide = lambda a: a[:].unsqueeze(2).broadcast_to([P, TILES, EXPERTS])
    vector_steps(core, [
        lambda: v.tensor_reduce(top[:], scores[:], AX_X, ALU.max),
        lambda: v.tensor_tensor(scores[:], scores[:], wide(top), ALU.subtract)])
    scalar_step(core, lambda: nc.scalar.activation(scores[:], scores[:], ACT.Exp))
    vector_steps(core, ([lambda: v.tensor_tensor(scores[:], scores[:], keep[:], ALU.mult)] if keep is not None else []) + [
        lambda: v.tensor_reduce(top[:], scores[:], AX_X, ALU.add),
        lambda: v.reciprocal(top[:], top[:]),
        lambda: v.tensor_tensor(scores[:], scores[:], wide(top), ALU.mult)])


def l2_ffn(core):
    nc, X = core.nc, core.X
    v = nc.vector
    with ExitStack() as own:
        w = weights(core, own, L2_ffn_W_gate=[P, DC, EXPERTS], L2_ffn_b2=[EXPERTS, DIM])
        d = core.dram
        bank = Experts(core, own, d["L2_ffn_W1"], d["L2_ffn_W2"], d["L2_ffn_b1"])
        U = core.sb(own, "u", [P, TILES, DIM])
        uT = core.sb(own, "uT", [P, DC, TOKENS])
        gates = core.sb(own, "gates", [P, TILES, EXPERTS])
        keep = core.sb(own, "keep", [P, TILES, EXPERTS])
        best = core.sb(own, "best", [P, TILES, 8])
        acc = core.sb(own, "acc", [P, TILES, DIM])
        top = core.sb(own, "top", [P, TILES])
        normalize(core, X, U, loads=w.loads + bank.loads)
        turn(core, U, DC, uT)
        linear_rows(core, uT, w["L2_ffn_W_gate"], gates)
        vector_steps(core, [(lambda t: lambda: v.max(best[:, t, :], gates[:, t, :]))(t) for t in range(TILES)] + [
            lambda: v.tensor_tensor(keep[:], gates[:], spread(best[:, :, 1:2]), ALU.is_ge)])
        softmax_experts(core, gates, top, keep)
        vector_steps(core, [lambda: v.tensor_scalar(gates[:], gates[:], 1.0 / EXPERTS, None, ALU.mult)])
        gate_bias(core, gates, w["L2_ffn_b2"], acc)
        experts(core, bank, uT, gates, acc, ACT.Relu)
        add(core, X, X, acc)


def l1_xattn(core):
    small_xattn(core, "L1_xattn_", True)


def l3_xattn(core):
    small_xattn(core, "L3_xattn_", False)


def small_xattn(core, pre, biased):
    heads, d, pad = 16, 16, 32
    X = core.X
    with ExitStack() as own:
        shapes = {"Wq": [P, DC, heads * pad], "WkT": [P, heads * pad // P, CDIM], "Wv": [P, DIM], "Wo": [P, DC, DIM],
                  "bv": [P, DC]}
        if biased:
            shapes.update({"bq": [P, heads * pad // P], "bo": [1, DIM]})
        w = weights(core, own, pre, **shapes)
        sums = core.sb(own, "sums", [P, BATCH, heads // 2, d])
        qT = core.sb(own, "qT", [P, heads * pad // P, TOKENS])
        room = ContextRoom(core, own, 1, heads * pad // P, P // pad)
        with ExitStack() as front:
            U = core.sb(front, "u", [P, TILES, DIM])
            uT = core.sb(front, "uT", [P, DC, TOKENS])
            normalize(core, X, U, loads=w.loads + room.loads, clear=room.q_tile)
            turn(core, U, DC, uT)
            linear_turned(core, uT, w["Wq"], qT, w["bq"] if biased else None)
        wv4 = w["Wv"][:].rearrange("c (a p d) -> c p a d", a=2, d=d)
        context_attention(core, room, qT, head_queries(w["WkT"]), 4, heads * SEQ, False, None,
                          lambda pair: wv4[:, pair], sums, heads // 2, 2, 2, 2, d ** -0.5, d)
        oT = core.sb(own, "oT", [P, DC, TOKENS])
        turn_sums(core, sums, heads // 2, d, oT, w["bv"])
        linear_rows(core, oT, w["Wo"], X, w["bo"] if biased else None, X)


def l2_xattn(core):
    X, nc = core.X, core.nc
    with ExitStack() as own:
        w = weights(core, own, L2_xattn_Wq=[P, DC, DIM], L2_xattn_bq=[P, DC], L2_xattn_WkT=[P, DC, CDIM],
                    L2_xattn_Wv=[P, DIM], L2_xattn_bv=[P, DIM])
        sums = core.sb(own, "sums", [SEQ, BATCH, 1, DIM])
        qT = core.sb(own, "qT", [P, DC, TOKENS])
        room = ContextRoom(core, own, 2, DC, 1)
        with ExitStack() as front:
            U = core.sb(front, "u", [P, TILES, DIM])
            uT = core.sb(front, "uT", [P, DC, TOKENS])
            normalize(core, X, U, loads=w.loads + room.loads)
            turn(core, U, DC, uT)
            linear_turned(core, uT, w["L2_xattn_Wq"], qT, w["L2_xattn_bq"])

        def queries(j, q):
            return [(slice(0, SEQ), w["L2_xattn_WkT"][:, c, :], q[:, c, :], c == 0, c == DC - 1) for c in range(DC)]

        context_attention(core, room, qT, queries, 1, SEQ, False, None,
                          lambda pair: w["L2_xattn_Wv"][:].unsqueeze(1), sums, 1, 1, 1, 4, 1.0, DIM)
        out = core.sb(own, "out", [P, TILES, DIM])
        s5 = sums[:].rearrange("s (t a) x d -> s t a (x d)", a=2)
        store(core, [(out[a * SEQ:(a + 1) * SEQ], s5[:, :, a, :]) for a in range(2)])
        v = nc.vector
        vector_steps(core, [
            lambda: v.tensor_tensor(out[:], out[:], w["L2_xattn_bv"][:].unsqueeze(1).broadcast_to([P, TILES, DIM]), ALU.add),
            lambda: v.tensor_tensor(X[:], X[:], out[:], ALU.add)])


def l1_attn(core):
    nc, X, PS = core.nc, core.X, core.PS
    v = nc.vector
    inner, states = 512, 16
    C = inner // P
    with ExitStack() as own:
        w = weights(core, own, L1_attn_norm_w=[P, DC], L1_attn_norm_b=[P, DC], L1_attn_W_in=[P, DC, inner],
                    L1_attn_W_gate=[P, DC, inner], L1_attn_W_dt=[P, C, inner], L1_attn_b_dt=[P, C],
                    L1_attn_W_BC=[P, C, 2 * states], L1_attn_A_log=[P, C, states], L1_attn_W_out=[P, C, DIM])
        zT = core.sb(own, "zT", [P, C, TOKENS])
        gateT = core.sb(own, "gateT", [P, C, TOKENS])
        dtT = core.sb(own, "dtT", [P, C, TOKENS])
        A = w["L1_attn_A_log"]
        with ExitStack() as front:
            U = core.sb(front, "u", [P, TILES, DIM])
            uT = core.sb(front, "uT", [P, DC, TOKENS])
            bcT = core.sb(front, "bcT", [2 * states, 1, TOKENS])
            e = core.sb(front, "e", [P, C, TOKENS])
            normalize(core, X, U, loads=w.loads)
            add(core, X, X, U)
            normalize(core, U, U)
            turn(core, U, DC, uT, w["L1_attn_norm_w"], w["L1_attn_norm_b"])
            linear_turned(core, uT, w["L1_attn_W_in"], zT)
            linear_turned(core, uT, w["L1_attn_W_gate"], gateT, None, ACT.Silu)
            linear_turned(core, zT, w["L1_attn_W_dt"], dtT, w["L1_attn_b_dt"])
            linear_turned(core, zT, w["L1_attn_W_BC"], bcT, rows=2 * states)
            store(core, [(core.dram["bc_turned"], bcT[:, 0, :])])
            scalar_step(core, lambda: nc.scalar.activation(e[:], dtT[:], ACT.Abs))
            scalar_step(core, lambda: nc.scalar.activation(e[:], e[:], ACT.Exp, scale=-1.0))
            scalar_step(core, lambda: nc.scalar.activation(A[:], A[:], ACT.Exp))
            scalar_step(core, lambda: nc.scalar.activation(e[:], e[:], ACT.Ln, bias=1.0))
            vector_steps(core, [
                lambda: v.scalar_tensor_tensor(dtT[:], dtT[:], 0.0, e[:], ALU.max, ALU.add),
                lambda: v.tensor_scalar(dtT[:], dtT[:], 0.001, 1.0, ALU.max, ALU.min),
                lambda: v.tensor_tensor(zT[:], zT[:], dtT[:], ALU.mult),
                lambda: v.tensor_scalar(A[:], A[:], 1e-6, 1.0, ALU.max, ALU.min),
                lambda: v.tensor_scalar(A[:], A[:], -1.0, None, ALU.mult),
                lambda: v.memset(dtT[:].rearrange("p c (b s) -> p c b s", s=SEQ)[:, :, :, 0:1], 1e30)])
        selective_scan(core, zT, dtT, A, C, states)
        y = dtT
        vector_steps(core, [lambda: v.tensor_tensor(y[:].rearrange("p c n -> p (c n)"), PS[:].rearrange("p b n -> p (b n)"),
                                                    gateT[:].rearrange("p c n -> p (c n)"), ALU.mult)])
        linear_rows(core, y, w["L1_attn_W_out"], X, None, X)


def selective_scan(core, dtz, dt, A, C, states):
    nc, PS = core.nc, core.PS
    landed = core.semaphores("rows_landed", 2)
    decay_ready, in_ready, h_ready, w_ready, summed = (core.semaphore("decay_ready"), core.semaphore("scan_in_ready"),
                                                       core.semaphore("state_ready"), core.semaphore("product_ready"),
                                                       core.semaphore("product_summed"))
    zero_ready = core.semaphore("zero_ready")
    bc = core.dram["bc_turned"]
    with ExitStack() as own:
        Bb = core.sb(own, "b_all", [P, 2, TOKENS])
        Cb = core.sb(own, "c_all", [P, 2, TOKENS])
        decay = core.sb(own, "decay", [P, 2, TOKENS])
        fresh = core.sb(own, "fresh", [P, 2, TOKENS])
        state = core.sb(own, "state", [P, 2, TOKENS])
        prod = core.sb(own, "prod", [P, 2, TOKENS])
        zeros = core.sb(own, "zeros", [P, 512])
        warm = core.sb(own, "warm", [1, 1])
        with nc.Block() as block:
            @block.sync
            def _(sp):
                with sp.Fori(0, states // 2) as it:
                    for u in range(2):
                        s = it * 2 + u
                        sp.wait_ge(w_ready.sem, w_ready.at(s * C + C))
                        sp.dma_start(Bb[:, u, :], bc[bass.ds(s, 1), :].broadcast_to([P, TOKENS])).then_inc(landed[u].sem, 16)
                        sp.dma_start(Cb[:, u, :], bc[bass.ds(s + states, 1), :].broadcast_to([P, TOKENS])).then_inc(landed[u].sem, 16)

            @block.scalar
            def _(act):
                nc.scalar.activation(warm[:], core.ident[0:1, 0:1], ACT.Exp)
                with act.Fori(0, states // 2) as it:
                    for u in range(2):
                        for c in range(C):
                            n = (it * 2 + u) * C + c
                            act.wait_ge(h_ready.sem, h_ready.at(n + 1))
                            nc.scalar.activation(decay[:, c % 2, :], dt[:, c, :], ACT.Exp,
                                                 scale=A[:, c, bass.ds(it * 2 + u, 1)]).then_inc(decay_ready.sem, 1)

            @block.gpsimd
            def _(pool):
                with pool.Fori(0, states // 2) as it:
                    for u in range(2):
                        pool.wait_ge(landed[u].sem, landed[u].at(it * 32 + 32))
                        for c in range(C):
                            n = (it * 2 + u) * C + c
                            pool.wait_ge(h_ready.sem, h_ready.at(n + 1))
                            nc.gpsimd.tensor_tensor(fresh[:, c % 2, :], dtz[:, c, :], Bb[:, u, :], ALU.mult).then_inc(in_ready.sem, 1)

            @block.vector
            def _(dve):
                nc.vector.memset(zeros[:], 0.0).then_inc(zero_ready.sem, 1)
                dve.sem_inc(h_ready.sem, 2)
                dve.sem_inc(w_ready.sem, 2 * C)
                with dve.Fori(0, states // 2) as it:
                    for u in range(2):
                        dve.wait_ge(landed[u].sem, landed[u].at(it * 32 + 32))
                        for c in range(C):
                            n = (it * 2 + u) * C + c
                            dve.wait_ge(decay_ready.sem, decay_ready.at(n + 1))
                            dve.wait_ge(in_ready.sem, in_ready.at(n + 1))
                            nc.vector.tensor_tensor_scan(state[:, c % 2, :], decay[:, c % 2, :], fresh[:, c % 2, :], 0.0,
                                                         ALU.mult, ALU.add).then_inc(h_ready.sem, 1)
                            dve.wait_ge(h_ready.sem, h_ready.at(n + 3))
                            dve.wait_ge(summed.sem, summed.at(n + 1))
                            nc.vector.tensor_tensor(prod[:, c % 2, :], state[:, c % 2, :], Cb[:, u, :], ALU.mult).then_inc(w_ready.sem, 1)

            @block.tensor
            def _(pe):
                pe.sem_inc(summed.sem, 2)
                pe.wait_ge(zero_ready.sem, zero_ready.at(1))
                for k in range(BANKS):
                    nc.tensor.matmul(PS[:, k, :], core.ident[:], zeros[:], start=True, stop=False, skip_group_check=True)
                with pe.Fori(0, states // 2) as it:
                    for u in range(2):
                        for c in range(C):
                            n = (it * 2 + u) * C + c
                            pe.wait_ge(w_ready.sem, w_ready.at(n + 1 + 2 * C))
                            for half in range(HALVES):
                                last = nc.tensor.matmul(PS[:, c * HALVES + half, :], core.ident[:],
                                                        prod[:, c % 2, half * 512:(half + 1) * 512], start=False, stop=False,
                                                        skip_group_check=True)
                            last.then_inc(summed.sem, 1)
                for k in range(BANKS):
                    last = nc.tensor.matmul(PS[:, k, :], core.ident[:], zeros[:], start=False, stop=True, skip_group_check=True)
                last.then_inc(summed.sem, 1)
                pe.wait_ge(summed.sem, summed.at(states * C + 3))
    n = states * C
    for s in landed:
        s.passed(32 * states // 2)
    decay_ready.passed(n)
    in_ready.passed(n)
    h_ready.passed(n + 2)
    w_ready.passed(n + 2 * C)
    summed.passed(n + 3)
    zero_ready.passed(1)


def l2_attn(core):
    nc, X = core.nc, core.X
    v = nc.vector
    heads, d = 16, 16
    with ExitStack() as own:
        w = weights(core, own, L2_attn_key_w=[P, DC, DIM], L2_attn_key_b=[P, DC], L2_attn_v_w=[P, DC, DIM],
                    L2_attn_q_w=[P, DC, DIM], L2_attn_out_w=[P, DC, DIM], L2_attn_out_b=[1, DIM], gather_rows=[P, d, P])
        kT = core.sb(own, "kT", [P, DC, TOKENS])
        freshT = core.sb(own, "freshT", [P, DC, TOKENS])
        qT = core.sb(own, "qT", [P, DC, TOKENS])
        vT = core.sb(own, "vT", [P, DC, TOKENS])
        U = core.sb(own, "u", [P, TILES, DIM])
        uT = core.sb(own, "uT", [P, DC, TOKENS])
        normalize(core, X, U, loads=w.loads)
        turn(core, U, DC, uT)
        linear_turned(core, uT, w["L2_attn_v_w"], vT)
        store(core, [(core.dram["v_turned"].rearrange("(c p) n -> p c n", p=P), vT[:])])
        linear_turned(core, uT, w["L2_attn_q_w"], qT)
        linear_turned(core, uT, w["L2_attn_key_w"], kT, w["L2_attn_key_b"], ACT.Sigmoid)
        vector_steps(core, [
            lambda: v.tensor_scalar(freshT[:], kT[:], -1.0, 1.0, ALU.mult, ALU.add),
            lambda: v.memset(kT[:].rearrange("p c (b s) -> p c b s", s=SEQ)[:, :, :, 0:1], 0.0)])
        memory_scan(core, kT, freshT, qT, w["gather_rows"], uT, d)
        linear_rows(core, uT, w["L2_attn_out_w"], X, w["L2_attn_out_b"], X)


def memory_scan(core, kT, freshT, qT, gather, dst, d):
    nc, PS = core.nc, core.PS
    landed, used = core.semaphores("rows_landed", 2 * DC), core.semaphore("rows_used")
    in_ready, h_ready, w_ready, summed = (core.semaphore("scan_in_ready"), core.semaphore("state_ready"),
                                          core.semaphore("product_ready"), core.semaphore("product_summed"))
    taken = core.semaphore("rows_taken")
    per = P // d
    vrows = core.dram["v_turned"].rearrange("(c h e) n -> c h e n", c=DC, e=d)
    with ExitStack() as own:
        Vb = core.sb(own, "v_all", [P, DC, 2, TOKENS])
        fresh = core.sb(own, "fresh", [P, DC, TOKENS])
        state = core.sb(own, "state", [P, DC, TOKENS])
        prod = core.sb(own, "prod", [P, DC, TOKENS])
        with nc.Block() as block:
            def load(eng, c):
                with eng.Fori(0, d // 2) as it:
                    for u in range(2):
                        e = it * 2 + u
                        eng.wait_ge(used.sem, used.at(e * DC + c + 1))
                        for h in range(per):
                            eng.dma_start(Vb[h * d:(h + 1) * d, c, u, :],
                                          vrows[c, h, bass.ds(e, 1), :].broadcast_to([d, TOKENS])).then_inc(
                                              landed[c * 2 + u].sem, 16)

            @block.sync
            def _(sp):
                load(sp, 0)

            @block.scalar
            def _(act):
                load(act, 1)

            @block.gpsimd
            def _(pool):
                pool.sem_inc(used.sem, 2 * DC)
                with pool.Fori(0, d // 2) as it:
                    for u in range(2):
                        for c in range(DC):
                            n = (it * 2 + u) * DC + c
                            pool.wait_ge(landed[c * 2 + u].sem, landed[c * 2 + u].at(it * 16 * per + 16 * per))
                            pool.wait_ge(h_ready.sem, h_ready.at(n + 1))
                            nc.gpsimd.tensor_tensor(fresh[:, c, :], freshT[:, c, :], Vb[:, c, u, :],
                                                    ALU.mult).then_inc(in_ready.sem, 1)
                            pool.wait_ge(in_ready.sem, in_ready.at(n + 1))
                            pool.sem_inc(used.sem, 1)

            @block.vector
            def _(dve):
                dve.sem_inc(h_ready.sem, DC)
                with dve.Fori(0, d) as e:
                    for c in range(DC):
                        n = e * DC + c
                        dve.wait_ge(in_ready.sem, in_ready.at(n + 1))
                        nc.vector.tensor_tensor_scan(state[:, c, :], kT[:, c, :], fresh[:, c, :], 0.0,
                                                     ALU.mult, ALU.add).then_inc(h_ready.sem, 1)
                        dve.wait_ge(h_ready.sem, h_ready.at(n + DC + 1))
                        dve.wait_ge(summed.sem, summed.at(n + 1))
                        nc.vector.tensor_tensor(prod[:, c, :], state[:, c, :], qT[:, c, :], ALU.mult).then_inc(w_ready.sem, 1)
                dve.wait_ge(summed.sem, summed.at(d * DC + DC))
                nc.vector.tensor_copy(dst[:].rearrange("p c n -> p (c n)"),
                                      PS[:, 0:DC * HALVES, :].rearrange("p b n -> p (b n)")).then_inc(taken.sem, 1)

            @block.tensor
            def _(pe):
                wait_weights(core, pe)
                pe.sem_inc(summed.sem, DC)
                for e in range(d):
                    for c in range(DC):
                        pe.wait_ge(w_ready.sem, w_ready.at(e * DC + c + 1))
                        for half in range(HALVES):
                            last = nc.tensor.matmul(PS[:, c * HALVES + half, :], gather[:, e, :],
                                                    prod[:, c, half * 512:(half + 1) * 512], start=(e == 0), stop=(e == d - 1),
                                                    skip_group_check=True)
                        last.then_inc(summed.sem, 1)
    n = d * DC
    for s in landed:
        s.passed(16 * per * d // 2)
    used.passed(n + 2 * DC)
    in_ready.passed(n)
    h_ready.passed(n + DC)
    w_ready.passed(n)
    summed.passed(n + DC)
    taken.passed(1)


def rotate(core, xT, swap, cos, sin):
    nc, PS = core.nc, core.PS
    ready, taken, step = core.semaphore("fill_ready"), core.semaphore("fill_taken_dve"), core.semaphore("norm_step")
    cos_done = core.semaphore("cos_done")
    fills = xT.shape[1] * HALVES
    nb = 512 // SEQ
    wide = lambda a: a[:].unsqueeze(1).broadcast_to([P, nb, SEQ])
    with ExitStack() as own:
        part = core.sb(own, "part", [P, 2, 512])
        with nc.Block() as block:
            @block.tensor
            def _(pe):
                wait_weights(core, pe)
                for f in range(fills):
                    c, half = f // HALVES, f % HALVES
                    if f >= BANKS:
                        pe.wait_ge(step.sem, step.at(f - BANKS + 1))
                    nc.tensor.matmul(PS[:, f % BANKS, :], swap[:], xT[:, c, half * 512:(half + 1) * 512],
                                     start=True, stop=True).then_inc(ready.sem, 1)

            @block.gpsimd
            def _(pool):
                wait_weights(core, pool)
                for f in range(fills):
                    c, half = f // HALVES, f % HALVES
                    x = xT[:, c, half * 512:(half + 1) * 512].rearrange("p (b s) -> p b s", s=SEQ)
                    pool.wait_ge(ready.sem, ready.at(f + 1))
                    nc.gpsimd.tensor_tensor(x, x, wide(cos), ALU.mult).then_inc(cos_done.sem, 1)

            @block.vector
            def _(dve):
                wait_weights(core, dve)
                for f in range(fills):
                    c, half = f // HALVES, f % HALVES
                    x = xT[:, c, half * 512:(half + 1) * 512]
                    dve.wait_ge(ready.sem, ready.at(f + 1))
                    nc.vector.tensor_tensor(part[:, f % 2, :].rearrange("p (b s) -> p b s", s=SEQ),
                                            PS[:, f % BANKS, :].rearrange("p (b s) -> p b s", s=SEQ), wide(sin),
                                            ALU.mult).then_inc(step.sem, 1)
                    dve.wait_ge(step.sem, step.at(f + 1))
                    dve.wait_ge(cos_done.sem, cos_done.at(f + 1))
                    nc.vector.tensor_tensor(x, x, part[:, f % 2, :], ALU.add).then_inc(taken.sem, 1)
    for s in (ready, taken, step, cos_done):
        s.passed(fills)


def l3_attn(core):
    heads, hd = 16, 64
    inner = heads * hd
    C = inner // P
    X = core.X
    with ExitStack() as own:
        w = weights(core, own, L3_attn_ln_gamma=[P, DC], L3_attn_ln_beta=[P, DC], L3_attn_w_out=[P, C, DIM],
                    L3_attn_b_out=[1, DIM], rope_cos=[P, SEQ], rope_sin=[P, SEQ], rope_swap=[P, P])
        qT = core.sb(own, "qT", [P, C, TOKENS])
        V = core.sb(own, "v", [P, TILES, inner])
        with ExitStack() as keys:
            kT = core.sb(keys, "kT", [P, C, TOKENS])
            with ExitStack() as front:
                wqkv = weights(core, front, L3_attn_w_qkv=[P, DC, 3 * inner])
                U = core.sb(front, "u", [P, TILES, DIM])
                uT = core.sb(front, "uT", [P, DC, TOKENS])
                normalize(core, X, U, loads=w.loads + wqkv.loads)
                normalize(core, U, U)
                turn(core, U, DC, uT, w["L3_attn_ln_gamma"], w["L3_attn_ln_beta"])
                linear_turned(core, uT, wqkv["L3_attn_w_qkv"][:, :, 0:inner], qT)
                linear_turned(core, uT, wqkv["L3_attn_w_qkv"][:, :, inner:2 * inner], kT)
                linear_rows(core, uT, wqkv["L3_attn_w_qkv"][:, :, 2 * inner:3 * inner], V)
            rotate(core, qT, w["rope_swap"], w["rope_cos"], w["rope_sin"])
            rotate(core, kT, w["rope_swap"], w["rope_cos"], w["rope_sin"])
            self_attention(core, qT, kT, V, V, heads, hd, hd, hd ** -0.5)
        turn(core, V, C, qT)
        linear_rows(core, qT, w["L3_attn_w_out"], X, w["L3_attn_b_out"], X)


def l3_ffn(core):
    heads, d = 8, 32
    nc, X = core.nc, core.X
    v = nc.vector
    pre = "L3_ffn_"
    with ExitStack() as own:
        shapes = {"norm_w": [P, DC], "norm_b": [P, DC], "q_w": [P, DC, DIM], "k_w": [P, DC, DIM], "v_w": [P, DC, DIM],
                  "o_w": [P, DC, DIM], "q_b": [P, DC], "k_b": [P, DC], "v_b": [1, DIM], "o_b": [1, DIM]}
        w = weights(core, own, pre, **shapes)
        masks = weights(core, own, width_turned=[P, DC, SEQ], width_rows=[P, DIM])
        U = core.sb(own, "u", [P, TILES, DIM])
        hat = core.sb(own, "hat", [P, TILES, DIM])
        uT = core.sb(own, "uT", [P, DC, TOKENS])
        qT = core.sb(own, "qT", [P, DC, TOKENS])
        kT = core.sb(own, "kT", [P, DC, TOKENS])
        V = core.sb(own, "v", [P, TILES, DIM])
        O = core.sb(own, "o", [P, TILES, DIM])
        normalize(core, X, U, loads=w.loads + masks.loads)
        normalize(core, U, hat)
        turn(core, hat, DC, uT, w["norm_w"], w["norm_b"])

        def cut(c):
            x = uT[:, c, :].rearrange("p (b s) -> p b s", s=SEQ)
            return v.tensor_tensor(x, x, masks["width_turned"][:, c, :].unsqueeze(1).broadcast_to([P, BATCH, SEQ]), ALU.mult)

        vector_steps(core, [(lambda c: lambda: cut(c))(c) for c in range(DC)])
        linear_turned(core, uT, w["q_w"], qT, w["q_b"])
        linear_turned(core, uT, w["k_w"], kT, w["k_b"])
        linear_rows(core, uT, w["v_w"], V, w["v_b"])
        self_attention(core, qT, kT, V, O, heads, d, d, DIM ** -0.5)
        rows_mask = masks["width_rows"][:].unsqueeze(1).broadcast_to([P, TILES, DIM])
        vector_steps(core, [lambda: v.tensor_tensor(O[:], O[:], rows_mask, ALU.mult)])
        turn(core, O, DC, uT)
        linear_rows(core, uT, w["o_w"], O, w["o_b"])
        vector_steps(core, [lambda: v.tensor_tensor(O[:], O[:], rows_mask, ALU.mult),
                            lambda: v.tensor_tensor(O[:], O[:], U[:], ALU.add),
                            lambda: v.tensor_tensor(X[:], X[:], O[:], ALU.add)])


def perceiver(nc, dram):
    sublayers = (l0_xattn, l0_attn, l0_ffn, l1_xattn, l1_attn, l1_ffn, l2_xattn, l2_attn, l2_ffn, l3_xattn, l3_attn, l3_ffn)
    with ExitStack() as hold:
        core = Core(nc, dram, hold)
        landed, first = core.semaphore("weights_landed"), core.semaphore("vector_step")
        loads = [(core.X[:], dram["x"].rearrange("(t p) d -> p t d", p=P), landed), (core.ident[:], dram["ident"], landed)]
        landed.passed(16 * len(loads))
        with nc.Block() as block:
            start_loads(block, loads)

            @block.vector
            def _(dve):
                nc.vector.memset(core.ones_row[:], 1.0).then_inc(first.sem, 1)
                wait_weights(core, dve)

            @block.tensor
            def _(pe):
                wait_weights(core, pe)

            @block.scalar
            def _(act):
                wait_weights(core, act)
        first.passed(1)
        for n in LAYERS:
            sublayers[n](core)
        store(core, [(dram["out"].rearrange("(t p) d -> p t d", p=P), core.X[:])])




def layouts(inputs):
    import numpy as np

    a = {k: np.asarray(v) for k, v in inputs.items()}
    out = {}

    def chunked(w):
        return w.reshape(-1, P, w.shape[-1]).transpose(1, 0, 2)

    def column(b):
        return b.reshape(-1, P).T

    def pad_heads(w, d, to):
        k = w.shape[0]
        r = np.zeros((k, w.shape[1] // d, to), w.dtype)
        r[:, :, :d] = w.reshape(k, -1, d)
        return r.reshape(k, -1)

    def halves_first(w, d):
        return w.reshape(-1, 2, d, w.shape[-1]).transpose(1, 0, 2, 3).reshape(w.shape)

    out["x"] = a["x"].reshape(TOKENS, DIM)
    out["ctx_512"] = a["ctx_512"]
    for n in ("ln1_g", "ln1_b", "ln2_g", "ln2_b"):
        out[f"L0_xattn_{n}"] = a[f"L0_xattn_{n}"][None]
    for p in ("L0_xattn_a1_", "L0_xattn_a2_"):
        cols = lambda w: w.transpose(1, 0, 2).reshape(w.shape[1], -1)
        out[p + "wq"] = chunked(cols(a[p + "wq"]))
        if "a1" in p:
            out[p + "wk"] = chunked(cols(a[p + "wk"]))
            out[p + "wv"] = chunked(cols(a[p + "wv"]))
            out[p + "li1_w"] = chunked(a[p + "li1_w"])
        else:
            out[p + "wkT"] = chunked(cols(a[p + "wk"]).T)
            out[p + "wv"] = chunked(halves_first(cols(a[p + "wv"]).T, 32).T)
            out[p + "li1_w"] = chunked(halves_first(a[p + "li1_w"], 32))
        for n in ("li2_w", "li3_w"):
            out[p + n] = chunked(a[p + n])
        for n in ("lnx_g", "lnx_b", "lny_g", "lny_b", "ln3_g", "ln3_b", "li2_b"):
            out[p + n] = column(a[p + n])
        for n in ("li1_b", "li3_b"):
            out[p + n] = a[p + n][None]
    for n in ("Wq", "Wk"):
        out["L0_attn_" + n] = chunked(pad_heads(a["L0_attn_" + n], 16, 32))
    for n in ("Wv", "Wo"):
        out["L0_attn_" + n] = chunked(a["L0_attn_" + n])
    for n in ("lq1", "lk1", "lq2", "lk2", "ln_g", "ln_b"):
        out["L0_attn_" + n] = a["L0_attn_" + n][None]

    def per_expert(w):
        return w.reshape(EXPERTS, -1, P, w.shape[-1]).transpose(0, 2, 1, 3)

    def expert_columns(b):
        return b.reshape(EXPERTS, -1, P).transpose(0, 2, 1)

    out["L0_ffn_router_W"] = chunked(a["L0_ffn_router_W"])
    out["L0_ffn_router_b"] = a["L0_ffn_router_b"][None]
    out["L0_ffn_b2"] = a["L0_ffn_b2"]
    out["L0_ffn_W1"], out["L0_ffn_W2"] = per_expert(a["L0_ffn_W1"]), per_expert(a["L0_ffn_W2"])
    for n in ("b1", "ln_g", "ln_b"):
        out["L0_ffn_" + n] = expert_columns(a["L0_ffn_" + n])
    for n in ("wg_w", "w1_w", "w2_w"):
        out["L1_ffn_" + n] = per_expert(a["L1_ffn_" + n].transpose(0, 2, 1))
    for n in ("wg_b", "w1_b"):
        out["L1_ffn_" + n] = expert_columns(a["L1_ffn_" + n])
    out["L1_ffn_w2_b"] = a["L1_ffn_w2_b"]
    out["L1_ffn_router_w"] = chunked(a["L1_ffn_router_w"].T)
    out["L2_ffn_W_gate"] = chunked(a["L2_ffn_W_gate"])
    out["L2_ffn_b2"] = a["L2_ffn_b2"]
    out["L2_ffn_W1"], out["L2_ffn_W2"] = per_expert(a["L2_ffn_W1"]), per_expert(a["L2_ffn_W2"])
    out["L2_ffn_b1"] = expert_columns(a["L2_ffn_b1"])

    p = "L1_xattn_"
    out[p + "Wq"] = chunked(pad_heads(a[p + "Wq"], 16, 32))
    out[p + "bq"] = column(pad_heads(a[p + "bq"][None], 16, 32)[0])
    out[p + "WkT"] = chunked(pad_heads(a[p + "Wk"], 16, 32).T)
    out[p + "Wv"] = halves_first(a[p + "Wv"].T, 16).T
    out[p + "bv"] = column(halves_first(a[p + "bv"][:, None], 16)[:, 0])
    out[p + "Wo"] = chunked(halves_first(a[p + "Wo"], 16))
    out[p + "bo"] = a[p + "bo"][None]
    p = "L3_xattn_"
    out[p + "Wq"] = chunked(pad_heads(a[p + "Wq"].T, 16, 32))
    out[p + "WkT"] = chunked(pad_heads(a[p + "Wkv"][:DIM].T, 16, 32).T)
    out[p + "Wv"] = halves_first(a[p + "Wkv"][DIM:], 16).T
    out[p + "bv"] = np.zeros((P, DC), np.float32)
    out[p + "Wo"] = chunked(halves_first(a[p + "Wo"].T, 16))
    p = "L2_xattn_"
    out[p + "Wq"], out[p + "bq"] = chunked(a[p + "Wq"]), column(a[p + "bq"])
    out[p + "WkT"] = chunked(a[p + "Wk"].T)
    out[p + "Wv"], out[p + "bv"] = a[p + "Wv"], a[p + "bv"][None]

    p = "L1_attn_"
    for n in ("norm_w", "norm_b", "b_dt"):
        out[p + n] = column(a[p + n])
    for n in ("W_in", "W_gate", "W_dt", "W_out", "A_log"):
        out[p + n] = chunked(a[p + n])
    out[p + "W_BC"] = chunked(np.concatenate([a[p + "W_B"], a[p + "W_C"]], axis=1))
    p = "L2_attn_"
    out[p + "key_w"], out[p + "key_b"] = chunked(a[p + "key_w"].T), column(a[p + "key_b"])
    out[p + "v_w"], out[p + "q_w"] = chunked(a[p + "vq_w"][:DIM].T), chunked(a[p + "vq_w"][DIM:].T)
    out[p + "out_w"], out[p + "out_b"] = chunked(a[p + "out_w"].T), a[p + "out_b"][None]
    p = "L3_attn_"
    out[p + "ln_gamma"], out[p + "ln_beta"] = column(a[p + "ln_gamma"]), column(a[p + "ln_beta"])
    out[p + "w_qkv"], out[p + "w_out"], out[p + "b_out"] = chunked(a[p + "w_qkv"]), chunked(a[p + "w_out"]), a[p + "b_out"][None]
    p = "L3_ffn_"
    for n in ("q_w", "k_w", "v_w", "o_w"):
        out[p + n] = chunked(a[p + n].T)
    for n in ("norm_w", "norm_b", "q_b", "k_b"):
        out[p + n] = column(a[p + n])
    for n in ("v_b", "o_b"):
        out[p + n] = a[p + n][None]
    return {k: np.ascontiguousarray(v) for k, v in out.items()}


def constants():
    import numpy as np

    f = np.float32
    out = {"ident": np.eye(P, dtype=f), "iota8": np.arange(EXPERTS, dtype=f)[None]}
    s = np.arange(SEQ)
    out["causal"] = np.tile((s[None, :] > s[:, None]).astype(f), (2, 1))
    r = np.arange(P)
    g = np.zeros((P, 16, P), f)
    for e in range(16):
        g[:, e, :] = (r[:, None] // 16 == r[None, :] // 16) & (r[None, :] % 16 == e)
    out["gather_rows"] = g
    inv = (1.0 / 10000.0 ** (np.arange(0, 64, 2, dtype=f) / f(64))).astype(f)
    ang = (np.arange(SEQ, dtype=f)[:, None] * inv[None, :]).astype(f)
    out["rope_cos"] = np.tile(np.cos(ang).T, (4, 1)).astype(f)
    out["rope_sin"] = np.tile(np.sin(ang).T, (4, 1)).astype(f)
    w = np.zeros((P, P), f)
    for h in (0, 64):
        for i in range(32):
            w[h + 32 + i, h + i] = -1
            w[h + i, h + 32 + i] = 1
    out["rope_swap"] = w
    width = DIM >> (s // 16)
    m = (np.arange(DIM)[:, None] < width[None, :]).astype(f)
    out["width_turned"] = m.reshape(DC, P, SEQ).transpose(1, 0, 2)
    out["width_rows"] = np.tile(m.T, (2, 1))
    return {k: np.ascontiguousarray(v) for k, v in out.items()}


def kernel(**inputs):
    import concourse.bacc as _bacc
    from concourse.bass_utils import run_bass_kernel_spmd as _run

    nc = _bacc.Bacc("TRN2", target_bir_lowering=False, num_devices=1)
    arrays, dram = {}, {}
    for name, a in {**layouts(inputs), **constants()}.items():
        arrays[f"in_{name}"] = a
        dram[name] = nc.dram_tensor(f"in_{name}", a.shape, F32, kind="ExternalInput").ap()
    for name, shape, dtype in (("bc_turned", (32, TOKENS), F32), ("v_turned", (DIM, TOKENS), F32)):
        dram[name] = nc.dram_tensor(name, shape, dtype, kind="Internal").ap()
    dram["out"] = nc.dram_tensor("out_x", (TOKENS, DIM), F32, kind="ExternalOutput").ap()
    perceiver(nc, dram)
    r = _run(nc, [arrays], core_ids=[0])
    return r.results[0]["out_x"].reshape(BATCH, SEQ, DIM)
```
